# Optimizing a Trainium2 kernel written in Bass

```python
import numpy as np
import jax
import jax.numpy as jnp

def _softmax(x, axis=-1):
    return jax.nn.softmax(x, axis=axis)

def _gelu(x):
    return jax.nn.gelu(x, approximate=True)

def _silu(x):
    return jax.nn.silu(x)

def _sigmoid(x):
    return jax.nn.sigmoid(x)

def _layernorm(x, axis=-1, eps=1e-05):
    m = jnp.mean(x, axis=axis, keepdims=True)
    v = jnp.var(x, axis=axis, keepdims=True)
    return (x - m) / jnp.sqrt(v + eps)

def _scatter_add(tgt, idx, src, axis=0):
    return tgt.at[idx].add(src)

def _segment_sum(src, seg, n):
    return jax.ops.segment_sum(src, seg, n)
kernel_name = 'mk_adj_ffn_d1_adj_r2_8f9eaf'

def setup_inputs(seed: int=0):
    np.random.seed(seed)
    _w = jnp.asarray

    def _rec_inputs():
        import jax
        import jax.numpy as jnp
        _gk = jax.random.key(seed)
        x = -0.0005207 + 1.001 * jax.random.normal(jax.random.fold_in(_gk, 1), (8192, 128), jnp.float32)
        _w = (1.0 + jnp.arange(8192, dtype=jnp.float32)) ** (-0.5)
        _w = _w / _w.mean()
        _pij = jnp.clip(0.000976562 * _w[:, None] * _w[None, :], 0.0, 1.0)
        _a = jax.random.uniform(jax.random.fold_in(_gk, 2), (8192, 8192)) < _pij
        adj = _a.astype(jnp.int32)
        return (x, adj)
    x, adj = _rec_inputs()

    def _L0_gnn_setup():
        import jax, jax.numpy as jnp
        import numpy as np
        MIN_NORM = 1e-15
        EPS = 1e-07
        MASK_FILL = -9000000000000000.0

        def logmap0(x, c):
            K = 1.0 / c
            sqrtK = K ** 0.5
            y = x[:, 1:]
            y_norm = jnp.clip(jnp.linalg.norm(y, axis=-1, keepdims=True), MIN_NORM)
            theta = jnp.clip(x[:, :1] / sqrtK, 1.0 + EPS)
            res = sqrtK * jnp.arccosh(theta) * y / y_norm
            return jnp.concatenate([jnp.zeros_like(x[:, :1]), res], axis=1)

        def proj(x, c):
            K = 1.0 / c
            y = x[:, 1:]
            x0 = jnp.sqrt(K + jnp.sum(y * y, axis=-1, keepdims=True))
            return jnp.concatenate([x0, y], axis=1)

        def expmap0(u, c):
            K = 1.0 / c
            sqrtK = K ** 0.5
            x = u[:, 1:]
            x_norm = jnp.clip(jnp.linalg.norm(x, axis=-1, keepdims=True), MIN_NORM)
            theta = x_norm / sqrtK
            res = jnp.concatenate([sqrtK * jnp.cosh(theta), sqrtK * jnp.sinh(theta) * x / x_norm], axis=1)
            return proj(res, c)
        key = jax.random.key(seed)
        k1, k2, k3, k4, k5 = jax.random.split(key, 5)
        N, D_in, D_out = (4096, 128, 128)
        x = jax.random.normal(k1, (N, D_in), dtype=jnp.float32)
        adj = jax.random.randint(k2, (N, N), 0, 2, dtype=jnp.int32)
        W_gcn = jax.random.normal(k3, (D_in - 1, D_out - 1), dtype=jnp.float32)
        std_w = 1.414 * (2.0 / (D_out + D_out)) ** 0.5
        W_att = jax.random.normal(k4, (D_out, D_out), dtype=jnp.float32) * std_w
        std_a = 1.414 * (2.0 / (2 * D_out + 1)) ** 0.5
        a_att = jax.random.normal(k5, (2 * D_out, 1), dtype=jnp.float32) * std_a
        return {'x': x, 'adj': adj, 'k': 1, 'W_gcn': W_gcn, 'W_att': W_att, 'a_att': a_att}
    _L0_gnn_all = _L0_gnn_setup()
    _L0_gnn_in = {k: v for k, v in _L0_gnn_all.items() if k in ('W_gcn', 'W_att', 'a_att')}
    del _L0_gnn_all

    def _L0_ffn_setup():
        import jax, jax.numpy as jnp
        import numpy as np
        H, P, G, NS, K = (8, 64, 64, 64, 3)
        D_INNER = H * P
        CONV_DIM = D_INNER + 2 * NS
        D_IN_PROJ = 2 * D_INNER + 2 * NS + 2 * H

        def _hydra(u, in_w, conv_w, conv_b, dt_bias, A_log, Dp, fcD_w, norm_w, out_w):
            Bt, L, _ = u.shape
            zxbcdt = u @ in_w.T
            z = zxbcdt[..., :D_INNER]
            xBC = zxbcdt[..., D_INNER:D_INNER + CONV_DIM]
            dt = zxbcdt[..., -2 * H:]
            dt = jnp.concatenate([dt[..., :H], jnp.flip(dt[..., H:], axis=1)], axis=0)
            dt = jax.nn.softplus(dt + dt_bias)
            xp = jnp.pad(xBC, ((0, 0), (K - 1, 0), (0, 0)))
            xBC = sum((xp[:, k:k + L, :] * conv_w[:, k] for k in range(K))) + conv_b
            xBC = jax.nn.silu(xBC)
            x = xBC[..., :D_INNER]
            Bm = xBC[..., D_INNER:D_INNER + NS]
            Cm = xBC[..., D_INNER + NS:]
            x_og = x
            x2 = jnp.concatenate([x, jnp.flip(x, 1)], 0).reshape(2 * Bt, L, H, P)
            B2 = jnp.concatenate([Bm, jnp.flip(Bm, 1)], 0)
            C2 = jnp.concatenate([Cm, jnp.flip(Cm, 1)], 0)
            dA = jnp.exp(dt * -jnp.exp(A_log))
            dBx = jnp.einsum('blh,bln,blhp->blhpn', dt, B2, x2)

            def step(h, inp):
                dA_t, dBx_t, C_t = inp
                h = h * dA_t[:, :, None, None] + dBx_t
                return (h, jnp.einsum('bhpn,bn->bhp', h, C_t))
            h0 = jnp.zeros((2 * Bt, H, P, NS), u.dtype)
            _, ys = jax.lax.scan(step, h0, (dA.transpose(1, 0, 2), dBx.transpose(1, 0, 2, 3, 4), C2.transpose(1, 0, 2)))
            y = ys.transpose(1, 0, 2, 3).reshape(2 * Bt, L, D_INNER)
            y_fw, y_bw = (y[:Bt], jnp.flip(y[Bt:], 1))
            y = jnp.pad(y_fw[:, :-1], ((0, 0), (1, 0), (0, 0))) + jnp.pad(y_bw[:, 1:], ((0, 0), (0, 1), (0, 0)))
            y = y + x_og * jnp.repeat(x_og @ fcD_w.T + Dp, P, axis=-1)
            yg = y * jax.nn.silu(z)
            yg = yg * jax.lax.rsqrt(jnp.mean(jnp.square(yg), -1, keepdims=True) + 1e-05) * norm_w
            return yg @ out_w.T
        key = jax.random.key(seed)
        ks = jax.random.split(key, 10)
        dim, Bsz, N = (128, 4, 4096)
        s = 0.02
        return {'x': jax.random.normal(ks[0], (Bsz, N, dim), jnp.float32), 'W_fx': jax.random.normal(ks[1], (D_INNER, dim), jnp.float32) * s, 'b_fx': jnp.zeros((D_INNER,), jnp.float32), 'W_x': jax.random.normal(ks[2], (D_INNER, dim), jnp.float32) * s, 'b_x': jnp.zeros((D_INNER,), jnp.float32), 'W_slice': jax.random.normal(ks[3], (G, P), jnp.float32) * s, 'b_slice': jnp.zeros((G,), jnp.float32), 'temperature': jnp.full((1, H, 1, 1), 0.5, jnp.float32), 'hy_in_w': jax.random.normal(ks[4], (D_IN_PROJ, D_INNER), jnp.float32) * s, 'hy_conv_w': jax.random.normal(ks[5], (CONV_DIM, K), jnp.float32) * s, 'hy_conv_b': jnp.zeros((CONV_DIM,), jnp.float32), 'hy_dt_bias': jnp.log(jnp.expm1(jnp.full((H,), 0.01, jnp.float32))), 'hy_A_log': jnp.log(jnp.linspace(1.0, 16.0, H)).astype(jnp.float32), 'hy_D': jnp.ones((H,), jnp.float32), 'hy_fcD_w': jax.random.normal(ks[6], (H, D_INNER), jnp.float32) * s, 'hy_norm_w': jnp.ones((D_INNER,), jnp.float32), 'hy_out_w': jax.random.normal(ks[7], (D_INNER, D_INNER), jnp.float32) * s, 'out_w': jax.random.normal(ks[8], (dim, D_INNER), jnp.float32) * s, 'out_b': jnp.zeros((dim,), jnp.float32)}
    _L0_ffn_all = _L0_ffn_setup()
    _L0_ffn_in = {k: v for k, v in _L0_ffn_all.items() if k in ('W_fx', 'b_fx', 'W_x', 'b_x', 'W_slice', 'b_slice', 'temperature', 'hy_in_w', 'hy_conv_w', 'hy_conv_b', 'hy_dt_bias', 'hy_A_log', 'hy_D', 'hy_fcD_w', 'hy_norm_w', 'hy_out_w', 'out_w', 'out_b')}
    del _L0_ffn_all
    return {'x': x, 'adj': adj, 'L0_gnn_W_gcn': _L0_gnn_in['W_gcn'], 'L0_gnn_W_att': _L0_gnn_in['W_att'], 'L0_gnn_a_att': _L0_gnn_in['a_att'], 'L0_ffn_W_fx': _L0_ffn_in['W_fx'], 'L0_ffn_b_fx': _L0_ffn_in['b_fx'], 'L0_ffn_W_x': _L0_ffn_in['W_x'], 'L0_ffn_b_x': _L0_ffn_in['b_x'], 'L0_ffn_W_slice': _L0_ffn_in['W_slice'], 'L0_ffn_b_slice': _L0_ffn_in['b_slice'], 'L0_ffn_temperature': _L0_ffn_in['temperature'], 'L0_ffn_hy_in_w': _L0_ffn_in['hy_in_w'], 'L0_ffn_hy_conv_w': _L0_ffn_in['hy_conv_w'], 'L0_ffn_hy_conv_b': _L0_ffn_in['hy_conv_b'], 'L0_ffn_hy_dt_bias': _L0_ffn_in['hy_dt_bias'], 'L0_ffn_hy_A_log': _L0_ffn_in['hy_A_log'], 'L0_ffn_hy_D': _L0_ffn_in['hy_D'], 'L0_ffn_hy_fcD_w': _L0_ffn_in['hy_fcD_w'], 'L0_ffn_hy_norm_w': _L0_ffn_in['hy_norm_w'], 'L0_ffn_hy_out_w': _L0_ffn_in['hy_out_w'], 'L0_ffn_out_w': _L0_ffn_in['out_w'], 'L0_ffn_out_b': _L0_ffn_in['out_b']}

def reference(x, adj, L0_gnn_W_gcn, L0_gnn_W_att, L0_gnn_a_att, L0_ffn_W_fx, L0_ffn_b_fx, L0_ffn_W_x, L0_ffn_b_x, L0_ffn_W_slice, L0_ffn_b_slice, L0_ffn_temperature, L0_ffn_hy_in_w, L0_ffn_hy_conv_w, L0_ffn_hy_conv_b, L0_ffn_hy_dt_bias, L0_ffn_hy_A_log, L0_ffn_hy_D, L0_ffn_hy_fcD_w, L0_ffn_hy_norm_w, L0_ffn_hy_out_w, L0_ffn_out_w, L0_ffn_out_b):
    import jax
    import jax.numpy as jnp

    def _L0_gnn_ref(x, adj, k, W_gcn, W_att, a_att):
        import jax, jax.numpy as jnp
        import numpy as np
        MIN_NORM = 1e-15
        EPS = 1e-07
        MASK_FILL = -9000000000000000.0

        def logmap0(x, c):
            K = 1.0 / c
            sqrtK = K ** 0.5
            y = x[:, 1:]
            y_norm = jnp.clip(jnp.linalg.norm(y, axis=-1, keepdims=True), MIN_NORM)
            theta = jnp.clip(x[:, :1] / sqrtK, 1.0 + EPS)
            res = sqrtK * jnp.arccosh(theta) * y / y_norm
            return jnp.concatenate([jnp.zeros_like(x[:, :1]), res], axis=1)

        def proj(x, c):
            K = 1.0 / c
            y = x[:, 1:]
            x0 = jnp.sqrt(K + jnp.sum(y * y, axis=-1, keepdims=True))
            return jnp.concatenate([x0, y], axis=1)

        def expmap0(u, c):
            K = 1.0 / c
            sqrtK = K ** 0.5
            x = u[:, 1:]
            x_norm = jnp.clip(jnp.linalg.norm(x, axis=-1, keepdims=True), MIN_NORM)
            theta = x_norm / sqrtK
            res = jnp.concatenate([sqrtK * jnp.cosh(theta), sqrtK * jnp.sinh(theta) * x / x_norm], axis=1)
            return proj(res, c)
        c = float(k)
        N = x.shape[0]
        logx = logmap0(x, c)
        Wx = logx[:, 1:] @ W_gcn
        tmp = jnp.concatenate([jnp.zeros((N, 1), x.dtype), Wx], axis=1)
        fun7 = proj(expmap0(tmp, c), c)
        h_in = logmap0(fun7, c)
        h = h_in @ W_att
        F_ = h.shape[1]
        e = h @ a_att[:F_] + (h @ a_att[F_:]).T
        att = jnp.where(adj > 0, e, MASK_FILL)
        att = jax.nn.softmax(att, axis=1)
        h_prime = att @ h
        emb = jax.nn.elu(h_prime)
        emb = proj(emb, c)
        out = expmap0(jax.nn.sigmoid(logmap0(emb, c)), c)
        return out

    def _L0_ffn_ref(x, W_fx, b_fx, W_x, b_x, W_slice, b_slice, temperature, hy_in_w, hy_conv_w, hy_conv_b, hy_dt_bias, hy_A_log, hy_D, hy_fcD_w, hy_norm_w, hy_out_w, out_w, out_b):
        import jax, jax.numpy as jnp
        import numpy as np
        H, P, G, NS, K = (8, 64, 64, 64, 3)
        D_INNER = H * P
        CONV_DIM = D_INNER + 2 * NS
        D_IN_PROJ = 2 * D_INNER + 2 * NS + 2 * H

        def _hydra(u, in_w, conv_w, conv_b, dt_bias, A_log, Dp, fcD_w, norm_w, out_w):
            Bt, L, _ = u.shape
            zxbcdt = u @ in_w.T
            z = zxbcdt[..., :D_INNER]
            xBC = zxbcdt[..., D_INNER:D_INNER + CONV_DIM]
            dt = zxbcdt[..., -2 * H:]
            dt = jnp.concatenate([dt[..., :H], jnp.flip(dt[..., H:], axis=1)], axis=0)
            dt = jax.nn.softplus(dt + dt_bias)
            xp = jnp.pad(xBC, ((0, 0), (K - 1, 0), (0, 0)))
            xBC = sum((xp[:, k:k + L, :] * conv_w[:, k] for k in range(K))) + conv_b
            xBC = jax.nn.silu(xBC)
            x = xBC[..., :D_INNER]
            Bm = xBC[..., D_INNER:D_INNER + NS]
            Cm = xBC[..., D_INNER + NS:]
            x_og = x
            x2 = jnp.concatenate([x, jnp.flip(x, 1)], 0).reshape(2 * Bt, L, H, P)
            B2 = jnp.concatenate([Bm, jnp.flip(Bm, 1)], 0)
            C2 = jnp.concatenate([Cm, jnp.flip(Cm, 1)], 0)
            dA = jnp.exp(dt * -jnp.exp(A_log))
            dBx = jnp.einsum('blh,bln,blhp->blhpn', dt, B2, x2)

            def step(h, inp):
                dA_t, dBx_t, C_t = inp
                h = h * dA_t[:, :, None, None] + dBx_t
                return (h, jnp.einsum('bhpn,bn->bhp', h, C_t))
            h0 = jnp.zeros((2 * Bt, H, P, NS), u.dtype)
            _, ys = jax.lax.scan(step, h0, (dA.transpose(1, 0, 2), dBx.transpose(1, 0, 2, 3, 4), C2.transpose(1, 0, 2)))
            y = ys.transpose(1, 0, 2, 3).reshape(2 * Bt, L, D_INNER)
            y_fw, y_bw = (y[:Bt], jnp.flip(y[Bt:], 1))
            y = jnp.pad(y_fw[:, :-1], ((0, 0), (1, 0), (0, 0))) + jnp.pad(y_bw[:, 1:], ((0, 0), (0, 1), (0, 0)))
            y = y + x_og * jnp.repeat(x_og @ fcD_w.T + Dp, P, axis=-1)
            yg = y * jax.nn.silu(z)
            yg = yg * jax.lax.rsqrt(jnp.mean(jnp.square(yg), -1, keepdims=True) + 1e-05) * norm_w
            return yg @ out_w.T
        B, N, _ = x.shape
        fx = (x @ W_fx.T + b_fx).reshape(B, N, H, P).transpose(0, 2, 1, 3)
        xm = (x @ W_x.T + b_x).reshape(B, N, H, P).transpose(0, 2, 1, 3)
        temp = jnp.maximum(temperature, 1e-06)
        sw = jax.nn.softmax((xm @ W_slice.T + b_slice) / temp, axis=-1)
        snorm = sw.sum(2)
        st = jnp.einsum('bhnc,bhng->bhgc', fx, sw) / (snorm + 1e-05)[..., None]
        st = st.transpose(0, 2, 1, 3).reshape(B, G, D_INNER)
        ot = _hydra(st, hy_in_w, hy_conv_w, hy_conv_b, hy_dt_bias, hy_A_log, hy_D, hy_fcD_w, hy_norm_w, hy_out_w)
        ot = ot.reshape(B, G, H, P).transpose(0, 2, 1, 3)
        out = jnp.einsum('bhgc,bhng->bhnc', ot, sw).transpose(0, 2, 1, 3).reshape(B, N, D_INNER)
        return out @ out_w.T + out_b
    x = x + _L0_gnn_ref(_layernorm(x, axis=-1), adj, 1, L0_gnn_W_gcn, L0_gnn_W_att, L0_gnn_a_att)
    x = x + _L0_ffn_ref(_layernorm(x, axis=-1)[None], L0_ffn_W_fx, L0_ffn_b_fx, L0_ffn_W_x, L0_ffn_b_x, L0_ffn_W_slice, L0_ffn_b_slice, L0_ffn_temperature, L0_ffn_hy_in_w, L0_ffn_hy_conv_w, L0_ffn_hy_conv_b, L0_ffn_hy_dt_bias, L0_ffn_hy_A_log, L0_ffn_hy_D, L0_ffn_hy_fcD_w, L0_ffn_hy_norm_w, L0_ffn_hy_out_w, L0_ffn_out_w, L0_ffn_out_b)[0]
    return x

_drawn_inputs = setup_inputs


def setup_inputs(seed=0):
    import zlib

    import numpy as np

    out = dict(_drawn_inputs(seed))
    spreads = {'L0_ffn_b_fx': (0.0, 0.8),
     'L0_ffn_b_x': (0.0, 0.8),
     'L0_ffn_b_slice': (0.0, 0.8),
     'L0_ffn_temperature': (0.5, 0.6),
     'L0_ffn_hy_conv_b': (0.0, 0.8),
     'L0_ffn_hy_dt_bias': (-4.600166320800781, 0.6),
     'L0_ffn_hy_D': (1.0, 0.6),
     'L0_ffn_hy_norm_w': (1.0, 0.6),
     'L0_ffn_out_b': (0.0, 0.8)}
    factors = {'L0_ffn_W_fx': 7.986,
     'L0_ffn_W_x': 8.0,
     'L0_ffn_W_slice': 8.0,
     'L0_ffn_hy_in_w': 8.0,
     'L0_ffn_hy_conv_w': 8.0,
     'L0_ffn_hy_A_log': 8.0,
     'L0_ffn_hy_fcD_w': 8.0,
     'L0_ffn_hy_out_w': 7.975,
     'L0_ffn_out_w': 7.06}
    for name, (base, spread) in spreads.items():
        noise = np.random.default_rng([zlib.crc32(name.encode()), seed]).standard_normal(out[name].shape)
        drawn = base * np.exp(spread * noise) if base else spread * noise
        out[name] = jnp.asarray(drawn.astype(out[name].dtype))
    for name, factor in factors.items():
        out[name] = (out[name] * factor).astype(out[name].dtype)
    return out
```

```python
from contextlib import ExitStack

import numpy as np

import concourse.bass as bass
from concourse import mybir

F32 = mybir.dt.float32
F32R = mybir.dt.float32r
BF16 = mybir.dt.bfloat16
I32 = mybir.dt.int32
ALU = mybir.AluOpType
ACT = mybir.ActivationFunctionType
AXX = mybir.AxisListType.X

P = 128
D = 128
TA = 4
ROWS = TA * P
STEP = 1024
GROUP = 2
NBUF = 4
NTP = 4
NAT = 4
LEAD = 2
MASKED = -9.0e15
EPS1 = float(np.float32(1.0 + 1e-7) - np.float32(1.0))
MIN_NORM = 1e-15
SPREAD = 80.0

PRO_ROOTS = [(6, 5, -0.5), (7, 4, 0.5), (8, 3, 0.5), (10, 9, 0.5), (13, 12, 0.5), (13, 12, 0.5)]
PRO_ACTS = [(13, 12, ACT.Ln, 1.0), (10, 9, ACT.Exp, 1.0), (11, 9, ACT.Exp, -1.0), (13, 12, ACT.Ln, 1.0)]
EPI_ROOTS = [(2, 0, 2, 0.5), (5, 4, 1, 0.5), (15, 14, 1, 0.5), (21, 20, 1, 0.5), (24, 23, 1, -0.5)]
EPI_NR = len(EPI_ROOTS)
EPI_LINKS = 72
(F_UT, F_ZEXP, F_SILU, F_DTEXP, F_AD, F_XA, F_SEG, F_M, F_YQ, F_RMS, F_YN, F_OT, F_MO) = range(1, 14)
NFW = 18


def fetch_shapes(adj, in_w, fc):
    return adj.shape[0], in_w.shape[0], fc.shape[0]


def gnn_ffn(nc, x, adj, W_gcn, W_att, a_att, W_fx, b_fx, W_x, b_x, W_slice, b_slice, temperature,
            in_w, conv_w, conv_b, dt_bias, A_log, hy_D, fcD_w, norm_w, hy_out_w, out_w, out_b, out):
    N, DIP, H = fetch_shapes(adj, in_w, fcD_w)
    NT = N // P
    NSB = N // ROWS
    NQ = N // STEP
    NG = NT // GROUP
    GPQ = STEP // (GROUP * P)
    G = W_slice.shape[0]
    HD = W_slice.shape[1]
    DI = H * HD
    KC = DI // P
    NS = (conv_w.shape[0] - DI) // 2
    assert G == 64 and HD == 64 and NS == 64 and D == P and KC == 4 and NQ % NBUF == 0

    x1_d = nc.dram_tensor("x1_scratch", [N, D], F32).ap()
    sw_d = nc.dram_tensor("slice_weights_scratch", [N, H * G], F32).ap()
    t_d = nc.dram_tensor("t_scratch", [N], F32).ap()

    ctx = ExitStack()
    with ctx:
        def sem(name):
            return ctx.enter_context(nc.semaphore(name))

        def sb(name, shape, dt=F32, c=None):
            return (c or ctx).enter_context(nc.sbuf_tensor(name, shape, dt))

        tp = [ctx.enter_context(nc.psum_tensor(f"tp{i}", [P, 1024], BF16)) for i in range(NTP)]
        tpf = [t[:, :].bitcast(F32) for t in tp]
        acc = ctx.enter_context(nc.psum_tensor("acc", [P, 512], F32))
        pW = ctx.enter_context(nc.psum_tensor("pW", [P, 512], F32))
        pS = tpf[3]
        pL = ctx.enter_context(nc.psum_tensor("pL", [P, 512], F32))
        pST = ctx.enter_context(nc.psum_tensor("pST", [P, 512], F32))

        identb = sb("identb", [P, P], BF16)
        identf = sb("identf", [P, P])
        ones = sb("ones", [P, P])
        Wg = sb("Wg", [P, P])
        WA = sb("WA", [P, P])
        e0 = sb("e0", [P, 1])
        Hs = sb("Hs", [P, P])
        WcT = sb("WcT", [P, H * G])
        bl = sb("bl", [P, H * G])
        STacc = sb("STacc", [P, H * G])
        swsum = sb("swsum", [P, H * G])
        beta = sb("beta", [P, NT])
        tt = sb("tt", [P, NT])
        tm = sb("tm", [P, 8])
        flag = sb("flag", [P, 1], I32)
        csum = sb("csum", [P, 1])
        csb = sb("csb", [P, P])
        accS = sb("accS", [P, ROWS])
        xin = sb("xin", [P, TA, D])
        hp = sb("hp", [P, TA, D])
        ex = sb("ex", [P, TA, D])
        yy = sb("yy", [P, TA, D])
        sq = sb("sq", [P, TA, D])
        x1 = sb("x1", [P, TA, D])
        x1n = sb("x1n", [P, TA, D])
        x1nT = sb("x1nT", [P, ROWS])
        lg = sb("lg", [P, H * G])
        es = sb("es", [P, H * G])
        sw = sb("sw", [P, TA, H * G])
        r8 = sb("r8", [P, 2, H])
        c4 = sb("c4", [P, 32, TA])
        expo = sb("expo", [P, 2, NT])

        n64 = sw[:, :, :].rearrange("p a b -> p (a b)")[:, 0:24 * NT].rearrange("p (k n) -> p k n", n=NT)
        obB = sb("obB", [P, D])
        adjb = sb("adjb", [P, NBUF, TA * STEP], I32)
        early = ExitStack()
        V = sb("V", [P, NT, D], F32, early)
        early.close()
        late = ctx
        mask = sb("mask", [P, 2, TA, STEP], BF16, late)
        adjT = sb("adjT", [P, NAT, GROUP * ROWS], F32R, late)
        gs = ExitStack()
        ghi = sb("ghi", [P, NT, D], F32R, gs)
        glo = sb("glo", [P, NT, D], F32R, gs)
        gs.close()
        pro = ExitStack()
        xs = sb("xs", [P, 2, TA, D], F32, pro)
        xc = sb("xc", [P, 2, TA, D], F32, pro)
        xq = sb("xq", [P, 2, TA, D], F32, pro)
        xcT = sb("xcT", [P, 2, ROWS], F32, pro)
        vq = sb("vq", [P, 2, TA, D], F32, pro)
        Wx_n = sb("Wx_n", [HD, H, D], F32, pro)
        Wsl = sb("Wsl", [G, HD], F32, pro)
        WslT = sb("WslT", [HD, G], F32, pro)
        bxT = sb("bxT", [HD, H], F32, pro)
        bxB = sb("bxB", [HD, H, P], F32, pro)
        bsB = sb("bsB", [P, G], F32, pro)
        tmpB = sb("tmpB", [P, H], F32, pro)
        WAT = sb("WAT", [P, P], F32, pro)
        WgT = sb("WgT", [P, P], F32, pro)
        WAf = sb("WAf", [P, P], F32, pro)
        a2 = sb("a2", [P, 1], F32, pro)
        v2 = sb("v2", [P, 1], F32, pro)
        m2 = sb("m2", [2, 4], F32, pro)
        pro.close()
        gen = ExitStack()
        tb = sb("tb", [P, STEP], F32, gen)
        eb = sb("eb", [P, STEP], F32, gen)
        mb = sb("mb", [P, STEP], F32, gen)
        pT = sb("pT", [P, STEP], F32, gen)
        rm = sb("rm", [P, NQ + 2], F32, gen)
        gen.close()
        inw = sb("inw", [P, 10, DI])
        inT = sb("inT", [P, KC, DIP])
        AB = adjb[:, :, :].rearrange("p a b -> p (a b)").bitcast(F32)
        cut = [0]

        def ab(w):
            a = cut[0]
            cut[0] += w
            assert cut[0] <= NBUF * TA * STEP
            return AB[:, a:a + w]

        ow = ab(KC * DI).rearrange("p (a b) -> p a b", a=KC)
        oT = ab(KC * DI).rearrange("p (a b) -> p a b", a=KC)
        wf = ab(KC * D).rearrange("p (a b) -> p a b", a=KC)
        wfT = ab(DI)
        wo = ab(DI)
        woT = ab(KC * D).rearrange("p (a b) -> p a b", a=KC)
        fc = ab(DI)
        fcT = ab(KC * DI).rearrange("p (a b) -> p a b", a=KC)
        z6 = lambda n, w=G: ab(n * w).rearrange("p (a b) -> p a b", a=n)
        uT = z6(KC)
        zT = z6(KC)
        xb = z6(6, G + 2)
        xa = z6(6)
        xg = z6(6)
        xt = ab(DI)
        cw = ab(18).rearrange("p (a b) -> p a b", a=6)
        cb = ab(6)
        bfx = ab(KC)
        Dc = ab(KC)
        nw = ab(KC)
        dtb = ab(2 * H)
        Ae = ab(2 * H)
        dts = ab(12 * 2 * H).rearrange("p (a b) -> p a b", a=12)
        M1 = ab(G)
        M2 = ab(G)
        SN = ab(H * G)
        rS = ab(H * G)
        aF = ab(H * G)
        aB = ab(H * G)
        EF = ab(H * G)
        EB = ab(H * G)
        Csh = ab(2 * G)
        CB = ab(2 * G)
        sgz = z6(KC)
        yT = z6(KC)
        yq = z6(KC)
        rms = ab(G)
        otT = z6(KC)
        Mo = sb("Mo", [P, KC, D])
        swl = sb("swl", [P, 2, TA, H * G])
        x1l = sb("x1l", [P, 2, TA, D])
        swT = sb("swT", [P, 2, KC * P])
        yo = sb("yo", [P, 2, TA, D])

        s_w = sem("weights_loaded")
        s_id = sem("idents_made")
        s_one = sem("ones_made")
        s_wz = sem("weights_zeroed")
        s_tr = sem("weight_transposed")
        s_trc = sem("weight_copied")
        s_xs = [sem(f"x_loaded{b}") for b in range(2)]
        s_xfree = sem("x_used")
        s_xc = sem("x_centred")
        s_xqd = sem("x_squared")
        s_pT = sem("x_transposed")
        s_pTc = sem("x_transposed_copied")
        s_V = sem("V_product")
        s_Vc = sem("V_copied")
        s_Vq = sem("V_squared")
        s_ssv = sem("V_sums_done")
        s_pg = sem("roots_asked")
        s_pr = sem("roots_done")
        s_pa = sem("acts_asked")
        s_pd = sem("acts_done")
        s_mx = sem("extrema_ready")
        s_mxT = sem("extrema_transposed")
        s_m2 = sem("extrema_reduced")
        s_mb = sem("extrema_spread")
        s_flag = sem("flag_ready")
        s_beta = sem("beta_ready")
        s_cs = sem("column_sums")
        s_csb = sem("column_sums_spread")
        s_hs = sem("mean_product")
        s_hsc = sem("Hs_ready")
        s_wexp = sem("w_ready")
        s_gv = sem("g_ready")
        s_gh = sem("ghi_ready")
        s_gl = sem("glo_ready")
        ch = sem("dve_chain")
        che = sem("dve_epilogue_chain")
        chf = sem("dve_mixer_chain")
        chg = sem("dve_general_chain")
        s_adj = [sem(f"adj_loaded{b}") for b in range(NBUF)]
        s_mask = sem("mask_made")
        s_tp = sem("group_transposed")
        s_ev = sem("group_evacuated")
        s_mm = sem("group_multiplied")
        s_acc = sem("acc_done")
        s_accS = sem("acc_copied")
        s_xin = sem("xin_loaded")
        s_agg = sem("agg_done")
        s_hp = sem("hp_ready")
        s_ex = sem("exp_hp")
        s_y = sem("elu_ready")
        s_sq = sem("squares")
        s_rq = sem("epilogue_roots_asked")
        s_rt = sem("epilogue_roots")
        s_u = sem("log_asked")
        s_ln = sem("log_done")
        s_rr = sem("sigmoid_arg")
        s_en = sem("sigmoid_exp")
        s_sg = sem("sigmoid_ready")
        s_nn = sem("norm_ready")
        s_sh = sem("sinh_exps")
        s_x1 = sem("x1_ready")
        s_xc1 = sem("x1_centred")
        s_x1n = sem("x1n_ready")
        s_x1T = sem("x1n_transposed")
        s_x1Tc = sem("x1nT_copied")
        s_lg = sem("logits_product")
        s_lm = sem("logits_shifted")
        s_es = sem("logits_exp")
        s_sw = sem("sw_ready")
        s_sws = sem("swsum_added")
        s_st = sem("st_product")
        s_std = sem("st_added")
        s_x1o = sem("x1_stored")
        s_swo = sem("sw_stored")
        sp_tick = sem("sp_tick")
        pool_tick = sem("pool_tick")
        s_out = [sem(f"out_stored{b}") for b in range(2)]
        s_tst = sem("t_stored")
        s_tout = sem("t_written")
        s_gt = sem("general_t_loaded")
        s_ga = sem("general_adj_loaded")
        s_gh2 = sem("h_in_ready")
        s_gm = sem("general_chunk_used")
        s_ge = sem("general_logits")
        s_gp = sem("general_probabilities")
        s_gT = sem("general_transposed")
        s_gTc = sem("general_transposed_copied")
        s_gmm = sem("general_product")
        s_fw = sem("mixer_weights_loaded")
        s_ft = sem("mixer_transposed")
        s_ftc = sem("mixer_transposed_copied")
        s_fp = sem("mixer_product")
        s_fd = sem("mixer_dve")
        s_fa = sem("mixer_act")
        s_fg = sem("mixer_pool")
        s_fl = [sem(f"final_loaded{b}") for b in range(2)]
        s_flf = sem("final_load_used")
        s_fT = sem("sw_transposed")
        s_fTc = sem("sw_transposed_copied")
        s_fm = sem("final_product")
        s_fy = sem("final_sum")
        s_ob = sem("out_b_loaded")
        s_fTd = sem("sw_transposed_copied_by_dve")
        s_fy2 = sem("final_bank_free")
        s_x1b = sem("x1_with_out_b")
        s_gw = sem("V_scaled")
        chp = sem("dve_prologue_chain")
        chm = sem("dve_row_maximum_chain")

        def turned():
            for k in range(KC):
                for a0, a1 in ((0, 4), (4, 8), (8, 10)):
                    blocks = [(inw[0:min(P, DIP - a * P), a, k * P:(k + 1) * P], min(P, DIP - a * P))
                              for a in range(a0, a1)]
                    w = sum(n for _, n in blocks)
                    yield blocks, [(inT[:, k, a0 * P:a0 * P + w], lambda bank, w=w: bank[:, 0:w])]
            for k in range(KC):
                yield [(ow[:, a, k * P:(k + 1) * P], P) for a in range(KC)], [(oT[:, k, :], lambda bank: bank)]
            yield [(wf[:, a, :], P) for a in range(KC)], [(wfT, lambda bank: bank)]
            yield [(wo[:, k * P:(k + 1) * P], P) for k in range(KC)], \
                [(woT.rearrange("p a b -> p (a b)"), lambda bank: bank)]
            yield [(fc[0:H, k * P:(k + 1) * P], H) for k in range(KC)], \
                [(fcT[:, k, :].rearrange("p (h c) -> p h c", h=H),
                  lambda bank, k=k: bank[:, k * P:k * P + H].unsqueeze(2).to_broadcast([P, H, HD]))
                 for k in range(KC)]
        TURNED = list(turned())

        block = ctx.enter_context(nc.Block())

        x_v = x.rearrange("(s a p) d -> s p a d", a=TA, p=P)
        adj_v = adj.rearrange("(s a p) (q j) -> s q p a j", a=TA, p=P, j=STEP)
        x1_v = x1_d.rearrange("(s a p) d -> s p a d", a=TA, p=P)
        sw_v = sw_d.rearrange("(s a p) g -> s p a g", a=TA, p=P)
        out_v = out.rearrange("(s a p) d -> s p a d", a=TA, p=P)

        NW = 10

        def pos(v):
            return not isinstance(v, int) or v > 0

        def wait(eng, s, v):
            if pos(v):
                eng.wait_ge(s, v)

        @block.sync
        def _(sp):
            def wait_sp(s, v):
                wait(sp, s, v)
                if not isinstance(v, int):
                    sp.sem_inc(sp_tick, 1)

            with nc.allow_non_contiguous_dma(reason="small weights"):
                sp.wait_ge(s_wz, 4)
                sp.dma_start(Wg[1:P, 1:P], W_gcn).then_inc(s_w, 16)
                sp.dma_start(WA[1:P, :], W_att[1:P, :]).then_inc(s_w, 16)
                sp.dma_start(WAf[:, :], W_att).then_inc(s_w, 16)
                sp.dma_start(a2[:, :], a_att[P:2 * P, :]).then_inc(s_w, 16)
                for b in range(2):
                    sp.dma_start(xs[:, b, :, :], x_v[b, :, :, :]).then_inc(s_xs[b], 16)
                sp.dma_start(Wx_n[:, :, :], W_x.rearrange("(h q) d -> q h d", q=HD)).then_inc(s_w, 16)
                sp.dma_start(Wsl[:, :], W_slice).then_inc(s_w, 16)
                sp.dma_start(bxT[:, :], b_x.rearrange("(h q) -> q h", q=HD)).then_inc(s_w, 16)
                sp.dma_start(bsB[:, :], b_slice.rearrange("(a g) -> a g", a=1).to_broadcast([P, G]))\
                    .then_inc(s_w, 16)
                sp.dma_start(tmpB[:, :], temperature.rearrange("a h b c -> a (h b c)").to_broadcast([P, H]))\
                    .then_inc(s_w, 16)
                sp.dma_start(obB[:, :], out_b.rearrange("(a d) -> a d", a=1).to_broadcast([P, D]))\
                    .then_inc(s_ob, 16)
            with sp.Fori(1, NSB // 2) as g:
                for b in range(2):
                    wait_sp(s_xfree, 2 * g + b - 1)
                    sp.dma_start(xs[:, b, :, :], x_v[2 * g + b, :, :, :]).then_inc(s_xs[b], 16)

            def load_adj(s, q):
                if not (isinstance(s, int) and s == 0 and q < NBUF):
                    wait_sp(s_mask, NQ * s + q - NBUF + 1)
                sp.dma_start(adjb[:, q % NBUF, :].rearrange("p (a j) -> p a j", a=TA),
                             adj_v[s, q, :, :, :]).then_inc(s_adj[q % NBUF], 16)

            sp.wait_ge(s_flag, 1)
            one_shift = sp.value_load(flag[0:1, 0:1])
            with sp.If(one_shift > 0):
                for q in range(NQ):
                    load_adj(0, q)
                with sp.Fori(1, NSB) as s:
                    for q in range(NQ):
                        load_adj(s, q)
            with sp.Else():
                sp.wait_ge(s_tst, 1)
                with nc.allow_non_contiguous_dma(reason="one value per row"):
                    sp.dma_start(t_d.rearrange("(c p) -> p c", p=P), tt[:, :]).then_inc(s_tout, 16)
                sp.wait_ge(s_tout, 16)
                with sp.Fori(0, NSB) as s:
                    for a in range(TA):
                        for c in range(2 * NQ):
                            wait_sp(s_gm, (s * TA + a) * 2 * NQ + c)
                            sp.dma_start(adjb[:, 0, 0:STEP], adj_v[s, c % NQ, :, a, :]).then_inc(s_ga, 16)
                            sp.dma_start(tb[:, :], t_d[c % NQ * STEP:(c % NQ + 1) * STEP]
                                         .rearrange("(a j) -> a j", a=1).to_broadcast([P, STEP]))\
                                .then_inc(s_gt, 16)
            sp.wait_ge(s_std, NSB)
            sp.wait_ge(s_x1o, 16 * NSB)
            sp.wait_ge(s_swo, 16 * NSB)
            with nc.allow_non_contiguous_dma(reason="small weights"):
                sp.dma_start(inw[:, 0:9, :], in_w[0:9 * P, :].rearrange("(a p) k -> p a k", p=P)).then_inc(s_fw, 16)
                sp.dma_start(inw[0:DIP - 9 * P, 9, :], in_w[9 * P:DIP, :]).then_inc(s_fw, 16)
                sp.dma_start(ow, hy_out_w.rearrange("(a p) k -> p a k", p=P)).then_inc(s_fw, 16)
                sp.dma_start(wf, W_fx.rearrange("(a p) k -> p a k", p=P)).then_inc(s_fw, 16)
                sp.dma_start(wo, out_w).then_inc(s_fw, 16)
                sp.dma_start(fc[0:H, :], fcD_w).then_inc(s_fw, 16)
                sp.dma_start(cw[:, 0:KC, :], conv_w[0:DI, :].rearrange("(a p) k -> p a k", p=P)).then_inc(s_fw, 16)
                sp.dma_start(cw[0:NS, KC:6, :], conv_w[DI:, :].rearrange("(a p) k -> p a k", p=NS)).then_inc(s_fw, 16)
                sp.dma_start(cb[:, 0:KC], conv_b[0:DI].rearrange("(a p) -> p a", p=P)).then_inc(s_fw, 16)
                sp.dma_start(cb[0:NS, KC:6], conv_b[DI:].rearrange("(a p) -> p a", p=NS)).then_inc(s_fw, 16)
                sp.dma_start(bfx, b_fx.rearrange("(a p) -> p a", p=P)).then_inc(s_fw, 16)
                sp.dma_start(nw, norm_w.rearrange("(a p) -> p a", p=P)).then_inc(s_fw, 16)
                for half in range(2):
                    sp.dma_start(Dc[half * 64:half * 64 + 64, :],
                                 hy_D.rearrange("(c t) -> t c", t=2)[half:half + 1, :].to_broadcast([64, KC]))\
                        .then_inc(s_fw, 16)
                    sp.dma_start(dtb[0:G, half * H:half * H + H],
                                 dt_bias.rearrange("(a h) -> a h", a=1).to_broadcast([G, H])).then_inc(s_fw, 16)
                    sp.dma_start(Ae[0:G, half * H:half * H + H],
                                 A_log.rearrange("(a h) -> a h", a=1).to_broadcast([G, H])).then_inc(s_fw, 16)

            def load_final(s, b):
                sp.dma_start(swl[:, b, :, :], sw_v[s, :, :, :]).then_inc(s_fl[b], 16)
                sp.dma_start(x1l[:, b, :, :], x1_v[s, :, :, :]).then_inc(s_fl[b], 16)

            def store_final(s, b):
                wait_sp(s_fy, s + 1)
                sp.dma_start(out_v[s, :, :, :], yo[:, b, :, :]).then_inc(s_out[b], 16)

            for b in range(2):
                load_final(b, b)
            with sp.Fori(0, NSB // 2 - 1) as g:
                for b in range(2):
                    store_final(2 * g + b, b)
                    load_final(2 * g + b + 2, b)
            for b in range(2):
                store_final(NSB - 2 + b, b)
            for b in range(2):
                sp.wait_ge(s_out[b], 16 * (NSB // 2))

        @block.gpsimd
        def _(pool):
            def wait_pool(s, v):
                wait(pool, s, v)
                if not isinstance(v, int):
                    pool.sem_inc(pool_tick, 1)

            pool.memset(Wg[:, :], 0.0).then_inc(s_wz, 1)
            pool.memset(WA[:, :], 0.0).then_inc(s_wz, 1)
            pool.memset(e0[:, :], 0.0).then_inc(s_wz, 1)
            pool.wait_ge(s_wz, 3)
            pool.memset(e0[0:1, :], 1.0).then_inc(s_wz, 1)
            pool.memset(ones[:, :], 1.0).then_inc(s_one, 1)
            pool.memset(swsum[:, :], 0.0).then_inc(s_one, 1)
            pool.memset(identf[:, :], 0.0).then_inc(s_id, 1)
            pool.memset(identb[:, :], 0.0).then_inc(s_id, 1)
            pool.wait_ge(s_id, 2)
            for m in (identf, identb):
                pool.affine_select(out=m[:, :], in_=m[:, :], compare_op=ALU.not_equal, fill=1.0, base=0,
                                   pattern=[[-1, P]], channel_multiplier=1).then_inc(s_id, 1)

            pool.memset(expo[:, 0, :], 0.5).then_inc(s_one, 1)
            pool.memset(expo[:, 1, :], -0.5).then_inc(s_one, 1)
            pool.wait_ge(s_one, 4)

            def root(out_ap, in_ap, power, asked, n, done):
                wait_pool(asked, n)
                w = expo[:, 0 if power > 0 else 1, 0:int(np.prod(in_ap.shape[1:]))]
                if len(in_ap.shape) == 3:
                    w = w.rearrange("p (a b) -> p a b", a=in_ap.shape[1])
                pool.tensor_tensor(out_ap, in_ap, w, ALU.pow).then_inc(done, 1)

            for k, (o, i, w) in enumerate(PRO_ROOTS):
                root(n64[:, o, :], n64[:, i, :], w, s_pg, k + 1, s_pr)

            def roots(e, k):
                o, i, n, power = EPI_ROOTS[k]
                root(c4[:, o:o + n, :], c4[:, i:i + n, :], power, s_rq, EPI_NR * e + k + 1, s_rt)

            def add_sw(e, a):
                wait_pool(s_sw, TA * e + a + 1)
                wait_pool(s_sws, TA * e + a)
                pool.tensor_tensor(swsum[:, :], swsum[:, :], sw[:, a, :], ALU.add).then_inc(s_sws, 1)

            def behind(e):
                for k in range(EPI_NR):
                    roots(e, k)
                for a in range(TA):
                    add_sw(e, a)

            pool.wait_ge(s_flag, 1)
            one_shift = pool.value_load(flag[0:1, 0:1])
            with pool.If(one_shift > 0):
                with pool.Fori(0, NSB) as e:
                    behind(e)
            with pool.Else():
                with pool.Fori(0, NSB) as e:
                    behind(e)
            pool.wait_ge(s_std, NSB)
            pool.memset(M1[0:G, :], 1.0).then_inc(s_fg, 1)
            pool.memset(M2[0:G, :], 1.0).then_inc(s_fg, 1)
            pool.wait_ge(s_fg, 2)
            pool.affine_select(out=M1[0:G, :], in_=M1[0:G, :], compare_op=ALU.is_gt, fill=0.0, base=0,
                               pattern=[[1, G]], channel_multiplier=-1).then_inc(s_fg, 1)
            pool.affine_select(out=M2[0:G, :], in_=M2[0:G, :], compare_op=ALU.is_gt, fill=0.0, base=0,
                               pattern=[[-1, G]], channel_multiplier=1).then_inc(s_fg, 1)
            pool.wait_ge(s_fd, F_RMS)
            pool.tensor_tensor(rms, rms, expo[:, 1, 0:G], ALU.pow).then_inc(s_fg, 1)

        @block.scalar
        def _(act):
            with act.Fori(0, NSB // 2) as g:
                for b in range(2):
                    k = 2 * g + b
                    act.wait_ge(s_xc, k + 1)
                    act.activation(xq[:, b, :, :], xc[:, b, :, :], ACT.Square).then_inc(s_xqd, 1)
                    act.wait_ge(s_pT, k + 1)
                    act.activation(xcT[:, b, :], tpf[b], ACT.Copy).then_inc(s_pTc, 1)
                    act.wait_ge(s_V, k + 1)
                    pv = (pW, pL)[b]
                    act.activation(V[:, bass.ds(TA * k, TA), :].rearrange("p a d -> p (a d)"), pv[:, :],
                                   ACT.Copy).then_inc(s_Vc, 1)
                    act.activation(vq[:, b, :, :].rearrange("p a d -> p (a d)"), pv[:, :], ACT.Square)\
                        .then_inc(s_Vq, 1)
            for k, (o, i, f, sc) in enumerate(PRO_ACTS):
                act.wait_ge(s_pa, k + 1)
                act.activation(n64[:, o, :], n64[:, i, :], f, scale=sc).then_inc(s_pd, 1)
            act.wait_ge(s_flag, 1)

            def copy_acc(e, general):
                act.wait_ge(*((s_acc, e + 1) if general else (s_mm, NG * e + NG)))
                act.activation(accS[:, :], acc[:, :], ACT.Copy).then_inc(s_accS, 1)

            def exp_hp(e):
                act.wait_ge(s_hp, e + 1)
                act.activation(ex[:, :, :], ex[:, :, :], ACT.Exp).then_inc(s_ex, 1)

            def square(e, k, src, ready):
                act.wait_ge(ready, e + 1)
                act.activation(sq[:, :, :], src[:, :, :], ACT.Square).then_inc(s_sq, 1)

            def log(e):
                act.wait_ge(s_u, e + 1)
                act.activation(c4[:, 8, :], c4[:, 7, :], ACT.Ln).then_inc(s_ln, 1)

            def exp_rr(e):
                act.wait_ge(s_rr, e + 1)
                act.activation(ex[:, :, :], hp[:, :, :], ACT.Exp, scale=-1.0).then_inc(s_en, 1)

            def exp_norm(e):
                act.wait_ge(s_nn, e + 1)
                act.activation(c4[:, 16, :], c4[:, 15, :], ACT.Exp).then_inc(s_sh, 1)
                act.activation(c4[:, 17, :], c4[:, 15, :], ACT.Exp, scale=-1.0).then_inc(s_sh, 1)

            def copy_x1nT(e):
                act.wait_ge(s_x1T, e + 1)
                act.activation(x1nT[:, :], pW[:, :], ACT.Copy).then_inc(s_x1Tc, 1)

            def exp_logits(e, a):
                act.wait_ge(s_lm, TA * e + a + 1)
                wait(act, s_sw, TA * e + a)
                act.activation(es[:, :], lg[:, :], ACT.Exp).then_inc(s_es, 1)

            def load_x(e):
                wait(act, s_x1, e)
                act.dma_start(xin[:, :, :], x_v[e, :, :, :]).then_inc(s_xin, 16)

            def store_x1(e):
                act.wait_ge(s_x1, e + 1)
                act.dma_start(x1_v[e, :, :, :], x1[:, :, :]).then_inc(s_x1o, 16)

            def store_sw(e):
                act.wait_ge(s_sw, TA * e + TA)
                act.dma_start(sw_v[e, :, :, :], sw[:, :, :]).then_inc(s_swo, 16)

            def behind(e, n, general=False):
                if n == 0:
                    copy_acc(e, general)
                    load_x(e)
                if n == 3:
                    exp_hp(e)
                if n == 5:
                    square(e, 0, yy, s_y)
                if n == 9:
                    log(e)
                if n == 11:
                    exp_rr(e)
                if n == 13:
                    square(e, 1, yy, s_sg)
                if n == 15:
                    exp_norm(e)
                if n == 18:
                    square(e, 2, x1n, s_xc1)
                    store_x1(e)
                if n == 21:
                    copy_x1nT(e)
                if n >= 24 and n % 2 == 0 and n < 32:
                    exp_logits(e, (n - 24) // 2)
                if n == NG - 1:
                    store_sw(e)

            def evacuate(s, n):
                k = NG * s + n
                act.wait_ge(s_tp, k + 1)
                if not (isinstance(s, int) and k < NAT):
                    act.wait_ge(s_mm, k - NAT + 1)
                act.activation(adjT[:, n % NAT, :], tp[n % NTP][:, :], ACT.Copy).then_inc(s_ev, 1)

            one_shift = act.value_load(flag[0:1, 0:1])
            with act.If(one_shift > 0):
                act.activation(n64[:, 23, :], tt[:, :], ACT.Exp, bias=tm[:, 3:4]).then_inc(s_wexp, 1)
                for c in range(4):
                    act.wait_ge(s_gv, c + 1)
                    act.activation(ghi[:, c * 16:c * 16 + 16, :], V[:, c * 16:c * 16 + 16, :], ACT.Copy)\
                        .then_inc(s_gh, 1)
                act.wait_ge(s_gl, 4)
                for n in range(NG):
                    evacuate(0, n)
                with act.Fori(1, NSB) as s:
                    for n in range(NG):
                        behind(s - 1, n)
                        evacuate(s, n)
                for n in range(NG):
                    behind(NSB - 1, n)
            with act.Else():
                with act.Fori(0, NSB) as s:
                    for a in range(TA):
                        for c in range(NQ):
                            k = (s * TA + a) * NQ + c
                            act.wait_ge(s_ge, k + 1)
                            act.activation(eb[:, :], eb[:, :], ACT.Exp, bias=rm[:, NQ + 1:NQ + 2])\
                                .then_inc(s_gp, 1)
                            act.wait_ge(s_gT, k + 1)
                            act.activation(pT[:, 0:512], pW[:, :], ACT.Copy).then_inc(s_gTc, 1)
                            act.activation(pT[:, 512:1024], pL[:, :], ACT.Copy).then_inc(s_gTc, 1)
                    for n in range(NG):
                        behind(s, n, general=True)


            def fa(need, *args, **kw):
                act.wait_ge(s_fd, need)
                act.activation(*args, **kw).then_inc(s_fa, 1)
            fa(F_SILU, xg[:, 0:KC, :], xa[:, 0:KC, :], ACT.Exp, scale=-1.0)
            act.activation(xg[0:NS, KC:6, :], xa[0:NS, KC:6, :], ACT.Exp, scale=-1.0).then_inc(s_fa, 1)
            fa(F_ZEXP, sgz, zT, ACT.Exp, scale=-1.0)
            act.wait_ge(s_fw, 16 * NFW)
            act.activation(Ae[0:G, :], Ae[0:G, :], ACT.Exp).then_inc(s_fa, 1)
            fa(F_DTEXP, dts[0:G, 2, :], dts[0:G, 1, :], ACT.Exp)
            fa(F_SEG, EF[0:G, :], EF[0:G, :], ACT.Exp)
            act.activation(EB[0:G, :], EB[0:G, :], ACT.Exp).then_inc(s_fa, 1)
            with act.Fori(0, NSB // 2) as g:
                for b in range(2):
                    for a in range(0, TA, 2):
                        k = (2 * g + b) * TA + a
                        act.wait_ge(s_fT, k + 1)
                        act.activation(swT[:, a % 2, :], tpf[a % 2], ACT.Copy).then_inc(s_fTc, 1)

        @block.tensor
        def _(pe):
            def mm(out_ap, lhsT, rhs, start=True, stop=True):
                return pe.matmul(out_ap, lhsT, rhs, start=start, stop=stop)

            pe.wait_ge(s_id, 4)
            pe.wait_ge(s_one, 2)
            pe.wait_ge(s_w, 16 * 9)
            pe.transpose(pW[:, 0:P], WAf[:, :], identf[:, :]).then_inc(s_tr, 1)
            pe.transpose(pL[:, 0:P], Wg[:, :], identf[:, :]).then_inc(s_tr, 1)
            pe.transpose(pS[0:HD, 0:G], Wsl[:, :], identf[0:G, 0:G]).then_inc(s_tr, 1)
            pe.wait_ge(s_trc, 3)
            mm(pST[:, 0:1], WAT[:, :], a2[:, :]).then_inc(s_tr, 1)
            pe.wait_ge(s_trc, 4)
            mm(pST[:, 2:3], WgT[:, :], v2[:, :]).then_inc(s_tr, 1)
            for h in range(H):
                last = mm(acc[:, h * G:(h + 1) * G], Wx_n[:, h, :], WslT[:, :])
            last.then_inc(s_tr, 1)
            pe.wait_ge(s_trc, 6)
            for h in range(H):
                last = mm(pS[:, h * G:(h + 1) * G], bxB[:, h, :], WslT[:, :])
            last.then_inc(s_tr, 1)
            pe.wait_ge(s_trc, 5)
            with pe.Fori(0, NSB // 2) as g:
                for b in range(2):
                    k = 2 * g + b
                    pe.wait_ge(s_xc, k + 1)
                    for a in range(TA):
                        last = pe.transpose(tpf[b][:, a * P:(a + 1) * P], xc[:, b, a, :], identf[:, :])
                    last.then_inc(s_pT, 1)
                    pe.wait_ge(s_pTc, k + 1)
                    for a in range(TA):
                        last = mm((pW, pL)[b][:, a * P:(a + 1) * P], xcT[:, b, a * P:(a + 1) * P], Wg[:, :])
                    last.then_inc(s_V, 1)
            pe.wait_ge(s_mx, 1)
            pe.transpose(pST[0:2, 0:P], tm[:, 0:2], identf[:, :]).then_inc(s_mxT, 1)
            pe.wait_ge(s_m2, 1)
            mm(pST[:, 256:258], ones[0:2, :], m2[:, 2:4]).then_inc(s_mb, 1)
            pe.wait_ge(s_beta, 1)
            for c in range(NT):
                last = mm(pL[:, 0:1], V[:, c, :], beta[:, c:c + 1], start=c == 0, stop=c == NT - 1)
            last.then_inc(s_cs, 1)
            pe.wait_ge(s_csb, 1)
            mm(pW[:, 0:P], csb[:, :], WA[:, :]).then_inc(s_hs, 1)

            def transposes(s, n):
                k = NG * s + n
                if n % GPQ == 0:
                    pe.wait_ge(s_mask, NQ * s + n // GPQ + 1)
                if not (isinstance(s, int) and k < NTP):
                    pe.wait_ge(s_ev, k - NTP + 1)
                q = n // GPQ
                for c in range(GROUP):
                    j = (n % GPQ) * GROUP + c
                    for a in range(TA):
                        last = pe.transpose(tp[n % NTP][:, c * ROWS + a * P:c * ROWS + (a + 1) * P],
                                            mask[:, q % 2, a, j * P:(j + 1) * P], identb[:, :])
                last.then_inc(s_tp, 1)

            def products(s, n):
                k = NG * s + n
                if n == 0 and not (isinstance(s, int) and s == 0):
                    pe.wait_ge(s_accS, s)
                pe.wait_ge(s_ev, k + 1)
                for c in range(GROUP):
                    jc = n * GROUP + c
                    for half in (ghi, glo):
                        last = mm(acc[:, :], half[:, jc, :], adjT[:, n % NAT, c * ROWS:(c + 1) * ROWS],
                                  start=jc == 0 and half is ghi, stop=jc == NT - 1 and half is glo)
                last.then_inc(s_mm, 1)

            def aggregate(e):
                pe.wait_ge(s_accS, e + 1)
                for a in range(TA):
                    mm(pW[:, a * P:(a + 1) * P], accS[:, a * P:(a + 1) * P], WA[:, :])
                for a in range(TA):
                    last = mm(pL[:, a:a + 1], accS[:, a * P:(a + 1) * P], e0[:, :])
                last.then_inc(s_agg, 1)

            def turn_x1n(e):
                pe.wait_ge(s_x1n, e + 1)
                for a in range(TA):
                    last = pe.transpose(pW[:, a * P:(a + 1) * P], x1n[:, a, :], identf[:, :])
                last.then_inc(s_x1T, 1)

            def logits(e, a):
                pe.wait_ge(s_x1Tc, e + 1)
                wait(pe, s_lm, TA * e + a)
                mm(pL[:, :], x1nT[:, a * P:(a + 1) * P], WcT[:, :]).then_inc(s_lg, 1)

            def slices(e, a):
                pe.wait_ge(s_sw, TA * e + a + 1)
                if a == 0:
                    wait(pe, s_std, e)
                last = mm(pST[:, :], x1n[:, a, :], sw[:, a, :], start=a == 0, stop=a == TA - 1)
                if a == TA - 1:
                    last.then_inc(s_st, 1)

            def behind(e, n):
                if n == 1:
                    aggregate(e)
                if n == 20:
                    turn_x1n(e)
                if n >= 22 and n % 2 == 0 and n < 30:
                    logits(e, (n - 22) // 2)
                if n >= 26 and n % 2 == 0:
                    slices(e, (n - 26) // 2)
                if n == NG - 1:
                    slices(e, TA - 1)

            one_shift = pe.value_load(flag[0:1, 0:1])
            with pe.If(one_shift > 0):
                pe.wait_ge(s_gl, 4)
                pe.wait_ge(s_hsc, 1)
                for n in range(LEAD):
                    transposes(0, n)

                def stream(s, first, final):
                    for n in range(NG):
                        if n + LEAD < NG:
                            transposes(s, n + LEAD)
                        elif not final:
                            transposes(s + 1, n + LEAD - NG)
                        if not first:
                            behind(s - 1, n)
                        products(s, n)

                stream(0, True, False)
                with pe.Fori(1, NSB - 1) as s:
                    stream(s, False, False)
                stream(NSB - 1, False, True)
                for n in range(NG):
                    behind(NSB - 1, n)
            with pe.Else():
                pe.wait_ge(s_gh2, 1)
                pe.wait_ge(s_hsc, 1)
                with pe.Fori(0, NSB) as s:
                    for a in range(TA):
                        for c in range(NQ):
                            k = (s * TA + a) * NQ + c
                            pe.wait_ge(s_gp, k + 1)
                            for j in range(8):
                                last = pe.transpose((pW, pL)[j // 4][:, j % 4 * P:(j % 4 + 1) * P],
                                                    eb[:, j * P:(j + 1) * P], identf[:, :])
                            last.then_inc(s_gT, 1)
                            pe.wait_ge(s_gTc, 2 * k + 2)
                            for j in range(8):
                                last = mm(acc[:, a * P:(a + 1) * P], V[:, c * 8 + j, :], pT[:, j * P:(j + 1) * P],
                                          start=c == 0 and j == 0, stop=c == NQ - 1 and j == 7)
                    last.then_inc(s_acc, 1)
                    for n in range(NG):
                        behind(s, n)

            pe.wait_ge(s_fw, 16 * NFW)
            for k, (blocks, _) in enumerate(TURNED):
                bank = (tpf[0], tpf[1], tpf[2])[k % 3]
                if k >= 3:
                    pe.wait_ge(s_ftc, k - 2)
                for j, (src, n) in enumerate(blocks):
                    last = pe.transpose(bank[:, j * P:j * P + n], src, identf[0:n, 0:n])
                last.then_inc(s_ft, 1)
            pe.wait_ge(s_sws, TA * NSB)
            mm(pW[:, :], ones[:, :], swsum[:, :]).then_inc(s_fp, 1)
            pe.wait_ge(s_ftc, len(TURNED))
            for h in range(H):
                r = (h % 2) * 64
                last = mm(pL[r:r + 64, (h // 2) * G:(h // 2 + 1) * G], wfT[:, h * HD:(h + 1) * HD],
                          STacc[:, h * G:(h + 1) * G])
            last.then_inc(s_fp, 1)
            pe.wait_ge(s_fd, F_UT)
            for c in range(KC):
                for k in range(KC):
                    last = mm(pS[:, c * G:(c + 1) * G], inT[:, k, c * P:(c + 1) * P], uT[:, k, :], k == 0, k == KC - 1)
            for c in range(KC):
                for k in range(KC):
                    last = mm(pST[:, c * G:(c + 1) * G], inT[:, k, DI + c * P:DI + (c + 1) * P], uT[:, k, :],
                              k == 0, k == KC - 1)
            for c in range(2):
                a = 2 * DI + c * NS
                for k in range(KC):
                    last = mm(acc[0:NS, c * G:(c + 1) * G], inT[:, k, a:a + NS], uT[:, k, :], k == 0, k == KC - 1)
            for k in range(KC):
                last = mm(tpf[0][0:G, 0:2 * H], uT[:, k, :], inT[:, k, DIP - 2 * H:DIP], k == 0, k == KC - 1)
            last.then_inc(s_fp, 1)
            pe.wait_ge(s_fd, F_AD)
            pe.wait_ge(s_fg, 4)
            mm(tpf[1][0:G, :], M2[0:G, :], aF[0:G, :])
            mm(tpf[2][0:G, :], M1[0:G, :], aB[0:G, :]).then_inc(s_fp, 1)
            pe.wait_ge(s_fd, F_XA)
            for c in range(KC):
                pe.transpose(pL[0:G, c * P:(c + 1) * P], xa[:, c, :], identf[:, :])
            mm(tpf[0][0:G, 64:64 + 2 * G], xa[0:NS, KC, :], Csh[0:NS, :])
            for c in range(KC):
                for k in range(KC):
                    last = mm(pW[:, c * G:(c + 1) * G], fcT[:, k, c * P:(c + 1) * P], xa[:, k, :], k == 0, k == KC - 1)
            last.then_inc(s_fp, 1)
            pe.wait_ge(s_fd, F_M)
            for h in range(H):
                r = (h % 2) * 64
                last = mm(acc[r:r + 64, (h // 2) * G:(h // 2 + 1) * G], xt[0:G, h * HD:(h + 1) * HD],
                          EF[0:G, h * G:(h + 1) * G])
            last.then_inc(s_fp, 1)
            pe.wait_ge(s_fd, F_YQ)
            for c in range(KC):
                last = mm(tpf[1][:, 0:G], ones[:, :], yq[:, c, :], c == 0, c == KC - 1)
            last.then_inc(s_fp, 1)
            pe.wait_ge(s_fd, F_YN)
            for c in range(KC):
                for k in range(KC):
                    last = mm(tpf[2][:, c * G:(c + 1) * G], oT[:, k, c * P:(c + 1) * P], yT[:, k, :], k == 0, k == KC - 1)
            last.then_inc(s_fp, 1)
            pe.wait_ge(s_fd, F_OT)
            for h in range(H):
                r = (h % 2) * 64
                last = mm(pW[r:r + 64, (h // 2) * D:(h // 2 + 1) * D], otT[r:r + 64, h // 2, :],
                          woT[r:r + 64, h // 2, :])
            last.then_inc(s_fp, 1)
            pe.wait_ge(s_fd, F_MO)

            with pe.Fori(0, NSB // 2) as g:
                for b in range(2):
                    s = 2 * g + b
                    pe.wait_ge(s_fl[b], 32 * g + 32)
                    for a in range(TA):
                        k = s * TA + a
                        for c in range(KC):
                            last = pe.transpose(tpf[a % 2][:, c * P:(c + 1) * P], swl[:, b, a, c * P:(c + 1) * P],
                                                identf[:, :])
                        last.then_inc(s_fT, 1)
                        if a % 2 == 1:
                            for aa in (a - 1, a):
                                pe.wait_ge((s_fTc, s_fTd)[aa % 2], 2 * s + a // 2 + 1)
                                if aa == 0:
                                    pe.wait_ge(s_fy2, s + 1)
                                for c in range(KC):
                                    last = mm((pW, pL)[b][:, aa * P:(aa + 1) * P], swT[:, aa % 2, c * P:(c + 1) * P],
                                              Mo[:, c, :], c == 0, c == KC - 1)
                    last.then_inc(s_fm, 1)

        @block.vector
        def _(dve):
            cnt = {}

            def linker(s):
                cnt[s.name] = 0

                def link(ins, wait=True):
                    ins.then_inc(s, 1)
                    cnt[s.name] += 1
                    if wait:
                        dve.wait_ge(s, cnt[s.name])
                    return ins
                return link
            link = linker(ch)
            ts, tts = dve.tensor_scalar, dve.tensor_tensor

            def log1p(link, u, ln, o, t1, t2, cap=0.5):
                link(ts(t1, u, cap, None, ALU.min))
                link(ts(t2, t1, 2.0, None, ALU.add))
                link(dve.reciprocal(t2, t2))
                link(tts(t1, t1, t2, ALU.mult))
                link(tts(t2, t1, t1, ALU.mult))
                odd = (17, 15, 13, 11, 9, 7, 5, 3) if cap > 0.5 else (13, 11, 9, 7, 5, 3)
                link(ts(o, t2, 1.0 / odd[0], 1.0 / odd[1], ALU.mult, ALU.add))
                for k in odd[2:] + (1,):
                    link(tts(o, o, t2, ALU.mult))
                    link(ts(o, o, 1.0 / k, None, ALU.add))
                link(tts(o, o, t1, ALU.mult))
                link(ts(o, o, 2.0, None, ALU.mult))
                if ln is not None:
                    link(ts(t1, u, cap, None, ALU.is_gt))
                    link(tts(t2, ln, o, ALU.subtract))
                    link(tts(t2, t2, t1, ALU.mult))
                    link(tts(o, o, t2, ALU.add))

            dve.wait_ge(s_tr, 1)
            dve.tensor_copy(WAT[:, :], pW[:, 0:P]).then_inc(s_trc, 1)
            dve.wait_ge(s_tr, 2)
            dve.tensor_copy(WgT[:, :], pL[:, 0:P]).then_inc(s_trc, 1)
            dve.wait_ge(s_tr, 3)
            dve.tensor_copy(WslT[:, :], pS[0:HD, 0:G]).then_inc(s_trc, 1)
            dve.wait_ge(s_tr, 4)
            dve.tensor_copy(v2[:, :], pST[:, 0:1]).then_inc(s_trc, 1)
            dve.wait_ge(s_tr, 5)
            dve.tensor_copy(Wg[:, 0:1], pST[:, 2:3]).then_inc(s_trc, 1)
            dve.tensor_copy(bxB[:, :, :], bxT[:, :].unsqueeze(2).to_broadcast([HD, H, P])).then_inc(s_trc, 1)
            link(ts(tmpB[:, :], tmpB[:, :], 1e-6, None, ALU.max))
            link(dve.reciprocal(tmpB[:, :], tmpB[:, :]))
            dve.wait_ge(s_tr, 6)
            hg = lambda ap: ap.rearrange("p (h g) -> p h g", h=H)
            link(tts(hg(WcT[:, :]), hg(acc[:, :]), tmpB[:, :].unsqueeze(2).to_broadcast([P, H, G]), ALU.mult))
            dve.wait_ge(s_tr, 7)
            link(tts(hg(bl[:, :]), hg(pS[:, :]), bsB[:, :].unsqueeze(1).to_broadcast([P, H, G]), ALU.add))
            link(tts(hg(bl[:, :]), hg(bl[:, :]), tmpB[:, :].unsqueeze(2).to_broadcast([P, H, G]), ALU.mult))
            link(dve.memset(STacc[:, :], 0.0))
            N64 = lambda k: n64[:, k, :]
            PER = 5
            with dve.Fori(0, NSB // 2) as g:
                k0 = [0]

                def step(ins):
                    k0[0] += 1
                    ins.then_inc(chp, 1)
                    dve.wait_ge(chp, g * 2 * PER + k0[0])
                for b in range(2):
                    k = 2 * g + b
                    col = bass.ds(TA * k, TA)
                    dve.wait_ge(s_xs[b], 16 * g + 16)
                    step(dve.tensor_reduce(n64[:, 0, col], xs[:, b, :, :], AXX, ALU.add))
                    step(ts(n64[:, 0, col], n64[:, 0, col], 1.0 / D, None, ALU.mult))
                    dve.wait_ge(s_pT, k)
                    tts(xc[:, b, :, :], xs[:, b, :, :], n64[:, 0, col].unsqueeze(2).to_broadcast([P, TA, D]),
                        ALU.subtract).then_inc(s_xc, 1)
                    dve.wait_ge(s_xc, k + 1)
                    dve.tensor_copy(n64[:, 2, col], xc[:, b, :, 0]).then_inc(s_xfree, 1)
                    dve.wait_ge(s_xqd, k + 1)
                    step(dve.tensor_reduce(n64[:, 4, col], xq[:, b, :, 1:D], AXX, ALU.add))
                    step(tts(n64[:, 1, col], n64[:, 4, col], xq[:, b, :, 0], ALU.add))
                    dve.wait_ge(s_Vq, k + 1)
                    step(dve.tensor_reduce(n64[:, 3, col], vq[:, b, :, 1:D], AXX, ALU.add))
                assert k0[0] == 2 * PER

            asked = [0, 0]

            def root():
                asked[0] += 1
                dve.sem_inc(s_pg, 1)
                dve.wait_ge(s_pr, asked[0])

            def hand_act(n=1):
                asked[1] += n
                dve.sem_inc(s_pa, n)
                dve.wait_ge(s_pd, asked[1])

            link(ts(N64(5), N64(1), 1.0 / D, 1e-5, ALU.mult, ALU.add))
            root()
            root()
            root()
            link(tts(N64(2), N64(2), N64(6), ALU.mult))
            link(ts(N64(2), N64(2), -1.0, EPS1, ALU.add, ALU.max))
            link(ts(N64(9), N64(2), 2.0, None, ALU.add))
            link(tts(N64(9), N64(9), N64(2), ALU.mult))
            root()
            link(tts(N64(11), N64(10), N64(2), ALU.add))
            link(ts(N64(12), N64(11), 1.0, None, ALU.add))
            hand_act()
            log1p(link, N64(11), N64(13), N64(14), N64(15), N64(16))
            link(tts(N64(7), N64(7), N64(6), ALU.mult))
            link(ts(N64(7), N64(7), MIN_NORM, None, ALU.max))
            link(dve.reciprocal(N64(7), N64(7)))
            link(tts(N64(14), N64(14), N64(7), ALU.mult))
            link(tts(N64(14), N64(14), N64(6), ALU.mult))
            link(tts(N64(8), N64(8), N64(14), ALU.mult))
            link(ts(N64(9), N64(8), MIN_NORM, None, ALU.max))
            hand_act(2)
            link(dve.reciprocal(N64(12), N64(9)))
            link(tts(N64(10), N64(10), N64(11), ALU.subtract))
            link(tts(N64(10), N64(10), N64(12), ALU.mult))
            link(ts(N64(10), N64(10), 0.5, None, ALU.mult))
            link(ts(N64(11), N64(9), 1.0, None, ALU.min))
            link(tts(N64(11), N64(11), N64(11), ALU.mult))
            link(ts(N64(12), N64(11), 1.0 / 72, 1.0, ALU.mult, ALU.add))
            for k in (42.0, 20.0, 6.0):
                link(tts(N64(12), N64(12), N64(11), ALU.mult))
                link(ts(N64(12), N64(12), 1.0 / k, 1.0, ALU.mult, ALU.add))
            link(ts(N64(11), N64(9), 1.0, None, ALU.is_gt))
            link(tts(N64(10), N64(10), N64(12), ALU.subtract))
            link(tts(N64(10), N64(10), N64(11), ALU.mult))
            link(tts(N64(10), N64(10), N64(12), ALU.add))
            link(tts(N64(8), N64(8), N64(10), ALU.mult))
            link(tts(N64(9), N64(8), N64(8), ALU.mult))
            link(ts(N64(12), N64(9), 1.0, None, ALU.add))
            root()
            link(ts(N64(13), N64(13), 1.0, None, ALU.add))
            link(dve.reciprocal(N64(13), N64(13)))
            link(tts(N64(9), N64(9), N64(13), ALU.mult))
            link(ts(N64(9), N64(9), EPS1, None, ALU.max))
            link(ts(N64(12), N64(9), 2.0, None, ALU.add))
            link(tts(N64(12), N64(12), N64(9), ALU.mult))
            root()
            link(tts(N64(9), N64(9), N64(13), ALU.add))
            link(ts(N64(12), N64(9), 1.0, None, ALU.add))
            hand_act()
            log1p(link, N64(9), N64(13), N64(17), N64(15), N64(16))
            link(ts(N64(8), N64(8), MIN_NORM, None, ALU.max))
            link(dve.reciprocal(N64(8), N64(8)))
            link(tts(N64(17), N64(17), N64(8), ALU.mult))
            link(tts(N64(17), N64(17), N64(10), ALU.mult))
            link(tts(beta[:, :], N64(17), N64(14), ALU.mult))
            dve.wait_ge(s_Vc, NSB)
            link(tts(tt[:, :], beta[:, :], V[:, :, 0], ALU.mult))
            link(ts(N64(18), tt[:, :], -1.0, None, ALU.mult))
            link(dve.tensor_reduce(tm[:, 0:1], tt[:, :], AXX, ALU.max))
            dve.tensor_reduce(tm[:, 1:2], N64(18), AXX, ALU.max).then_inc(s_mx, 1)
            dve.wait_ge(s_mx, 1)
            dve.sem_inc(s_beta, 1)
            dve.wait_ge(s_mxT, 1)
            link(dve.tensor_reduce(m2[:, 0:1], pST[0:2, 0:P], AXX, ALU.max))
            ts(m2[:, 2:4], identf[0:2, 0:2], m2[:, 0:1], None, ALU.mult).then_inc(s_m2, 1)
            dve.wait_ge(s_mb, 1)
            link(dve.tensor_copy(tm[:, 4:6], pST[:, 256:258]))
            link(tts(tm[:, 2:3], tm[:, 4:5], tm[:, 5:6], ALU.add))
            link(tts(tm[:, 3:4], tm[:, 5:6], tm[:, 4:5], ALU.subtract))
            link(ts(tm[:, 3:4], tm[:, 3:4], 0.5, None, ALU.mult))
            ts(flag[:, :], tm[:, 2:3], SPREAD, None, ALU.is_le).then_inc(s_flag, 1)
            dve.wait_ge(s_cs, 1)
            link(dve.tensor_copy(csum[:, :], pL[:, 0:1]))
            dve.tensor_copy(csb[:, :], csum[:, 0:1].to_broadcast([P, P])).then_inc(s_csb, 1)
            dve.wait_ge(s_hs, 1)
            dve.tensor_copy(Hs[:, :], pW[:, 0:P]).then_inc(s_hsc, 1)
            dve.wait_ge(s_flag, 1)

            C = lambda k, n=1: c4[:, k, :]
            bc = lambda k: c4[:, k, :].unsqueeze(2).to_broadcast([P, TA, D])

            class Behind:
                def __init__(self, e):
                    self.e, self.n = e, 0

                def link(self, ins):
                    self.n += 1
                    ins.then_inc(che, 1)
                    dve.wait_ge(che, EPI_LINKS * self.e + self.n)

                def roots(self, k):
                    dve.sem_inc(s_rq, 1)

                def normalise(self):
                    e, link = self.e, self.link
                    dve.wait_ge(s_agg, e + 1)
                    link(dve.tensor_copy(C(0), pL[:, 0:TA]))
                    link(ts(C(1), C(0), 0.0, None, ALU.is_equal))
                    link(dve.scalar_tensor_tensor(out=C(2), in0=C(1), scalar=float(N), in1=C(0), op0=ALU.mult,
                                                  op1=ALU.add))
                    link(dve.reciprocal(C(2), C(2)))
                    for a in range(TA):
                        last = dve.scalar_tensor_tensor(out=hp[:, a, :], in0=Hs[:, :], scalar=c4[:, 1, a:a + 1],
                                                        in1=pW[:, a * P:(a + 1) * P], op0=ALU.mult, op1=ALU.add)
                    link(last)
                    link(tts(hp[:, :, :], hp[:, :, :], bc(2), ALU.mult))
                    ts(ex[:, :, :], hp[:, :, :], 0.0, None, ALU.min).then_inc(s_hp, 1)

                def elu(self):
                    e, link = self.e, self.link
                    link(ts(yy[:, :, :], hp[:, :, :], 0.0, -1.0, ALU.max, ALU.add))
                    dve.wait_ge(s_ex, e + 1)
                    tts(yy[:, :, :], ex[:, :, :], yy[:, :, :], ALU.add).then_inc(s_y, 1)

                def norm_y(self):
                    e, link = self.e, self.link
                    dve.wait_ge(s_sq, 3 * e + 1)
                    link(dve.tensor_reduce(C(0), sq[:, :, 1:D], AXX, ALU.add))
                    link(ts(C(1), C(0), 1.0, None, ALU.add))
                    self.roots(0)

                def theta(self):
                    e, link = self.e, self.link
                    dve.wait_ge(s_rt, EPI_NR * e + 1)
                    link(ts(C(2), C(2), MIN_NORM, None, ALU.max))
                    link(dve.reciprocal(C(2), C(2)))
                    link(ts(C(3), C(3), 1.0, None, ALU.add))
                    link(dve.reciprocal(C(3), C(3)))
                    link(tts(C(3), C(3), C(0), ALU.mult))
                    link(ts(C(3), C(3), EPS1, None, ALU.max))
                    link(ts(C(4), C(3), 2.0, None, ALU.add))
                    link(tts(C(4), C(4), C(3), ALU.mult))
                    self.roots(1)

                def log_arg(self):
                    e, link = self.e, self.link
                    dve.wait_ge(s_rt, EPI_NR * e + 2)
                    link(tts(C(6), C(3), C(5), ALU.add))
                    ts(C(7), C(6), 1.0, None, ALU.add).then_inc(s_u, 1)

                def sigmoid_arg(self):
                    e, link = self.e, self.link
                    dve.wait_ge(s_ln, e + 1)
                    log1p(link, C(6), C(8), C(9), C(10), C(11))
                    link(tts(C(9), C(9), C(2), ALU.mult))
                    tts(hp[:, :, :], yy[:, :, :], bc(9), ALU.mult).then_inc(s_rr, 1)

                def sigmoid(self):
                    e, link = self.e, self.link
                    dve.wait_ge(s_en, e + 1)
                    link(ts(ex[:, :, :], ex[:, :, :], 1.0, None, ALU.add))
                    dve.reciprocal(yy[:, :, :], ex[:, :, :]).then_inc(s_sg, 1)

                def norm_s(self):
                    e, link = self.e, self.link
                    dve.wait_ge(s_sq, 3 * e + 2)
                    link(dve.tensor_reduce(C(14), sq[:, :, 1:D], AXX, ALU.add))
                    self.roots(2)
                    dve.wait_ge(s_rt, EPI_NR * e + 3)
                    ts(C(15), C(15), MIN_NORM, None, ALU.max).then_inc(s_nn, 1)
                    dve.wait_ge(s_nn, e + 1)

                def residual(self):
                    e, link = self.e, self.link
                    dve.wait_ge(s_sh, 2 * e + 2)
                    link(tts(C(18), C(16), C(17), ALU.subtract))
                    link(dve.reciprocal(C(19), C(15)))
                    link(tts(C(18), C(18), C(19), ALU.mult))
                    link(ts(C(18), C(18), 0.5, None, ALU.mult))
                    link(tts(C(20), C(18), C(18), ALU.mult))
                    link(tts(C(20), C(20), C(14), ALU.mult))
                    link(ts(C(20), C(20), 1.0, None, ALU.add))
                    self.roots(3)
                    link(tts(hp[:, :, :], yy[:, :, :], bc(18), ALU.mult))
                    dve.wait_ge(s_rt, EPI_NR * e + 4)
                    link(dve.tensor_copy(hp[:, :, 0], C(21)))
                    dve.wait_ge(s_xin, 16 * e + 16)
                    wait(dve, s_x1o, 16 * e)
                    tts(x1[:, :, :], hp[:, :, :], xin[:, :, :], ALU.add).then_inc(s_x1, 1)
                    dve.wait_ge(s_x1, e + 1)

                def centre(self):
                    e, link = self.e, self.link
                    link(dve.tensor_reduce(C(22), x1[:, :, :], AXX, ALU.add))
                    link(ts(C(22), C(22), 1.0 / D, None, ALU.mult))
                    tts(x1n[:, :, :], x1[:, :, :], bc(22), ALU.subtract).then_inc(s_xc1, 1)

                def layernorm(self):
                    e, link = self.e, self.link
                    dve.wait_ge(s_sq, 3 * e + 3)
                    link(dve.tensor_reduce(C(23), sq[:, :, :], AXX, ALU.add))
                    link(ts(C(23), C(23), 1.0 / D, 1e-5, ALU.mult, ALU.add))
                    self.roots(4)
                    dve.wait_ge(s_rt, EPI_NR * e + 5)
                    tts(x1n[:, :, :], x1n[:, :, :], bc(24), ALU.mult).then_inc(s_x1n, 1)

                def shift_logits(self, a):
                    e, link = self.e, self.link
                    dve.wait_ge(s_lg, TA * e + a + 1)
                    wait(dve, s_es, TA * e + a)
                    link(tts(lg[:, :], pL[:, :], bl[:, :], ALU.add))
                    link(dve.tensor_reduce(r8[:, 0, :], hg(lg[:, :]), AXX, ALU.max))
                    tts(hg(lg[:, :]), hg(lg[:, :]), r8[:, 0, :].unsqueeze(2).to_broadcast([P, H, G]),
                        ALU.subtract).then_inc(s_lm, 1)

                def slice_weights(self, a):
                    e, link = self.e, self.link
                    dve.wait_ge(s_es, TA * e + a + 1)
                    link(dve.tensor_reduce(r8[:, 1, :], hg(es[:, :]), AXX, ALU.add))
                    link(dve.reciprocal(r8[:, 1, :], r8[:, 1, :]))
                    if a == 0:
                        wait(dve, s_swo, 16 * e)
                        wait(dve, s_sws, TA * e)
                    tts(hg(sw[:, a, :]), hg(es[:, :]), r8[:, 1, :].unsqueeze(2).to_broadcast([P, H, G]),
                        ALU.mult).then_inc(s_sw, 1)

                def add_slices(self):
                    e, link = self.e, self.link
                    dve.wait_ge(s_st, e + 1)
                    tts(STacc[:, :], STacc[:, :], pST[:, :], ALU.add).then_inc(s_std, 1)
                    dve.wait_ge(s_std, e + 1)
                    assert self.n == EPI_LINKS, self.n

                def at(self, n):
                    if n == 2:
                        self.normalise()
                    if n == 4:
                        self.elu()
                    if n == 6:
                        self.norm_y()
                    if n == 7:
                        self.theta()
                    if n == 8:
                        self.log_arg()
                    if n == 10:
                        self.sigmoid_arg()
                    if n == 12:
                        self.sigmoid()
                    if n == 14:
                        self.norm_s()
                    if n == 16:
                        self.residual()
                    if n == 17:
                        self.centre()
                    if n == 19:
                        self.layernorm()
                    if n >= 23 and n % 2 == 1 and n < 31:
                        self.shift_logits((n - 23) // 2)
                    if n >= 25 and n % 2 == 1 and n < 33:
                        self.slice_weights((n - 25) // 2)
                    if n == NG - 1:
                        self.add_slices()

            def make_mask(s, q):
                dve.wait_ge(s_adj[q % NBUF], 16 * ((NQ // NBUF) * s + q // NBUF + 1))
                if not (isinstance(s, int) and s == 0 and q < 2):
                    dve.wait_ge(s_tp, NG * s + (q - 1) * GPQ)
                ts(mask[:, q % 2, :, :].rearrange("p a j -> p (a j)"), adjb[:, q % NBUF, :], 0, None,
                   ALU.is_gt).then_inc(s_mask, 1)

            one_shift = dve.value_load(flag[0:1, 0:1])
            with dve.If(one_shift > 0):
                dve.wait_ge(s_cs, 1)
                dve.wait_ge(s_wexp, 1)
                link(tts(N64(22), N64(23), beta[:, :], ALU.mult))
                for c in range(4):
                    k = slice(c * 16, c * 16 + 16)
                    tts(V[:, k, :], V[:, k, :], n64[:, 22, k].unsqueeze(2).to_broadcast([P, 16, D]), ALU.mult)\
                        .then_inc(s_gw, 1)
                    dve.wait_ge(s_gw, c + 1)
                    dve.tensor_copy(V[:, k, 0], n64[:, 23, k]).then_inc(s_gv, 1)
                for c in range(4):
                    k = slice(c * 16, c * 16 + 16)
                    dve.wait_ge(s_gv, 4)
                    dve.wait_ge(s_gh, c + 1)
                    tts(glo[:, k, :], V[:, k, :], ghi[:, k, :].bitcast(F32), ALU.subtract).then_inc(s_gl, 1)
                dve.wait_ge(s_gl, 4)
                make_mask(0, 0)
                for q in range(NQ):
                    if q + 1 < NQ:
                        make_mask(0, q + 1)
                    else:
                        make_mask(1, 0)

                def stream(s, final):
                    t = Behind(s - 1)
                    for n in range(NG):
                        if n % GPQ == 0:
                            q = n // GPQ + 1
                            if q < NQ:
                                make_mask(s, q)
                            elif not final:
                                make_mask(s + 1, 0)
                        t.at(n)
                with dve.Fori(1, NSB - 1) as s:
                    stream(s, False)
                stream(NSB - 1, True)
                t = Behind(NSB - 1)
                for n in range(NG):
                    t.at(n)
            with dve.Else():
                dve.wait_ge(s_cs, 1)
                dve.sem_inc(s_tst, 1)
                tts(V[:, :, :], V[:, :, :], beta[:, :].unsqueeze(2).to_broadcast([P, NT, D]), ALU.mult)\
                    .then_inc(s_gw, 1)
                dve.wait_ge(s_gw, 1)
                dve.memset(V[:, :, 0], 1.0).then_inc(s_gh2, 1)
                with dve.Fori(0, NSB) as s:
                    for a in range(TA):
                        for sweep in range(2):
                            for c in range(NQ):
                                k = ((s * TA + a) * 2 + sweep) * NQ + c
                                n = 3 * k
                                dve.wait_ge(s_ga, 16 * k + 16)
                                dve.wait_ge(s_gt, 16 * k + 16)
                                if c == 0 and sweep == 0:
                                    dve.wait_ge(s_gT, (s * TA + a) * NQ)
                                if sweep == 1 and c > 0:
                                    dve.wait_ge(s_gT, (s * TA + a) * NQ + c)
                                ts(mb[:, :], adjb[:, 0, 0:STEP], 0, None, ALU.is_gt).then_inc(chg, 1)
                                dve.wait_ge(chg, n + 1)
                                tts(eb[:, :], mb[:, :], tb[:, :], ALU.mult).then_inc(chg, 1)
                                dve.wait_ge(chg, n + 2)
                                ts(mb[:, :], mb[:, :], -MASKED, MASKED, ALU.mult, ALU.add).then_inc(chg, 1)
                                dve.wait_ge(chg, n + 3)
                                tts(eb[:, :], eb[:, :], mb[:, :], ALU.add).then_inc(s_gm, 1)
                                dve.wait_ge(s_gm, k + 1)
                                if sweep == 0:
                                    dve.tensor_reduce(rm[:, c:c + 1], eb[:, :], AXX, ALU.max).then_inc(chm, 1)
                                    if c == NQ - 1:
                                        m = (s * TA + a) * (NQ + 2) + NQ
                                        dve.wait_ge(chm, m)
                                        dve.tensor_reduce(rm[:, NQ:NQ + 1], rm[:, 0:NQ], AXX, ALU.max)\
                                            .then_inc(chm, 1)
                                        dve.wait_ge(chm, m + 1)
                                        ts(rm[:, NQ + 1:NQ + 2], rm[:, NQ:NQ + 1], -1.0, None, ALU.mult)\
                                            .then_inc(chm, 1)
                                        dve.wait_ge(chm, m + 2)
                                else:
                                    dve.sem_inc(s_ge, 1)
                    t = Behind(s)
                    for n in range(NG):
                        t.at(n)

            link = linker(chf)
            cnt_fd = [0]

            def mark(k, ins):
                cnt_fd[0] += 1
                assert cnt_fd[0] == k
                ins.then_inc(s_fd, 1)
                dve.wait_ge(s_fd, k)
            for k, (_, dst) in enumerate(TURNED):
                dve.wait_ge(s_ft, k + 1)
                bank = (tpf[0], tpf[1], tpf[2])[k % 3]
                for j, (d, src) in enumerate(dst):
                    last = dve.tensor_copy(d, src(bank))
                last.then_inc(s_ftc, 1)
            dve.wait_ge(s_fp, 1)
            link(dve.tensor_copy(SN, pW[:, :]))
            link(ts(rS, SN, 1e-5, None, ALU.add))
            link(dve.reciprocal(rS, rS))
            dve.wait_ge(s_fp, 2)
            for half in range(2):
                r = slice(half * 64, half * 64 + 64)
                snh = SN[r, :].rearrange("p (c t g) -> p c t g", t=2, g=G)[:, :, half, :]
                rsh = rS[r, :].rearrange("p (c t g) -> p c t g", t=2, g=G)[:, :, half, :]
                link(tts(uT[r, :, :], snh, bfx[r, :].unsqueeze(2).to_broadcast([64, KC, G]), ALU.mult))
                link(tts(uT[r, :, :], uT[r, :, :], pL[r, 0:KC * G].rearrange("p (c g) -> p c g", g=G), ALU.add))
                if half == 0:
                    link(tts(uT[r, :, :], uT[r, :, :], rsh, ALU.mult))
                else:
                    mark(F_UT, tts(uT[r, :, :], uT[r, :, :], rsh, ALU.mult))
            link(dve.memset(xb, 0.0))
            link(dve.memset(Csh[0:NS, :], 0.0))
            dve.wait_ge(s_fp, 3)
            v3 = lambda ap, g=G: ap.rearrange("p (c g) -> p c g", g=g)
            mark(F_ZEXP, dve.tensor_copy(zT, v3(pS[:, 0:KC * G])))
            dve.tensor_copy(xb[:, 0:KC, 2:], v3(pST[:, 0:KC * G])).then_inc(chf, 1)
            cnt[chf.name] += 1
            link(dve.tensor_copy(xb[0:NS, KC:6, 2:], v3(acc[0:NS, 0:2 * G])))
            for r, cs in ((slice(0, P), slice(0, KC)), (slice(0, NS), slice(KC, 6))):
                n = cs.stop - cs.start
                m = r.stop
                for k in range(3):
                    wk = cw[r, cs, k].unsqueeze(2).to_broadcast([m, n, G])
                    if k == 0:
                        link(tts(xa[r, cs, :], xb[r, cs, 0:G], wk, ALU.mult))
                    else:
                        link(tts(xg[r, cs, :], xb[r, cs, k:k + G], wk, ALU.mult))
                        link(tts(xa[r, cs, :], xa[r, cs, :], xg[r, cs, :], ALU.add))
                bk = cb[r, cs].unsqueeze(2).to_broadcast([m, n, G])
                if cs.start == 0:
                    link(tts(xa[r, cs, :], xa[r, cs, :], bk, ALU.add))
                else:
                    mark(F_SILU, tts(xa[r, cs, :], xa[r, cs, :], bk, ALU.add))
            T = lambda k: dts[0:G, k, :]
            link(tts(T(0), tpf[0][0:G, 0:2 * H], dtb[0:G, :], ALU.add))
            link(ts(T(3), T(0), -1.0, None, ALU.mult))
            mark(F_DTEXP, tts(T(1), T(0), T(3), ALU.min))
            dve.wait_ge(s_fa, 5)
            log1p(link, T(2), None, T(4), T(5), T(6), cap=1.0)
            link(ts(T(0), T(0), 0.0, None, ALU.max))
            link(tts(T(0), T(0), T(4), ALU.add))
            link(tts(T(7), T(0), Ae[0:G, :], ALU.mult))
            link(ts(T(7), T(7), -1.0, -1e30, ALU.mult, ALU.max))
            dve.wait_ge(s_fg, 4)
            link(tts(hg(aF[0:G, :]), dts[0:G, 7, 0:H].unsqueeze(2).to_broadcast([G, H, G]),
                     M1[0:G, :].unsqueeze(1).to_broadcast([G, H, G]), ALU.mult))
            mark(F_AD, tts(hg(aB[0:G, :]), dts[0:G, 7, H:2 * H].unsqueeze(2).to_broadcast([G, H, G]),
                           M2[0:G, :].unsqueeze(1).to_broadcast([G, H, G]), ALU.mult))
            for r, cs in ((slice(0, P), slice(0, KC)), (slice(0, NS), slice(KC, 6))):
                link(ts(xg[r, cs, :], xg[r, cs, :], 1.0, None, ALU.add))
                link(dve.reciprocal(xg[r, cs, :], xg[r, cs, :]))
                link(tts(xa[r, cs, :], xa[r, cs, :], xg[r, cs, :], ALU.mult))
            link(dve.tensor_copy(Csh[0:NS, 1:G], xa[0:NS, 5, 0:G - 1]))
            mark(F_XA, dve.tensor_copy(Csh[0:NS, G:2 * G - 1], xa[0:NS, 5, 1:G]))
            dve.wait_ge(s_fp, 4)
            link(dve.tensor_copy(EF[0:G, :], tpf[1][0:G, :]))
            mark(F_SEG, dve.tensor_copy(EB[0:G, :], tpf[2][0:G, :]))
            dve.wait_ge(s_fp, 5)
            link(dve.tensor_copy(xt[0:G, :], pL[0:G, :]))
            link(dve.tensor_copy(CB[0:G, :], tpf[0][0:G, 64:64 + 2 * G]))
            link(tts(CB[0:G, 0:G], CB[0:G, 0:G], M1[0:G, :], ALU.mult))
            link(tts(CB[0:G, G:2 * G], CB[0:G, G:2 * G], M2[0:G, :], ALU.mult))
            dve.wait_ge(s_fa, 7)
            for k, Et in enumerate((EF, EB)):
                link(tts(hg(Et[0:G, :]), hg(Et[0:G, :]),
                         CB[0:G, k * G:(k + 1) * G].unsqueeze(1).to_broadcast([G, H, G]), ALU.mult))
                link(tts(hg(Et[0:G, :]), hg(Et[0:G, :]),
                         dts[0:G, 0, k * H:(k + 1) * H].unsqueeze(2).to_broadcast([G, H, G]), ALU.mult))
            mark(F_M, tts(EF[0:G, :], EF[0:G, :], EB[0:G, :], ALU.add))
            link(tts(yT, v3(pW[:, 0:KC * G]), Dc.unsqueeze(2).to_broadcast([P, KC, G]), ALU.add))
            link(tts(yT, yT, xa[:, 0:KC, :], ALU.mult))
            link(ts(sgz, sgz, 1.0, None, ALU.add))
            link(dve.reciprocal(sgz, sgz))
            link(tts(sgz, sgz, zT, ALU.mult))
            dve.wait_ge(s_fp, 6)
            link(tts(yT, yT, v3(acc[:, 0:KC * G]), ALU.add))
            link(tts(yT, yT, sgz, ALU.mult))
            mark(F_YQ, tts(yq, yT, yT, ALU.mult))
            dve.wait_ge(s_fp, 7)
            mark(F_RMS, ts(rms, tpf[1][:, 0:G], 1.0 / DI, 1e-5, ALU.mult, ALU.add))
            link(tts(yT, yT, nw.unsqueeze(2).to_broadcast([P, KC, G]), ALU.mult))
            dve.wait_ge(s_fg, 5)
            mark(F_YN, tts(yT, yT, rms.unsqueeze(1).to_broadcast([P, KC, G]), ALU.mult))
            dve.wait_ge(s_fp, 8)
            mark(F_OT, dve.tensor_copy(otT, v3(tpf[2][:, 0:KC * G])))
            dve.wait_ge(s_fp, 9)
            mark(F_MO, dve.tensor_copy(Mo[:, :, :], v3(pW[:, :], D)))

            dve.wait_ge(s_ob, 16)
            dve.sem_inc(s_fy2, 2)
            with dve.Fori(0, NSB // 2) as g:
                for b in range(2):
                    s = 2 * g + b
                    for a in range(1, TA, 2):
                        dve.wait_ge(s_fT, s * TA + a + 1)
                        dve.tensor_copy(swT[:, 1, :], tpf[1]).then_inc(s_fTd, 1)
                    dve.wait_ge(s_fl[b], 32 * g + 32)
                    tts(x1l[:, b, :, :], x1l[:, b, :, :], obB[:, :].unsqueeze(1).to_broadcast([P, TA, D]), ALU.add)\
                        .then_inc(s_x1b, 1)
                    dve.wait_ge(s_x1b, s + 1)
                    dve.wait_ge(s_fm, s + 1)
                    dve.wait_ge(s_out[b], 16 * g)
                    tts(yo[:, b, :, :], v3((pW, pL)[b][:, :], D), x1l[:, b, :, :], ALU.add).then_inc(s_fy, 1)
                    dve.wait_ge(s_fy, s + 1)
                    dve.sem_inc(s_fy2, 1)


_INS = ['x', 'adj', 'L0_gnn_W_gcn', 'L0_gnn_W_att', 'L0_gnn_a_att', 'L0_ffn_W_fx', 'L0_ffn_b_fx', 'L0_ffn_W_x',
        'L0_ffn_b_x', 'L0_ffn_W_slice', 'L0_ffn_b_slice', 'L0_ffn_temperature', 'L0_ffn_hy_in_w',
        'L0_ffn_hy_conv_w', 'L0_ffn_hy_conv_b', 'L0_ffn_hy_dt_bias', 'L0_ffn_hy_A_log', 'L0_ffn_hy_D',
        'L0_ffn_hy_fcD_w', 'L0_ffn_hy_norm_w', 'L0_ffn_hy_out_w', 'L0_ffn_out_w', 'L0_ffn_out_b']


def kernel(**inputs):
    import numpy as _np
    import concourse.bacc as _bacc
    from concourse import mybir as _mybir
    from concourse.bass_utils import run_bass_kernel_spmd as _run

    nc = _bacc.Bacc("TRN2", target_bir_lowering=False, num_devices=1)
    arrays, args = {}, []
    for name in _INS:
        a = _np.ascontiguousarray(inputs[name])
        arrays[f"in_{name}_dram"] = a
        args.append(nc.dram_tensor(f"in_{name}_dram", a.shape, _mybir.dt.from_np(a.dtype), kind="ExternalInput").ap())
    out = nc.dram_tensor("out_0_dram", inputs["x"].shape, _mybir.dt.float32, kind="ExternalOutput").ap()
    gnn_ffn(nc, *args, out)
    r = _run(nc, [arrays], core_ids=[0])
    return r.results[0]["out_0_dram"]
```

```python
from contextlib import ExitStack

import numpy as np

import concourse.bass as bass
from concourse import mybir

F32 = mybir.dt.float32
F32R = mybir.dt.float32r
BF16 = mybir.dt.bfloat16
I32 = mybir.dt.int32
ALU = mybir.AluOpType
ACT = mybir.ActivationFunctionType
AXX = mybir.AxisListType.X

P = 128
D = 128
TA = 4
ROWS = TA * P
STEP = 1024
GROUP = 2
MCOLS = 512
NMB = 4
MLEAD = 5
MHEAD = 3
NBUF = 4
NTP = 4
NAT = 4
LEAD = 3
MASKED = -9.0e15
EPS1 = float(np.float32(1.0 + 1e-7) - np.float32(1.0))
MIN_NORM = 1e-15
LN2 = float(np.log(2.0))
SPREAD = 80.0

PRO_ROOTS = [(6, 5, -0.5), (7, 4, 0.5), (8, 3, 0.5), (10, 9, 0.5), (13, 12, 0.5), (13, 12, 0.5)]
PRO_ACTS = [(13, 12, ACT.Ln, 1.0), (10, 9, ACT.Exp, 1.0), (11, 9, ACT.Exp, -1.0), (13, 12, ACT.Ln, 1.0)]
EPI_ROOTS = [(2, 0, 2, 0.5), (5, 4, 1, 0.5), (15, 14, 1, 0.5), (21, 20, 1, 0.5), (24, 23, 1, -0.5)]
LOGITS = (13, 16, 19, 22)
MAXIMA = (16, 19, 22, 25)
SUBTRACT = (15, 18, 21, 24)
EXPS = (19, 22, 25, 28)
SUMS = (20, 23, 26, 29)
WEIGHTS = (19, 22, 25, 28)
SLICES = (23, 26, 29, 31)
CHAIN_A = 36
CHAIN_B = 12
(F_UT, F_ZEXP, F_SILU, F_DTEXP, F_AD, F_XA, F_SEG, F_M, F_YQ, F_RMS, F_YN, F_OT, F_MO) = range(1, 14)
NFW = 18


def fetch_shapes(adj, in_w, fc):
    return adj.shape[0], in_w.shape[0], fc.shape[0]


def gnn_ffn(nc, x, adj, W_gcn, W_att, a_att, W_fx, b_fx, W_x, b_x, W_slice, b_slice, temperature,
            in_w, conv_w, conv_b, dt_bias, A_log, hy_D, fcD_w, norm_w, hy_out_w, out_w, out_b, out):
    N, DIP, H = fetch_shapes(adj, in_w, fcD_w)
    NT = N // P
    NSB = N // ROWS
    NQ = N // STEP
    NG = NT // GROUP
    GPQ = STEP // (GROUP * P)
    MPQ = STEP // MCOLS
    GPM = GPQ // MPQ
    NM = NQ * MPQ
    G = W_slice.shape[0]
    HD = W_slice.shape[1]
    DI = H * HD
    KC = DI // P
    NS = (conv_w.shape[0] - DI) // 2
    assert G == 64 and HD == 64 and NS == 64 and D == P and KC == 4 and NQ % NBUF == 0

    x1_d = nc.dram_tensor("x1_scratch", [N, D], F32).ap()
    sw_d = nc.dram_tensor("slice_weights_scratch", [N, H * G], F32).ap()
    t_d = nc.dram_tensor("t_scratch", [N], F32).ap()

    ctx = ExitStack()
    with ctx:
        def sem(name):
            return ctx.enter_context(nc.semaphore(name))

        def sb(name, shape, dt=F32, c=None):
            return (c or ctx).enter_context(nc.sbuf_tensor(name, shape, dt))

        tp = [ctx.enter_context(nc.psum_tensor(f"tp{i}", [P, 1024], BF16)) for i in range(NTP)]
        tpf = [t[:, :].bitcast(F32) for t in tp]
        acc = ctx.enter_context(nc.psum_tensor("acc", [P, 512], F32))
        pW = ctx.enter_context(nc.psum_tensor("pW", [P, 512], F32))
        pS = tpf[3]
        pL = ctx.enter_context(nc.psum_tensor("pL", [P, 512], F32))
        pST = ctx.enter_context(nc.psum_tensor("pST", [P, 512], F32))

        identb = sb("identb", [P, P], BF16)
        identf = sb("identf", [P, P])
        ones = sb("ones", [P, P])
        Wg = sb("Wg", [P, P])
        WA = sb("WA", [P, P])
        e0 = sb("e0", [P, 1])
        Hs = sb("Hs", [P, P])
        WcT = sb("WcT", [P, H * G])
        bl = sb("bl", [P, H * G])
        STacc = sb("STacc", [P, H * G])
        zeros = STacc
        swsum = sb("swsum", [P, H * G])
        beta = sb("beta", [P, NT])
        tt = sb("tt", [P, NT])
        tm = sb("tm", [P, 8])
        flag = sb("flag", [P, 1], I32)
        csum = sb("csum", [P, 1])
        csb = sb("csb", [P, P])
        accS = sb("accS", [P, ROWS])
        xin = sb("xin", [P, TA, D])
        hp = sb("hp", [P, TA, D])
        ex = sb("ex", [P, TA, D])
        yy = sb("yy", [P, TA, D])
        sq = sb("sq", [P, TA, D])
        x1 = sb("x1", [P, TA, D])
        x1n = sb("x1n", [P, TA, D])
        x1nT = sb("x1nT", [P, ROWS])
        lg = sb("lg", [P, 2, H * G])
        es = sb("es", [P, 2, H * G])
        sw = sb("sw", [P, TA, H * G])
        r8 = sb("r8", [P, 2, 2, H])
        c4 = sb("c4", [P, 32, TA])
        bst = sb("bst", [P, TA, 6])
        mv = sb("mv", [P, TA, 2])
        bits = sb("bits", [P, 2, TA], I32)
        expo = sb("expo", [P, 2, NT])

        n64 = sw[:, :, :].rearrange("p a b -> p (a b)")[:, 0:24 * NT].rearrange("p (k n) -> p k n", n=NT)
        obB = sb("obB", [P, D])
        adjb = sb("adjb", [P, NBUF, TA * STEP], I32)
        early = ExitStack()
        V = sb("V", [P, NT, D], F32, early)
        early.close()
        late = ctx
        mask = sb("mask", [P, NMB, TA, MCOLS], BF16, late)
        adjT = sb("adjT", [P, NAT, GROUP * ROWS], F32R, late)
        gs = ExitStack()
        ghi = sb("ghi", [P, NT, D], F32R, gs)
        glo = sb("glo", [P, NT, D], F32R, gs)
        gs.close()
        pro = ExitStack()
        xs = sb("xs", [P, 2, TA, D], F32, pro)
        xc = sb("xc", [P, 2, TA, D], F32, pro)
        xq = sb("xq", [P, 2, TA, D], F32, pro)
        xcT = sb("xcT", [P, 2, ROWS], F32, pro)
        vq = sb("vq", [P, 2, TA, D], F32, pro)
        Wx_n = sb("Wx_n", [HD, H, D], F32, pro)
        Wsl = sb("Wsl", [G, HD], F32, pro)
        WslT = sb("WslT", [HD, G], F32, pro)
        bxT = sb("bxT", [HD, H], F32, pro)
        bxB = sb("bxB", [HD, H, P], F32, pro)
        bsB = sb("bsB", [P, G], F32, pro)
        tmpB = sb("tmpB", [P, H], F32, pro)
        WAT = sb("WAT", [P, P], F32, pro)
        WgT = sb("WgT", [P, P], F32, pro)
        WAf = sb("WAf", [P, P], F32, pro)
        a2 = sb("a2", [P, 1], F32, pro)
        v2 = sb("v2", [P, 1], F32, pro)
        m2 = sb("m2", [2, 4], F32, pro)
        pro.close()
        gen = ExitStack()
        tb = sb("tb", [P, STEP], F32, gen)
        eb = sb("eb", [P, STEP], F32, gen)
        mb = sb("mb", [P, STEP], F32, gen)
        pT = sb("pT", [P, STEP], F32, gen)
        rm = sb("rm", [P, NQ + 2], F32, gen)
        gen.close()
        inw = sb("inw", [P, 10, DI])
        inT = sb("inT", [P, KC, DIP])
        AB = adjb[:, :, :].rearrange("p a b -> p (a b)").bitcast(F32)
        cut = [0]

        def ab(w):
            a = cut[0]
            cut[0] += w
            assert cut[0] <= NBUF * TA * STEP
            return AB[:, a:a + w]

        ow = ab(KC * DI).rearrange("p (a b) -> p a b", a=KC)
        oT = ab(KC * DI).rearrange("p (a b) -> p a b", a=KC)
        wf = ab(KC * D).rearrange("p (a b) -> p a b", a=KC)
        wfT = ab(DI)
        wo = ab(DI)
        woT = ab(KC * D).rearrange("p (a b) -> p a b", a=KC)
        fc = ab(DI)
        fcT = ab(KC * DI).rearrange("p (a b) -> p a b", a=KC)
        z6 = lambda n, w=G: ab(n * w).rearrange("p (a b) -> p a b", a=n)
        uT = z6(KC)
        zT = z6(KC)
        xb = z6(6, G + 2)
        xa = z6(6)
        xg = z6(6)
        xt = ab(DI)
        cw = ab(18).rearrange("p (a b) -> p a b", a=6)
        cb = ab(6)
        bfx = ab(KC)
        Dc = ab(KC)
        nw = ab(KC)
        dtb = ab(2 * H)
        Ae = ab(2 * H)
        dts = ab(12 * 2 * H).rearrange("p (a b) -> p a b", a=12)
        M1 = ab(G)
        M2 = ab(G)
        SN = ab(H * G)
        rS = ab(H * G)
        aF = ab(H * G)
        aB = ab(H * G)
        EF = ab(H * G)
        EB = ab(H * G)
        Csh = ab(2 * G)
        CB = ab(2 * G)
        sgz = z6(KC)
        yT = z6(KC)
        yq = z6(KC)
        rms = ab(G)
        otT = z6(KC)
        Mo = sb("Mo", [P, KC, D])
        swl = sb("swl", [P, 2, TA, H * G])
        x1l = sb("x1l", [P, 2, TA, D])
        swT = es
        yo = lg[:, :, :].rearrange("p b (a d) -> p b a d", a=TA)

        s_w = sem("weights_loaded")
        s_id = sem("idents_made")
        s_one = sem("ones_made")
        s_wz = sem("weights_zeroed")
        s_tr = sem("weight_transposed")
        s_trc = sem("weight_copied")
        s_xs = [sem(f"x_loaded{b}") for b in range(2)]
        s_xfree = sem("x_used")
        s_xc = sem("x_centred")
        s_xqd = sem("x_squared")
        s_pT = sem("x_transposed")
        s_pTc = sem("x_transposed_copied")
        s_V = sem("V_product")
        s_Vc = sem("V_copied")
        s_Vq = sem("V_squared")
        s_ssv = sem("V_sums_done")
        s_pg = sem("roots_asked")
        s_pr = sem("roots_done")
        s_pa = sem("acts_asked")
        s_pd = sem("acts_done")
        s_mx = sem("extrema_ready")
        s_mxT = sem("extrema_transposed")
        s_m2 = sem("extrema_reduced")
        s_mb = sem("extrema_spread")
        s_flag = sem("flag_ready")
        s_beta = sem("beta_ready")
        s_cs = sem("column_sums")
        s_csb = sem("column_sums_spread")
        s_hs = sem("mean_product")
        s_hsc = sem("Hs_ready")
        s_wexp = sem("w_ready")
        s_gv = sem("g_ready")
        s_gh = sem("ghi_ready")
        s_gl = sem("glo_ready")
        ch = sem("dve_chain")
        che = sem("dve_first_chain")
        che2 = sem("dve_second_chain")
        chf = sem("dve_mixer_chain")
        chg = sem("dve_general_chain")
        s_adj = [sem(f"adj_loaded{b}") for b in range(NBUF)]
        s_mask = sem("mask_made")
        s_tp = sem("group_transposed")
        s_ev = sem("group_evacuated")
        s_mm = sem("group_multiplied")
        s_acc = sem("acc_done")
        s_accS = sem("acc_copied")
        s_xin = sem("xin_loaded")
        s_agg = sem("agg_done")
        s_hp = sem("hp_ready")
        s_ex = sem("exp_hp")
        s_den = sem("denominators_copied")
        s_rd = sem("row_scales_ready")
        s_hps = sem("means_scaled")
        s_re = sem("relu_ready")
        s_y = sem("elu_ready")
        s_sy = sem("elu_squares_summed")
        s_x0 = sem("one_added")
        s_lf = sem("log_factor_ready")
        s_th = sem("tanh_ready")
        s_ss = sem("sigmoid_squares_summed")
        s_kr = sem("sinh_factor_ready")
        s_sv = sem("sinh_applied")
        s_lb = sem("logits_bank_read")
        s_lx = sem("logits_maximum")
        s_rs = sem("logits_sum_inverted")
        s_rq1 = sem("first_root_asked")
        s_rq2 = sem("second_roots_asked")
        s_rt = sem("first_roots")
        s_rt2 = sem("second_roots")
        s_nn = sem("norm_ready")
        s_sh = sem("sinh_exps")
        s_x1 = sem("x1_ready")
        s_x1n = sem("x1n_ready")
        s_x1T = sem("x1n_transposed")
        s_x1Tc = sem("x1nT_copied")
        s_lg = sem("logits_product")
        s_lm = sem("logits_shifted")
        s_es = sem("logits_exp")
        s_sw = sem("sw_ready")
        s_sws = sem("swsum_added")
        s_st = sem("st_product")
        s_zero = sem("zeroes_made")
        s_std = sem("st_copied")
        s_x1o = sem("x1_stored")
        s_swo = sem("sw_stored")
        sp_tick = sem("sp_tick")
        pool_tick = sem("pool_tick")
        dve_tick = sem("dve_tick")
        s_out = [sem(f"out_stored{b}") for b in range(2)]
        s_tst = sem("t_stored")
        s_tout = sem("t_written")
        s_gt = sem("general_t_loaded")
        s_ga = sem("general_adj_loaded")
        s_gh2 = sem("h_in_ready")
        s_gm = sem("general_chunk_used")
        s_ge = sem("general_logits")
        s_gp = sem("general_probabilities")
        s_gT = sem("general_transposed")
        s_gTc = sem("general_transposed_copied")
        s_gmm = sem("general_product")
        s_fw = sem("mixer_weights_loaded")
        s_ft = sem("mixer_transposed")
        s_ftc = sem("mixer_transposed_copied")
        s_fp = sem("mixer_product")
        s_fd = sem("mixer_dve")
        s_fa = sem("mixer_act")
        s_fg = sem("mixer_pool")
        s_fl = [sem(f"final_loaded{b}") for b in range(2)]
        s_flf = sem("final_load_used")
        s_fT = sem("sw_transposed")
        s_fTc = sem("sw_transposed_copied")
        s_fm = sem("final_product")
        s_fy = sem("final_sum")
        s_ob = sem("out_b_loaded")
        s_fTd = sem("sw_transposed_copied_by_dve")
        s_fy2 = sem("final_bank_free")
        s_x1b = sem("x1_with_out_b")
        s_gw = sem("V_scaled")
        chp = sem("dve_prologue_chain")
        chm = sem("dve_row_maximum_chain")

        def turned():
            for k in range(KC):
                for a0, a1 in ((0, 4), (4, 8), (8, 10)):
                    blocks = [(inw[0:min(P, DIP - a * P), a, k * P:(k + 1) * P], min(P, DIP - a * P))
                              for a in range(a0, a1)]
                    w = sum(n for _, n in blocks)
                    yield blocks, [(inT[:, k, a0 * P:a0 * P + w], lambda bank, w=w: bank[:, 0:w])]
            for k in range(KC):
                yield [(ow[:, a, k * P:(k + 1) * P], P) for a in range(KC)], [(oT[:, k, :], lambda bank: bank)]
            yield [(wf[:, a, :], P) for a in range(KC)], [(wfT, lambda bank: bank)]
            yield [(wo[:, k * P:(k + 1) * P], P) for k in range(KC)], \
                [(woT.rearrange("p a b -> p (a b)"), lambda bank: bank)]
            yield [(fc[0:H, k * P:(k + 1) * P], H) for k in range(KC)], \
                [(fcT[:, k, :].rearrange("p (h c) -> p h c", h=H),
                  lambda bank, k=k: bank[:, k * P:k * P + H].unsqueeze(2).to_broadcast([P, H, HD]))
                 for k in range(KC)]
        TURNED = list(turned())

        block = ctx.enter_context(nc.Block())

        x_v = x.rearrange("(s a p) d -> s p a d", a=TA, p=P)
        adj_v = adj.rearrange("(s a p) (q j) -> s q p a j", a=TA, p=P, j=STEP)
        x1_v = x1_d.rearrange("(s a p) d -> s p a d", a=TA, p=P)
        sw_v = sw_d.rearrange("(s a p) g -> s p a g", a=TA, p=P)
        out_v = out.rearrange("(s a p) d -> s p a d", a=TA, p=P)

        NW = 10

        def pos(v):
            return not isinstance(v, int) or v > 0

        def wait(eng, s, v):
            if pos(v):
                eng.wait_ge(s, v)

        hg = lambda ap: ap.rearrange("p (h g) -> p h g", h=H)

        @block.sync
        def _(sp):
            def wait_sp(s, v):
                wait(sp, s, v)
                if not isinstance(v, int):
                    sp.sem_inc(sp_tick, 1)

            with nc.allow_non_contiguous_dma(reason="small weights"):
                sp.wait_ge(s_wz, 4)
                sp.dma_start(Wg[1:P, 1:P], W_gcn).then_inc(s_w, 16)
                sp.dma_start(WA[1:P, :], W_att[1:P, :]).then_inc(s_w, 16)
                sp.dma_start(WAf[:, :], W_att).then_inc(s_w, 16)
                sp.dma_start(a2[:, :], a_att[P:2 * P, :]).then_inc(s_w, 16)
                for b in range(2):
                    sp.dma_start(xs[:, b, :, :], x_v[b, :, :, :]).then_inc(s_xs[b], 16)
                sp.dma_start(Wx_n[:, :, :], W_x.rearrange("(h q) d -> q h d", q=HD)).then_inc(s_w, 16)
                sp.dma_start(Wsl[:, :], W_slice).then_inc(s_w, 16)
                sp.dma_start(bxT[:, :], b_x.rearrange("(h q) -> q h", q=HD)).then_inc(s_w, 16)
                sp.dma_start(bsB[:, :], b_slice.rearrange("(a g) -> a g", a=1).to_broadcast([P, G]))\
                    .then_inc(s_w, 16)
                sp.dma_start(tmpB[:, :], temperature.rearrange("a h b c -> a (h b c)").to_broadcast([P, H]))\
                    .then_inc(s_w, 16)
                sp.dma_start(obB[:, :], out_b.rearrange("(a d) -> a d", a=1).to_broadcast([P, D]))\
                    .then_inc(s_ob, 16)
            with sp.Fori(1, NSB // 2) as g:
                for b in range(2):
                    wait_sp(s_xfree, 2 * g + b - 1)
                    sp.dma_start(xs[:, b, :, :], x_v[2 * g + b, :, :, :]).then_inc(s_xs[b], 16)

            def load_adj(s, q):
                if not (isinstance(s, int) and s == 0 and q < NBUF):
                    wait_sp(s_mask, (NQ * s + q - NBUF + 1) * MPQ)
                sp.dma_start(adjb[:, q % NBUF, :].rearrange("p (a j) -> p a j", a=TA),
                             adj_v[s, q, :, :, :]).then_inc(s_adj[q % NBUF], 16)

            sp.wait_ge(s_flag, 1)
            one_shift = sp.value_load(flag[0:1, 0:1])
            with sp.If(one_shift > 0):
                for q in range(NQ):
                    load_adj(0, q)
                with sp.Fori(1, NSB) as s:
                    for q in range(NQ):
                        load_adj(s, q)
            with sp.Else():
                sp.wait_ge(s_tst, 1)
                with nc.allow_non_contiguous_dma(reason="one value per row"):
                    sp.dma_start(t_d.rearrange("(c p) -> p c", p=P), tt[:, :]).then_inc(s_tout, 16)
                sp.wait_ge(s_tout, 16)
                with sp.Fori(0, NSB) as s:
                    for a in range(TA):
                        for c in range(2 * NQ):
                            wait_sp(s_gm, (s * TA + a) * 2 * NQ + c)
                            sp.dma_start(adjb[:, 0, 0:STEP], adj_v[s, c % NQ, :, a, :]).then_inc(s_ga, 16)
                            sp.dma_start(tb[:, :], t_d[c % NQ * STEP:(c % NQ + 1) * STEP]
                                         .rearrange("(a j) -> a j", a=1).to_broadcast([P, STEP]))\
                                .then_inc(s_gt, 16)
            sp.wait_ge(s_st, NSB + 1)
            sp.wait_ge(s_x1o, 16 * NSB)
            sp.wait_ge(s_swo, 16 * NSB)
            with nc.allow_non_contiguous_dma(reason="small weights"):
                sp.dma_start(inw[:, 0:9, :], in_w[0:9 * P, :].rearrange("(a p) k -> p a k", p=P)).then_inc(s_fw, 16)
                sp.dma_start(inw[0:DIP - 9 * P, 9, :], in_w[9 * P:DIP, :]).then_inc(s_fw, 16)
                sp.dma_start(ow, hy_out_w.rearrange("(a p) k -> p a k", p=P)).then_inc(s_fw, 16)
                sp.dma_start(wf, W_fx.rearrange("(a p) k -> p a k", p=P)).then_inc(s_fw, 16)
                sp.dma_start(wo, out_w).then_inc(s_fw, 16)
                sp.dma_start(fc[0:H, :], fcD_w).then_inc(s_fw, 16)
                sp.dma_start(cw[:, 0:KC, :], conv_w[0:DI, :].rearrange("(a p) k -> p a k", p=P)).then_inc(s_fw, 16)
                sp.dma_start(cw[0:NS, KC:6, :], conv_w[DI:, :].rearrange("(a p) k -> p a k", p=NS)).then_inc(s_fw, 16)
                sp.dma_start(cb[:, 0:KC], conv_b[0:DI].rearrange("(a p) -> p a", p=P)).then_inc(s_fw, 16)
                sp.dma_start(cb[0:NS, KC:6], conv_b[DI:].rearrange("(a p) -> p a", p=NS)).then_inc(s_fw, 16)
                sp.dma_start(bfx, b_fx.rearrange("(a p) -> p a", p=P)).then_inc(s_fw, 16)
                sp.dma_start(nw, norm_w.rearrange("(a p) -> p a", p=P)).then_inc(s_fw, 16)
                for half in range(2):
                    sp.dma_start(Dc[half * 64:half * 64 + 64, :],
                                 hy_D.rearrange("(c t) -> t c", t=2)[half:half + 1, :].to_broadcast([64, KC]))\
                        .then_inc(s_fw, 16)
                    sp.dma_start(dtb[0:G, half * H:half * H + H],
                                 dt_bias.rearrange("(a h) -> a h", a=1).to_broadcast([G, H])).then_inc(s_fw, 16)
                    sp.dma_start(Ae[0:G, half * H:half * H + H],
                                 A_log.rearrange("(a h) -> a h", a=1).to_broadcast([G, H])).then_inc(s_fw, 16)

            def load_final(s, b):
                sp.dma_start(swl[:, b, :, :], sw_v[s, :, :, :]).then_inc(s_fl[b], 16)
                sp.dma_start(x1l[:, b, :, :], x1_v[s, :, :, :]).then_inc(s_fl[b], 16)

            def store_final(s, b):
                wait_sp(s_fy, s + 1)
                sp.dma_start(out_v[s, :, :, :], yo[:, b, :, :]).then_inc(s_out[b], 16)

            for b in range(2):
                load_final(b, b)
            with sp.Fori(0, NSB // 2 - 1) as g:
                for b in range(2):
                    store_final(2 * g + b, b)
                    load_final(2 * g + b + 2, b)
            for b in range(2):
                store_final(NSB - 2 + b, b)
            for b in range(2):
                sp.wait_ge(s_out[b], 16 * (NSB // 2))

        @block.gpsimd
        def _(pool):
            def wait_pool(s, v):
                wait(pool, s, v)
                if not isinstance(v, int):
                    pool.sem_inc(pool_tick, 1)

            pool.memset(Wg[:, :], 0.0).then_inc(s_wz, 1)
            pool.memset(WA[:, :], 0.0).then_inc(s_wz, 1)
            pool.memset(e0[:, :], 0.0).then_inc(s_wz, 1)
            pool.wait_ge(s_wz, 3)
            pool.memset(e0[0:1, :], 1.0).then_inc(s_wz, 1)
            pool.memset(ones[:, :], 1.0).then_inc(s_one, 1)
            pool.memset(swsum[:, :], 0.0).then_inc(s_one, 1)
            pool.memset(identf[:, :], 0.0).then_inc(s_id, 1)
            pool.memset(identb[:, :], 0.0).then_inc(s_id, 1)
            pool.wait_ge(s_id, 2)
            for m in (identf, identb):
                pool.affine_select(out=m[:, :], in_=m[:, :], compare_op=ALU.not_equal, fill=1.0, base=0,
                                   pattern=[[-1, P]], channel_multiplier=1).then_inc(s_id, 1)

            pool.memset(expo[:, 0, :], 0.5).then_inc(s_one, 1)
            pool.memset(expo[:, 1, :], -0.5).then_inc(s_one, 1)
            pool.wait_ge(s_one, 4)

            def root(out_ap, in_ap, power, asked, n, done):
                wait_pool(asked, n)
                w = expo[:, 0 if power > 0 else 1, 0:int(np.prod(in_ap.shape[1:]))]
                if len(in_ap.shape) == 3:
                    w = w.rearrange("p (a b) -> p a b", a=in_ap.shape[1])
                pool.tensor_tensor(out_ap, in_ap, w, ALU.pow).then_inc(done, 1)

            for k, (o, i, w) in enumerate(PRO_ROOTS):
                root(n64[:, o, :], n64[:, i, :], w, s_pg, k + 1, s_pr)

            def roots(e, k):
                o, i, n, power = EPI_ROOTS[k]
                if k == 0:
                    wait_pool(s_sy, e + 1)
                    pool.tensor_scalar(c4[:, 1, :], c4[:, 0, :], 1.0, None, ALU.add).then_inc(s_x0, 1)
                    root(c4[:, o:o + n, :], c4[:, i:i + n, :], power, s_x0, e + 1, s_rt)
                elif k == 2:
                    root(c4[:, o:o + n, :], c4[:, i:i + n, :], power, s_ss, e + 1, s_rt)
                else:
                    root(c4[:, o:o + n, :], c4[:, i:i + n, :], power, *((s_rq1, e + 1, s_rt) if k == 1 else
                                                                        (s_rq2, 2 * e + k - 2, s_rt2)))

            def subtract_maximum(e, a):
                wait_pool(s_lx, TA * e + a + 1)
                pool.tensor_tensor(hg(lg[:, a % 2, :]), hg(lg[:, a % 2, :]),
                                   r8[:, a % 2, 0, :].unsqueeze(2).to_broadcast([P, H, G]),
                                   ALU.subtract).then_inc(s_lm, 1)

            def slice_weights(e, a):
                if a == 0:
                    wait_pool(s_swo, 16 * e)
                    wait_pool(s_st, e)
                wait_pool(s_rs, TA * e + a + 1)
                pool.tensor_tensor(hg(sw[:, a, :]), hg(es[:, a % 2, :]),
                                   r8[:, a % 2, 1, :].unsqueeze(2).to_broadcast([P, H, G]),
                                   ALU.mult).then_inc(s_sw, 1)
                wait_pool(s_sw, TA * e + a + 1)
                wait_pool(s_sws, TA * e + a)
                pool.tensor_tensor(swsum[:, :], swsum[:, :], sw[:, a, :], ALU.add).then_inc(s_sws, 1)

            def first(e, n):
                if n in (13, 17, 23):
                    roots(e, (13, 17, 23).index(n))

            def second(e, n):
                if n in (0, 3):
                    roots(e, 3 + (0, 3).index(n))
                if n in SUBTRACT:
                    subtract_maximum(e, SUBTRACT.index(n))
                if n in WEIGHTS:
                    slice_weights(e, WEIGHTS.index(n))

            pool.wait_ge(s_flag, 1)
            one_shift = pool.value_load(flag[0:1, 0:1])
            with pool.If(one_shift > 0):
                for n in range(NG):
                    first(0, n)
                with pool.Fori(1, NSB) as e:
                    for n in range(NG):
                        second(e - 1, n)
                        first(e, n)
                for n in range(NG):
                    second(NSB - 1, n)
            with pool.Else():
                with pool.Fori(0, NSB) as e:
                    for n in range(NG):
                        first(e, n)
                    for n in range(NG):
                        second(e, n)
            pool.wait_ge(s_st, NSB + 1)
            pool.memset(M1[0:G, :], 1.0).then_inc(s_fg, 1)
            pool.memset(M2[0:G, :], 1.0).then_inc(s_fg, 1)
            pool.wait_ge(s_fg, 2)
            pool.affine_select(out=M1[0:G, :], in_=M1[0:G, :], compare_op=ALU.is_gt, fill=0.0, base=0,
                               pattern=[[1, G]], channel_multiplier=-1).then_inc(s_fg, 1)
            pool.affine_select(out=M2[0:G, :], in_=M2[0:G, :], compare_op=ALU.is_gt, fill=0.0, base=0,
                               pattern=[[-1, G]], channel_multiplier=1).then_inc(s_fg, 1)
            pool.wait_ge(s_fd, F_RMS)
            pool.tensor_tensor(rms, rms, expo[:, 1, 0:G], ALU.pow).then_inc(s_fg, 1)

        @block.scalar
        def _(act):
            with act.Fori(0, NSB // 2) as g:
                for b in range(2):
                    k = 2 * g + b
                    act.wait_ge(s_xc, k + 1)
                    act.activation(xq[:, b, :, :], xc[:, b, :, :], ACT.Square).then_inc(s_xqd, 1)
                    act.wait_ge(s_pT, k + 1)
                    act.activation(xcT[:, b, :], tpf[b], ACT.Copy).then_inc(s_pTc, 1)
                    act.wait_ge(s_V, k + 1)
                    pv = (pW, pL)[b]
                    act.activation(V[:, bass.ds(TA * k, TA), :].rearrange("p a d -> p (a d)"), pv[:, :],
                                   ACT.Copy).then_inc(s_Vc, 1)
                    act.activation(vq[:, b, :, :].rearrange("p a d -> p (a d)"), pv[:, :], ACT.Square)\
                        .then_inc(s_Vq, 1)
            for k, (o, i, f, sc) in enumerate(PRO_ACTS):
                act.wait_ge(s_pa, k + 1)
                act.activation(n64[:, o, :], n64[:, i, :], f, scale=sc).then_inc(s_pd, 1)
            act.wait_ge(s_flag, 1)

            def copy_acc(e, general):
                act.wait_ge(*((s_acc, e + 1) if general else (s_mm, NG * e + NG)))
                act.activation(accS[:, :], acc[:, :], ACT.Copy).then_inc(s_accS, 1)

            def load_x(e):
                wait(act, s_x1, e)
                act.dma_start(xin[:, :, :], x_v[e, :, :, :]).then_inc(s_xin, 16)

            def scale_means(e):
                act.wait_ge(s_rd, e + 1)
                for a in range(TA):
                    last = act.activation(hp[:, a, :], pW[:, a * P:(a + 1) * P], ACT.Copy, scale=c4[:, 2, a:a + 1])
                last.then_inc(s_hps, 1)

            def elu_parts(e):
                act.wait_ge(s_hp, e + 1)
                act.activation(yy[:, :, :], hp[:, :, :], ACT.Relu).then_inc(s_re, 1)
                act.activation(ex[:, :, :], ex[:, :, :], ACT.Exp).then_inc(s_ex, 1)

            def square_elu(e):
                act.wait_ge(s_y, e + 1)
                for a in range(TA):
                    last = act.activation(sq[:, a, 1:D], yy[:, a, 1:D], ACT.Square, accum_out=c4[:, 0, a:a + 1])
                last.then_inc(s_sy, 1)

            def sigmoid(e):
                act.wait_ge(s_lf, e + 1)
                for a in range(TA):
                    last = act.activation(ex[:, a, :], yy[:, a, :], ACT.Tanh, scale=c4[:, 9, a:a + 1])
                last.then_inc(s_th, 1)
                act.wait_ge(s_th, e + 1)
                for a in range(TA):
                    last = act.activation(sq[:, a, 1:D], ex[:, a, 1:D], ACT.Square, scale=0.5, bias=expo[:, 0, 0:1],
                                          accum_out=c4[:, 14, a:a + 1])
                last.then_inc(s_ss, 1)

            def exp_norm(e):
                act.wait_ge(s_nn, e + 1)
                act.activation(c4[:, 16, :], c4[:, 15, :], ACT.Exp).then_inc(s_sh, 1)
                act.activation(c4[:, 17, :], c4[:, 15, :], ACT.Exp, scale=-1.0).then_inc(s_sh, 1)

            def apply_sinh(e):
                act.wait_ge(s_kr, e + 1)
                for a in range(TA):
                    last = act.activation(hp[:, a, :], ex[:, a, :], ACT.Identity, scale=c4[:, 25, a:a + 1],
                                          bias=c4[:, 25, a:a + 1])
                last.then_inc(s_sv, 1)

            def copy_x1nT(e):
                act.wait_ge(s_x1T, e + 1)
                act.activation(x1nT[:, :], pW[:, :], ACT.Copy).then_inc(s_x1Tc, 1)

            def exp_logits(e, a):
                act.wait_ge(s_lm, TA * e + a + 1)
                wait(act, s_sw, TA * e + max(a - 1, 0))
                act.activation(es[:, a % 2, :], lg[:, a % 2, :], ACT.Exp).then_inc(s_es, 1)

            def store_x1(e):
                act.wait_ge(s_x1, e + 1)
                act.dma_start(x1_v[e, :, :, :], x1[:, :, :]).then_inc(s_x1o, 16)

            def store_sw(e):
                act.wait_ge(s_sw, TA * e + TA)
                act.dma_start(sw_v[e, :, :, :], sw[:, :, :]).then_inc(s_swo, 16)

            def first(e, n, general=False):
                if n == LEAD:
                    copy_acc(e, general)
                if n == 7:
                    scale_means(e)
                if n == 11:
                    elu_parts(e)
                if n == 15:
                    square_elu(e)
                if n == 24:
                    sigmoid(e)
                if n == 28:
                    exp_norm(e)

            def second(e, n):
                if n == 0:
                    load_x(e)
                if n == 2:
                    apply_sinh(e)
                if n == 8:
                    store_x1(e)
                if n == 12:
                    copy_x1nT(e)
                if n in EXPS:
                    exp_logits(e, EXPS.index(n))

            def evacuate(s, n):
                k = NG * s + n
                act.wait_ge(s_tp, k + 1)
                if not (isinstance(s, int) and k < NAT):
                    act.wait_ge(s_mm, k - NAT + 1)
                act.activation(adjT[:, n % NAT, :], tp[n % NTP][:, :], ACT.Copy).then_inc(s_ev, 1)

            one_shift = act.value_load(flag[0:1, 0:1])
            with act.If(one_shift > 0):
                act.activation(n64[:, 23, :], tt[:, :], ACT.Exp, bias=tm[:, 3:4]).then_inc(s_wexp, 1)
                for c in range(4):
                    act.wait_ge(s_gv, c + 1)
                    act.activation(ghi[:, c * 16:c * 16 + 16, :], V[:, c * 16:c * 16 + 16, :], ACT.Copy)\
                        .then_inc(s_gh, 1)
                act.wait_ge(s_gl, 4)
                for n in range(NG):
                    evacuate(0, n)
                for n in range(NG):
                    first(0, n)
                    evacuate(1, n)
                with act.Fori(2, NSB) as s:
                    for n in range(NG):
                        second(s - 2, n)
                        first(s - 1, n)
                        evacuate(s, n)
                    store_sw(s - 2)
                for n in range(NG):
                    second(NSB - 2, n)
                    first(NSB - 1, n)
                store_sw(NSB - 2)
                for n in range(NG):
                    second(NSB - 1, n)
                store_sw(NSB - 1)
            with act.Else():
                with act.Fori(0, NSB) as s:
                    for a in range(TA):
                        for c in range(NQ):
                            k = (s * TA + a) * NQ + c
                            act.wait_ge(s_ge, k + 1)
                            act.activation(eb[:, :], eb[:, :], ACT.Exp, bias=rm[:, NQ + 1:NQ + 2])\
                                .then_inc(s_gp, 1)
                            act.wait_ge(s_gT, k + 1)
                            act.activation(pT[:, 0:512], pW[:, :], ACT.Copy).then_inc(s_gTc, 1)
                            act.activation(pT[:, 512:1024], pL[:, :], ACT.Copy).then_inc(s_gTc, 1)
                    for n in range(NG):
                        first(s, n, general=True)
                    for n in range(NG):
                        second(s, n)
                    store_sw(s)


            def fa(need, *args, **kw):
                act.wait_ge(s_fd, need)
                act.activation(*args, **kw).then_inc(s_fa, 1)
            fa(F_SILU, xg[:, 0:KC, :], xa[:, 0:KC, :], ACT.Exp, scale=-1.0)
            act.activation(xg[0:NS, KC:6, :], xa[0:NS, KC:6, :], ACT.Exp, scale=-1.0).then_inc(s_fa, 1)
            fa(F_ZEXP, sgz, zT, ACT.Exp, scale=-1.0)
            act.wait_ge(s_fw, 16 * NFW)
            act.activation(Ae[0:G, :], Ae[0:G, :], ACT.Exp).then_inc(s_fa, 1)
            fa(F_DTEXP, dts[0:G, 2, :], dts[0:G, 1, :], ACT.Exp)
            fa(F_SEG, EF[0:G, :], EF[0:G, :], ACT.Exp)
            act.activation(EB[0:G, :], EB[0:G, :], ACT.Exp).then_inc(s_fa, 1)
            with act.Fori(0, NSB // 2) as g:
                for b in range(2):
                    for a in range(0, TA, 2):
                        k = (2 * g + b) * TA + a
                        act.wait_ge(s_fT, k + 1)
                        act.activation(swT[:, a % 2, :], tpf[a % 2], ACT.Copy).then_inc(s_fTc, 1)

        @block.tensor
        def _(pe):
            def mm(out_ap, lhsT, rhs, start=True, stop=True):
                return pe.matmul(out_ap, lhsT, rhs, start=start, stop=stop)

            pe.wait_ge(s_id, 4)
            pe.wait_ge(s_one, 2)
            pe.wait_ge(s_w, 16 * 9)
            pe.transpose(pW[:, 0:P], WAf[:, :], identf[:, :]).then_inc(s_tr, 1)
            pe.transpose(pL[:, 0:P], Wg[:, :], identf[:, :]).then_inc(s_tr, 1)
            pe.transpose(pS[0:HD, 0:G], Wsl[:, :], identf[0:G, 0:G]).then_inc(s_tr, 1)
            pe.wait_ge(s_trc, 3)
            mm(pST[:, 0:1], WAT[:, :], a2[:, :]).then_inc(s_tr, 1)
            pe.wait_ge(s_trc, 4)
            mm(pST[:, 2:3], WgT[:, :], v2[:, :]).then_inc(s_tr, 1)
            for h in range(H):
                last = mm(acc[:, h * G:(h + 1) * G], Wx_n[:, h, :], WslT[:, :])
            last.then_inc(s_tr, 1)
            pe.wait_ge(s_trc, 6)
            for h in range(H):
                last = mm(pS[:, h * G:(h + 1) * G], bxB[:, h, :], WslT[:, :])
            last.then_inc(s_tr, 1)
            pe.wait_ge(s_trc, 5)
            with pe.Fori(0, NSB // 2) as g:
                for b in range(2):
                    k = 2 * g + b
                    pe.wait_ge(s_xc, k + 1)
                    for a in range(TA):
                        last = pe.transpose(tpf[b][:, a * P:(a + 1) * P], xc[:, b, a, :], identf[:, :])
                    last.then_inc(s_pT, 1)
                    pe.wait_ge(s_pTc, k + 1)
                    for a in range(TA):
                        last = mm((pW, pL)[b][:, a * P:(a + 1) * P], xcT[:, b, a * P:(a + 1) * P], Wg[:, :])
                    last.then_inc(s_V, 1)
            pe.wait_ge(s_mx, 1)
            pe.transpose(pST[0:2, 0:P], tm[:, 0:2], identf[:, :]).then_inc(s_mxT, 1)
            pe.wait_ge(s_m2, 1)
            mm(pST[:, 256:258], ones[0:2, :], m2[:, 2:4]).then_inc(s_mb, 1)
            pe.wait_ge(s_beta, 1)
            for c in range(NT):
                last = mm(pL[:, 0:1], V[:, c, :], beta[:, c:c + 1], start=c == 0, stop=c == NT - 1)
            last.then_inc(s_cs, 1)
            pe.wait_ge(s_csb, 1)
            mm(pW[:, 0:P], csb[:, :], WA[:, :]).then_inc(s_hs, 1)

            def transposes(s, n):
                k = NG * s + n
                if n % GPM == 0:
                    pe.wait_ge(s_mask, NM * s + n // GPM + 1)
                if not (isinstance(s, int) and k < NTP):
                    pe.wait_ge(s_ev, k - NTP + 1)
                for c in range(GROUP):
                    j = (n % GPM) * GROUP + c
                    for a in range(TA):
                        last = pe.transpose(tp[n % NTP][:, c * ROWS + a * P:c * ROWS + (a + 1) * P],
                                            mask[:, n // GPM % NMB, a, j * P:(j + 1) * P], identb[:, :])
                last.then_inc(s_tp, 1)

            def products(s, n):
                k = NG * s + n
                if n == 0 and not (isinstance(s, int) and s == 0):
                    pe.wait_ge(s_accS, s)
                pe.wait_ge(s_ev, k + 1)
                for c in range(GROUP):
                    jc = n * GROUP + c
                    for half in (ghi, glo):
                        last = mm(acc[:, :], half[:, jc, :], adjT[:, n % NAT, c * ROWS:(c + 1) * ROWS],
                                  start=jc == 0 and half is ghi, stop=jc == NT - 1 and half is glo)
                last.then_inc(s_mm, 1)

            def aggregate(e):
                pe.wait_ge(s_accS, e + 1)
                for a in range(TA):
                    mm(pW[:, a * P:(a + 1) * P], accS[:, a * P:(a + 1) * P], WA[:, :])
                for a in range(TA):
                    last = mm(pL[:, a:a + 1], accS[:, a * P:(a + 1) * P], e0[:, :])
                last.then_inc(s_agg, 1)

            def turn_x1n(e, sums):
                pe.wait_ge(s_x1n, e + 1)
                pe.wait_ge(s_hps, sums)
                for a in range(TA):
                    last = pe.transpose(pW[:, a * P:(a + 1) * P], x1n[:, a, :], identf[:, :])
                last.then_inc(s_x1T, 1)

            def logits(e, a, dens):
                pe.wait_ge(s_x1Tc, e + 1)
                if a == 0:
                    pe.wait_ge(s_den, dens)
                wait(pe, s_lb, TA * e + a)
                mm(pL[:, :], x1nT[:, a * P:(a + 1) * P], WcT[:, :]).then_inc(s_lg, 1)

            def zero_slices():
                pe.wait_ge(s_zero, 1)
                mm(pST[:, :], zeros[:, 0:P], zeros[:, :], start=True, stop=False)

            def slices(e, a):
                pe.wait_ge(s_sw, TA * e + a + 1)
                last = mm(pST[:, :], x1n[:, a, :], sw[:, a, :], start=False, stop=False)
                if a == TA - 1:
                    last.then_inc(s_st, 1)

            def first(e, n):
                if n == 1:
                    aggregate(e)

            def second(e, n, dens):
                if n == 9:
                    turn_x1n(e, dens)
                if n in LOGITS:
                    logits(e, LOGITS.index(n), dens)
                if n in SLICES:
                    slices(e, SLICES.index(n))

            one_shift = pe.value_load(flag[0:1, 0:1])
            with pe.If(one_shift > 0):
                pe.wait_ge(s_gl, 4)
                pe.wait_ge(s_hsc, 1)
                zero_slices()
                for n in range(LEAD):
                    transposes(0, n)

                def stream(s, behind, final):
                    for n in range(NG):
                        if n + LEAD < NG:
                            transposes(s, n + LEAD)
                        elif not final:
                            transposes(s + 1, n + LEAD - NG)
                        if behind > 1:
                            second(s - 2, n, s)
                        if behind > 0:
                            first(s - 1, n)
                        products(s, n)

                stream(0, 0, False)
                stream(1, 1, False)
                with pe.Fori(2, NSB - 1) as s:
                    stream(s, 2, False)
                stream(NSB - 1, 2, True)
                for n in range(NG):
                    second(NSB - 2, n, NSB)
                    first(NSB - 1, n)
                for n in range(NG):
                    second(NSB - 1, n, NSB)
            with pe.Else():
                pe.wait_ge(s_gh2, 1)
                pe.wait_ge(s_hsc, 1)
                zero_slices()
                with pe.Fori(0, NSB) as s:
                    for a in range(TA):
                        for c in range(NQ):
                            k = (s * TA + a) * NQ + c
                            pe.wait_ge(s_gp, k + 1)
                            for j in range(8):
                                last = pe.transpose((pW, pL)[j // 4][:, j % 4 * P:(j % 4 + 1) * P],
                                                    eb[:, j * P:(j + 1) * P], identf[:, :])
                            last.then_inc(s_gT, 1)
                            pe.wait_ge(s_gTc, 2 * k + 2)
                            for j in range(8):
                                last = mm(acc[:, a * P:(a + 1) * P], V[:, c * 8 + j, :], pT[:, j * P:(j + 1) * P],
                                          start=c == 0 and j == 0, stop=c == NQ - 1 and j == 7)
                    last.then_inc(s_acc, 1)
                    for n in range(NG):
                        first(s, n)
                    for n in range(NG):
                        second(s, n, s + 1)

            mm(pST[:, :], zeros[:, 0:P], zeros[:, :], start=False, stop=True).then_inc(s_st, 1)
            pe.wait_ge(s_fw, 16 * NFW)
            for k, (blocks, _) in enumerate(TURNED):
                bank = (tpf[0], tpf[1], tpf[2])[k % 3]
                if k >= 3:
                    pe.wait_ge(s_ftc, k - 2)
                for j, (src, n) in enumerate(blocks):
                    last = pe.transpose(bank[:, j * P:j * P + n], src, identf[0:n, 0:n])
                last.then_inc(s_ft, 1)
            pe.wait_ge(s_sws, TA * NSB)
            mm(pW[:, :], ones[:, :], swsum[:, :]).then_inc(s_fp, 1)
            pe.wait_ge(s_ftc, len(TURNED))
            pe.wait_ge(s_std, 1)
            for h in range(H):
                r = (h % 2) * 64
                last = mm(pL[r:r + 64, (h // 2) * G:(h // 2 + 1) * G], wfT[:, h * HD:(h + 1) * HD],
                          STacc[:, h * G:(h + 1) * G])
            last.then_inc(s_fp, 1)
            pe.wait_ge(s_fd, F_UT)
            for c in range(KC):
                for k in range(KC):
                    last = mm(pS[:, c * G:(c + 1) * G], inT[:, k, c * P:(c + 1) * P], uT[:, k, :], k == 0, k == KC - 1)
            for c in range(KC):
                for k in range(KC):
                    last = mm(pST[:, c * G:(c + 1) * G], inT[:, k, DI + c * P:DI + (c + 1) * P], uT[:, k, :],
                              k == 0, k == KC - 1)
            for c in range(2):
                a = 2 * DI + c * NS
                for k in range(KC):
                    last = mm(acc[0:NS, c * G:(c + 1) * G], inT[:, k, a:a + NS], uT[:, k, :], k == 0, k == KC - 1)
            for k in range(KC):
                last = mm(tpf[0][0:G, 0:2 * H], uT[:, k, :], inT[:, k, DIP - 2 * H:DIP], k == 0, k == KC - 1)
            last.then_inc(s_fp, 1)
            pe.wait_ge(s_fd, F_AD)
            pe.wait_ge(s_fg, 4)
            mm(tpf[1][0:G, :], M2[0:G, :], aF[0:G, :])
            mm(tpf[2][0:G, :], M1[0:G, :], aB[0:G, :]).then_inc(s_fp, 1)
            pe.wait_ge(s_fd, F_XA)
            for c in range(KC):
                pe.transpose(pL[0:G, c * P:(c + 1) * P], xa[:, c, :], identf[:, :])
            mm(tpf[0][0:G, 64:64 + 2 * G], xa[0:NS, KC, :], Csh[0:NS, :])
            for c in range(KC):
                for k in range(KC):
                    last = mm(pW[:, c * G:(c + 1) * G], fcT[:, k, c * P:(c + 1) * P], xa[:, k, :], k == 0, k == KC - 1)
            last.then_inc(s_fp, 1)
            pe.wait_ge(s_fd, F_M)
            for h in range(H):
                r = (h % 2) * 64
                last = mm(acc[r:r + 64, (h // 2) * G:(h // 2 + 1) * G], xt[0:G, h * HD:(h + 1) * HD],
                          EF[0:G, h * G:(h + 1) * G])
            last.then_inc(s_fp, 1)
            pe.wait_ge(s_fd, F_YQ)
            for c in range(KC):
                last = mm(tpf[1][:, 0:G], ones[:, :], yq[:, c, :], c == 0, c == KC - 1)
            last.then_inc(s_fp, 1)
            pe.wait_ge(s_fd, F_YN)
            for c in range(KC):
                for k in range(KC):
                    last = mm(tpf[2][:, c * G:(c + 1) * G], oT[:, k, c * P:(c + 1) * P], yT[:, k, :], k == 0, k == KC - 1)
            last.then_inc(s_fp, 1)
            pe.wait_ge(s_fd, F_OT)
            for h in range(H):
                r = (h % 2) * 64
                last = mm(pW[r:r + 64, (h // 2) * D:(h // 2 + 1) * D], otT[r:r + 64, h // 2, :],
                          woT[r:r + 64, h // 2, :])
            last.then_inc(s_fp, 1)
            pe.wait_ge(s_fd, F_MO)

            with pe.Fori(0, NSB // 2) as g:
                for b in range(2):
                    s = 2 * g + b
                    pe.wait_ge(s_fl[b], 32 * g + 32)
                    for a in range(TA):
                        k = s * TA + a
                        for c in range(KC):
                            last = pe.transpose(tpf[a % 2][:, c * P:(c + 1) * P], swl[:, b, a, c * P:(c + 1) * P],
                                                identf[:, :])
                        last.then_inc(s_fT, 1)
                        if a % 2 == 1:
                            for aa in (a - 1, a):
                                pe.wait_ge((s_fTc, s_fTd)[aa % 2], 2 * s + a // 2 + 1)
                                if aa == 0:
                                    pe.wait_ge(s_fy2, s + 1)
                                for c in range(KC):
                                    last = mm((pW, pL)[b][:, aa * P:(aa + 1) * P], swT[:, aa % 2, c * P:(c + 1) * P],
                                              Mo[:, c, :], c == 0, c == KC - 1)
                    last.then_inc(s_fm, 1)

        @block.vector
        def _(dve):
            cnt = {}

            def linker(s):
                cnt[s.name] = 0

                def link(ins, wait=True):
                    ins.then_inc(s, 1)
                    cnt[s.name] += 1
                    if wait:
                        dve.wait_ge(s, cnt[s.name])
                    return ins
                return link
            link = linker(ch)
            ts, tts, stt = dve.tensor_scalar, dve.tensor_tensor, dve.scalar_tensor_tensor

            def log1p(link, u, ln, o, t1, t2, cap=0.5):
                link(ts(t1, u, cap, None, ALU.min))
                link(ts(t2, t1, 2.0, None, ALU.add))
                link(dve.reciprocal(t2, t2))
                link(tts(t1, t1, t2, ALU.mult))
                link(tts(t2, t1, t1, ALU.mult))
                odd = (17, 15, 13, 11, 9, 7, 5, 3) if cap > 0.5 else (13, 11, 9, 7, 5, 3)
                link(ts(o, t2, 1.0 / odd[0], 1.0 / odd[1], ALU.mult, ALU.add))
                for k in odd[2:] + (1,):
                    link(tts(o, o, t2, ALU.mult))
                    link(ts(o, o, 1.0 / k, None, ALU.add))
                link(tts(o, o, t1, ALU.mult))
                link(ts(o, o, 2.0, None, ALU.mult))
                if ln is not None:
                    link(ts(t1, u, cap, None, ALU.is_gt))
                    link(tts(t2, ln, o, ALU.subtract))
                    link(tts(t2, t2, t1, ALU.mult))
                    link(tts(o, o, t2, ALU.add))

            def log1p_fraction(link, u, z, el, t, b):
                link(ts(t, u, 1.0, None, ALU.add))
                link(ts(b, t.bitcast(I32), 23, None, ALU.logical_shift_right))
                link(ts(el, b, -127.0, LN2, ALU.add, ALU.mult))
                link(ts(b, t.bitcast(I32), 0x7fffff, 0x3f800000, ALU.bitwise_and, ALU.bitwise_or))
                link(ts(z, b.bitcast(F32), -1.0, None, ALU.add))
                link(tts(t, u, z, ALU.subtract))
                link(stt(out=t, in0=el, scalar=0.0, in1=t, op0=ALU.is_equal, op1=ALU.mult))
                link(tts(z, z, t, ALU.add))
                link(ts(t, z, 2.0, None, ALU.add))
                link(dve.reciprocal(t, t))
                link(tts(z, z, t, ALU.mult))

            def log1p_sum(link, o, z, el, t):
                link(tts(t, z, z, ALU.mult))
                link(ts(o, t, 1.0 / 17, None, ALU.mult))
                for k in (15, 13, 11, 9, 7, 5, 3):
                    link(stt(out=o, in0=o, scalar=1.0 / k, in1=t, op0=ALU.add, op1=ALU.mult))
                link(stt(out=o, in0=o, scalar=1.0, in1=z, op0=ALU.add, op1=ALU.mult))
                link(stt(out=o, in0=o, scalar=2.0, in1=el, op0=ALU.mult, op1=ALU.add))

            dve.wait_ge(s_tr, 1)
            dve.tensor_copy(WAT[:, :], pW[:, 0:P]).then_inc(s_trc, 1)
            dve.wait_ge(s_tr, 2)
            dve.tensor_copy(WgT[:, :], pL[:, 0:P]).then_inc(s_trc, 1)
            dve.wait_ge(s_tr, 3)
            dve.tensor_copy(WslT[:, :], pS[0:HD, 0:G]).then_inc(s_trc, 1)
            dve.wait_ge(s_tr, 4)
            dve.tensor_copy(v2[:, :], pST[:, 0:1]).then_inc(s_trc, 1)
            dve.wait_ge(s_tr, 5)
            dve.tensor_copy(Wg[:, 0:1], pST[:, 2:3]).then_inc(s_trc, 1)
            dve.tensor_copy(bxB[:, :, :], bxT[:, :].unsqueeze(2).to_broadcast([HD, H, P])).then_inc(s_trc, 1)
            link(ts(tmpB[:, :], tmpB[:, :], 1e-6, None, ALU.max))
            link(dve.reciprocal(tmpB[:, :], tmpB[:, :]))
            dve.wait_ge(s_tr, 6)
            link(tts(hg(WcT[:, :]), hg(acc[:, :]), tmpB[:, :].unsqueeze(2).to_broadcast([P, H, G]), ALU.mult))
            dve.wait_ge(s_tr, 7)
            link(tts(hg(bl[:, :]), hg(pS[:, :]), bsB[:, :].unsqueeze(1).to_broadcast([P, H, G]), ALU.add))
            link(tts(hg(bl[:, :]), hg(bl[:, :]), tmpB[:, :].unsqueeze(2).to_broadcast([P, H, G]), ALU.mult))
            dve.memset(zeros[:, :], 0.0).then_inc(s_zero, 1)
            N64 = lambda k: n64[:, k, :]
            PER = 5
            with dve.Fori(0, NSB // 2) as g:
                k0 = [0]

                def step(ins):
                    k0[0] += 1
                    ins.then_inc(chp, 1)
                    dve.wait_ge(chp, g * 2 * PER + k0[0])
                for b in range(2):
                    k = 2 * g + b
                    col = bass.ds(TA * k, TA)
                    dve.wait_ge(s_xs[b], 16 * g + 16)
                    step(dve.tensor_reduce(n64[:, 0, col], xs[:, b, :, :], AXX, ALU.add))
                    step(ts(n64[:, 0, col], n64[:, 0, col], 1.0 / D, None, ALU.mult))
                    dve.wait_ge(s_pT, k)
                    tts(xc[:, b, :, :], xs[:, b, :, :], n64[:, 0, col].unsqueeze(2).to_broadcast([P, TA, D]),
                        ALU.subtract).then_inc(s_xc, 1)
                    dve.wait_ge(s_xc, k + 1)
                    dve.tensor_copy(n64[:, 2, col], xc[:, b, :, 0]).then_inc(s_xfree, 1)
                    dve.wait_ge(s_xqd, k + 1)
                    step(dve.tensor_reduce(n64[:, 4, col], xq[:, b, :, 1:D], AXX, ALU.add))
                    step(tts(n64[:, 1, col], n64[:, 4, col], xq[:, b, :, 0], ALU.add))
                    dve.wait_ge(s_Vq, k + 1)
                    step(dve.tensor_reduce(n64[:, 3, col], vq[:, b, :, 1:D], AXX, ALU.add))
                assert k0[0] == 2 * PER

            asked = [0, 0]

            def root():
                asked[0] += 1
                dve.sem_inc(s_pg, 1)
                dve.wait_ge(s_pr, asked[0])

            def hand_act(n=1):
                asked[1] += n
                dve.sem_inc(s_pa, n)
                dve.wait_ge(s_pd, asked[1])

            link(ts(N64(5), N64(1), 1.0 / D, 1e-5, ALU.mult, ALU.add))
            root()
            root()
            root()
            link(tts(N64(2), N64(2), N64(6), ALU.mult))
            link(ts(N64(2), N64(2), -1.0, EPS1, ALU.add, ALU.max))
            link(ts(N64(9), N64(2), 2.0, None, ALU.add))
            link(tts(N64(9), N64(9), N64(2), ALU.mult))
            root()
            link(tts(N64(11), N64(10), N64(2), ALU.add))
            link(ts(N64(12), N64(11), 1.0, None, ALU.add))
            hand_act()
            log1p(link, N64(11), N64(13), N64(14), N64(15), N64(16))
            link(tts(N64(7), N64(7), N64(6), ALU.mult))
            link(ts(N64(7), N64(7), MIN_NORM, None, ALU.max))
            link(dve.reciprocal(N64(7), N64(7)))
            link(tts(N64(14), N64(14), N64(7), ALU.mult))
            link(tts(N64(14), N64(14), N64(6), ALU.mult))
            link(tts(N64(8), N64(8), N64(14), ALU.mult))
            link(ts(N64(9), N64(8), MIN_NORM, None, ALU.max))
            hand_act(2)
            link(dve.reciprocal(N64(12), N64(9)))
            link(tts(N64(10), N64(10), N64(11), ALU.subtract))
            link(tts(N64(10), N64(10), N64(12), ALU.mult))
            link(ts(N64(10), N64(10), 0.5, None, ALU.mult))
            link(ts(N64(11), N64(9), 1.0, None, ALU.min))
            link(tts(N64(11), N64(11), N64(11), ALU.mult))
            link(ts(N64(12), N64(11), 1.0 / 72, 1.0, ALU.mult, ALU.add))
            for k in (42.0, 20.0, 6.0):
                link(tts(N64(12), N64(12), N64(11), ALU.mult))
                link(ts(N64(12), N64(12), 1.0 / k, 1.0, ALU.mult, ALU.add))
            link(ts(N64(11), N64(9), 1.0, None, ALU.is_gt))
            link(tts(N64(10), N64(10), N64(12), ALU.subtract))
            link(tts(N64(10), N64(10), N64(11), ALU.mult))
            link(tts(N64(10), N64(10), N64(12), ALU.add))
            link(tts(N64(8), N64(8), N64(10), ALU.mult))
            link(tts(N64(9), N64(8), N64(8), ALU.mult))
            link(ts(N64(12), N64(9), 1.0, None, ALU.add))
            root()
            link(ts(N64(13), N64(13), 1.0, None, ALU.add))
            link(dve.reciprocal(N64(13), N64(13)))
            link(tts(N64(9), N64(9), N64(13), ALU.mult))
            link(ts(N64(9), N64(9), EPS1, None, ALU.max))
            link(ts(N64(12), N64(9), 2.0, None, ALU.add))
            link(tts(N64(12), N64(12), N64(9), ALU.mult))
            root()
            link(tts(N64(9), N64(9), N64(13), ALU.add))
            link(ts(N64(12), N64(9), 1.0, None, ALU.add))
            hand_act()
            log1p(link, N64(9), N64(13), N64(17), N64(15), N64(16))
            link(ts(N64(8), N64(8), MIN_NORM, None, ALU.max))
            link(dve.reciprocal(N64(8), N64(8)))
            link(tts(N64(17), N64(17), N64(8), ALU.mult))
            link(tts(N64(17), N64(17), N64(10), ALU.mult))
            link(tts(beta[:, :], N64(17), N64(14), ALU.mult))
            dve.wait_ge(s_Vc, NSB)
            link(tts(tt[:, :], beta[:, :], V[:, :, 0], ALU.mult))
            link(ts(N64(18), tt[:, :], -1.0, None, ALU.mult))
            link(dve.tensor_reduce(tm[:, 0:1], tt[:, :], AXX, ALU.max))
            dve.tensor_reduce(tm[:, 1:2], N64(18), AXX, ALU.max).then_inc(s_mx, 1)
            dve.wait_ge(s_mx, 1)
            dve.sem_inc(s_beta, 1)
            dve.wait_ge(s_mxT, 1)
            link(dve.tensor_reduce(m2[:, 0:1], pST[0:2, 0:P], AXX, ALU.max))
            ts(m2[:, 2:4], identf[0:2, 0:2], m2[:, 0:1], None, ALU.mult).then_inc(s_m2, 1)
            dve.wait_ge(s_mb, 1)
            link(dve.tensor_copy(tm[:, 4:6], pST[:, 256:258]))
            link(tts(tm[:, 2:3], tm[:, 4:5], tm[:, 5:6], ALU.add))
            link(tts(tm[:, 3:4], tm[:, 5:6], tm[:, 4:5], ALU.subtract))
            link(ts(tm[:, 3:4], tm[:, 3:4], 0.5, None, ALU.mult))
            ts(flag[:, :], tm[:, 2:3], SPREAD, None, ALU.is_le).then_inc(s_flag, 1)
            dve.wait_ge(s_cs, 1)
            link(dve.tensor_copy(csum[:, :], pL[:, 0:1]))
            dve.tensor_copy(csb[:, :], csum[:, 0:1].to_broadcast([P, P])).then_inc(s_csb, 1)
            dve.wait_ge(s_hs, 1)
            dve.tensor_copy(Hs[:, :], pW[:, 0:P]).then_inc(s_hsc, 1)
            dve.wait_ge(s_flag, 1)

            C = lambda k, n=1: c4[:, k, :]
            bc = lambda k: c4[:, k, :].unsqueeze(2).to_broadcast([P, TA, D])

            class Chain:
                def __init__(self, s, e, total):
                    self.s, self.e, self.total, self.n = s, e, total, 0

                def __call__(self, ins):
                    self.n += 1
                    ins.then_inc(self.s, 1)
                    dve.wait_ge(self.s, self.total * self.e + self.n)

            class First:
                def __init__(self, e):
                    self.e, self.link = e, Chain(che, e, CHAIN_A)

                def row_scales(self):
                    e, link = self.e, self.link
                    dve.wait_ge(s_agg, e + 1)
                    dve.tensor_copy(C(0), pL[:, 0:TA]).then_inc(s_den, 1)
                    dve.wait_ge(s_den, e + 1)
                    link(ts(C(1), C(0), 0.0, None, ALU.is_equal))
                    link(stt(out=C(2), in0=C(1), scalar=float(N), in1=C(0), op0=ALU.mult, op1=ALU.add))
                    link(dve.reciprocal(C(2), C(2)))
                    tts(C(1), C(1), C(2), ALU.mult).then_inc(s_rd, 1)

                def means(self):
                    e, link = self.e, self.link
                    dve.wait_ge(s_hps, e + 1)
                    for a in range(TA):
                        last = stt(out=hp[:, a, :], in0=Hs[:, :], scalar=c4[:, 1, a:a + 1], in1=hp[:, a, :],
                                   op0=ALU.mult, op1=ALU.add)
                    link(last)
                    ts(ex[:, :, :], hp[:, :, :], 0.0, None, ALU.min).then_inc(s_hp, 1)

                def elu(self):
                    e = self.e
                    dve.wait_ge(s_re, e + 1)
                    dve.wait_ge(s_ex, e + 1)
                    stt(out=yy[:, :, :], in0=ex[:, :, :], scalar=-1.0, in1=yy[:, :, :], op0=ALU.add, op1=ALU.add)\
                        .then_inc(s_y, 1)

                def theta(self):
                    e, link = self.e, self.link
                    dve.wait_ge(s_rt, 3 * e + 1)
                    link(ts(C(2), C(2), MIN_NORM, None, ALU.max))
                    link(ts(C(3), C(3), 1.0, None, ALU.add))
                    link(dve.reciprocal(C(3), C(3)))
                    link(tts(C(3), C(3), C(0), ALU.mult))
                    link(ts(C(3), C(3), EPS1, None, ALU.max))
                    link(stt(out=C(4), in0=C(3), scalar=2.0, in1=C(3), op0=ALU.add, op1=ALU.mult))
                    dve.sem_inc(s_rq1, 1)
                    link(dve.reciprocal(C(2), C(2)))
                    link(ts(C(2), C(2), 0.5, None, ALU.mult))

                def log_argument(self):
                    e, link = self.e, self.link
                    dve.wait_ge(s_rt, 3 * e + 2)
                    link(tts(C(6), C(3), C(5), ALU.add))
                    log1p_fraction(link, C(6), C(7), C(8), C(10), bits[:, 0, :])

                def log_factor(self):
                    log1p_sum(self.link, C(9), C(7), C(8), C(10))
                    tts(C(9), C(9), C(2), ALU.mult).then_inc(s_lf, 1)

                def norm_s(self):
                    e, link = self.e, self.link
                    dve.wait_ge(s_rt, 3 * e + 3)
                    ts(C(15), C(15), MIN_NORM, None, ALU.max).then_inc(s_nn, 1)
                    dve.wait_ge(s_nn, e + 1)
                    link(dve.reciprocal(C(19), C(15)))

                    assert self.link.n == CHAIN_A, self.link.n

                def at(self, n):
                    if n == 5:
                        self.row_scales()
                    if n == 8:
                        self.means()
                    if n == 12:
                        self.elu()
                    if n == 18:
                        self.theta()
                    if n == 20:
                        self.log_argument()
                    if n == 21:
                        self.log_factor()
                    if n == 26:
                        self.norm_s()

            class Second:
                def __init__(self, e):
                    self.e, self.link = e, Chain(che2, e, CHAIN_B)

                def sinh(self):
                    e, link = self.e, self.link
                    dve.wait_ge(s_sh, 2 * e + 2)
                    link(tts(C(18), C(16), C(17), ALU.subtract))
                    stt(out=C(25), in0=C(18), scalar=0.25, in1=C(19), op0=ALU.mult, op1=ALU.mult).then_inc(s_kr, 1)
                    dve.wait_ge(s_kr, e + 1)
                    link(tts(C(20), C(25), C(25), ALU.mult))
                    link(tts(C(20), C(20), C(14), ALU.mult))
                    link(ts(C(20), C(20), 4.0, 1.0, ALU.mult, ALU.add))
                    dve.sem_inc(s_rq2, 1)

                def residual(self):
                    e, link = self.e, self.link
                    dve.wait_ge(s_sv, e + 1)
                    dve.wait_ge(s_rt2, 2 * e + 1)
                    link(dve.tensor_copy(hp[:, :, 0], C(21)))
                    dve.wait_ge(s_xin, 16 * e + 16)
                    wait(dve, s_x1o, 16 * e)
                    tts(x1[:, :, :], hp[:, :, :], xin[:, :, :], ALU.add).then_inc(s_x1, 1)
                    dve.wait_ge(s_x1, e + 1)

                def statistics(self):
                    link = self.link
                    for a in range(TA):
                        last = dve.bn_stats(bst[:, a, :], x1[:, a, :])
                    link(last)
                    dve.sem_inc(dve_tick, 1)
                    for a in range(TA):
                        last = dve.bn_aggr(mv[:, a, :], bst[:, a, :])
                    link(last)
                    link(ts(C(23), mv[:, :, 1], 1e-5, None, ALU.add))
                    dve.sem_inc(s_rq2, 1)

                def layernorm(self):
                    dve.wait_ge(s_rt2, 2 * self.e + 2)
                    wait(dve, s_st, self.e)
                    for a in range(TA):
                        last = ts(x1n[:, a, :], x1[:, a, :], mv[:, a, 0:1], c4[:, 24, a:a + 1], ALU.subtract, ALU.mult)
                    last.then_inc(s_x1n, 1)

                def logits(self, a):
                    e = self.e
                    dve.wait_ge(s_lg, TA * e + a + 1)
                    wait(dve, s_es, TA * e + max(a - 1, 0))
                    tts(lg[:, a % 2, :], pL[:, :], bl[:, :], ALU.add).then_inc(s_lb, 1)
                    dve.wait_ge(s_lb, TA * e + a + 1)
                    dve.tensor_reduce(r8[:, a % 2, 0, :], hg(lg[:, a % 2, :]), AXX, ALU.max).then_inc(s_lx, 1)

                def sums(self, a):
                    e, link = self.e, self.link
                    dve.wait_ge(s_es, TA * e + a + 1)
                    link(dve.tensor_reduce(r8[:, a % 2, 1, :], hg(es[:, a % 2, :]), AXX, ALU.add))
                    dve.reciprocal(r8[:, a % 2, 1, :], r8[:, a % 2, 1, :]).then_inc(s_rs, 1)

                def at(self, n):
                    if n == 0:
                        self.sinh()
                    if n == 4:
                        self.residual()
                        self.statistics()
                    if n == 6:
                        self.layernorm()
                    if n in MAXIMA:
                        self.logits(MAXIMA.index(n))
                    if n in SUMS:
                        self.sums(SUMS.index(n))
                    if n == NG - 1:
                        assert self.link.n == CHAIN_B, self.link.n

            def make_mask(s, h):
                if h >= NM:
                    s, h = s + 1, h - NM
                q = h // MPQ
                dve.wait_ge(s_adj[q % NBUF], 16 * ((NQ // NBUF) * s + q // NBUF + 1))
                if not (isinstance(s, int) and s == 0 and h < NMB):
                    dve.wait_ge(s_tp, NG * s + (h - NMB + 1) * GPM)
                ts(mask[:, h % NMB, :, :], adjb[:, q % NBUF, :].rearrange("p (a j) -> p a j", a=TA)
                   [:, :, h % MPQ * MCOLS:(h % MPQ + 1) * MCOLS], 0, None, ALU.is_gt).then_inc(s_mask, 1)

            one_shift = dve.value_load(flag[0:1, 0:1])
            with dve.If(one_shift > 0):
                dve.wait_ge(s_cs, 1)
                dve.wait_ge(s_wexp, 1)
                link(tts(N64(22), N64(23), beta[:, :], ALU.mult))
                for c in range(4):
                    k = slice(c * 16, c * 16 + 16)
                    tts(V[:, k, :], V[:, k, :], n64[:, 22, k].unsqueeze(2).to_broadcast([P, 16, D]), ALU.mult)\
                        .then_inc(s_gw, 1)
                    dve.wait_ge(s_gw, c + 1)
                    dve.tensor_copy(V[:, k, 0], n64[:, 23, k]).then_inc(s_gv, 1)
                for c in range(4):
                    k = slice(c * 16, c * 16 + 16)
                    dve.wait_ge(s_gv, 4)
                    dve.wait_ge(s_gh, c + 1)
                    tts(glo[:, k, :], V[:, k, :], ghi[:, k, :].bitcast(F32), ALU.subtract).then_inc(s_gl, 1)
                dve.wait_ge(s_gl, 4)
                for h in range(NM + MHEAD):
                    make_mask(0, h)

                def stream(s, second, final):
                    b = Second(s - 2)
                    a = First(s - 1)
                    for n in range(NG):
                        if n % GPM == 1 and not (final and (n + MLEAD) // GPM >= NM):
                            make_mask(s, (n + MLEAD) // GPM)
                        if second:
                            b.at(n)
                        a.at(n)
                stream(1, False, False)
                with dve.Fori(2, NSB - 1) as s:
                    stream(s, True, False)
                stream(NSB - 1, True, True)
                b, a = Second(NSB - 2), First(NSB - 1)
                for n in range(NG):
                    b.at(n)
                    a.at(n)
                b = Second(NSB - 1)
                for n in range(NG):
                    b.at(n)
            with dve.Else():
                dve.wait_ge(s_cs, 1)
                dve.sem_inc(s_tst, 1)
                tts(V[:, :, :], V[:, :, :], beta[:, :].unsqueeze(2).to_broadcast([P, NT, D]), ALU.mult)\
                    .then_inc(s_gw, 1)
                dve.wait_ge(s_gw, 1)
                dve.memset(V[:, :, 0], 1.0).then_inc(s_gh2, 1)
                with dve.Fori(0, NSB) as s:
                    for a in range(TA):
                        for sweep in range(2):
                            for c in range(NQ):
                                k = ((s * TA + a) * 2 + sweep) * NQ + c
                                n = 3 * k
                                dve.wait_ge(s_ga, 16 * k + 16)
                                dve.wait_ge(s_gt, 16 * k + 16)
                                if c == 0 and sweep == 0:
                                    dve.wait_ge(s_gT, (s * TA + a) * NQ)
                                if sweep == 1 and c > 0:
                                    dve.wait_ge(s_gT, (s * TA + a) * NQ + c)
                                ts(mb[:, :], adjb[:, 0, 0:STEP], 0, None, ALU.is_gt).then_inc(chg, 1)
                                dve.wait_ge(chg, n + 1)
                                tts(eb[:, :], mb[:, :], tb[:, :], ALU.mult).then_inc(chg, 1)
                                dve.wait_ge(chg, n + 2)
                                ts(mb[:, :], mb[:, :], -MASKED, MASKED, ALU.mult, ALU.add).then_inc(chg, 1)
                                dve.wait_ge(chg, n + 3)
                                tts(eb[:, :], eb[:, :], mb[:, :], ALU.add).then_inc(s_gm, 1)
                                dve.wait_ge(s_gm, k + 1)
                                if sweep == 0:
                                    dve.tensor_reduce(rm[:, c:c + 1], eb[:, :], AXX, ALU.max).then_inc(chm, 1)
                                    if c == NQ - 1:
                                        m = (s * TA + a) * (NQ + 2) + NQ
                                        dve.wait_ge(chm, m)
                                        dve.tensor_reduce(rm[:, NQ:NQ + 1], rm[:, 0:NQ], AXX, ALU.max)\
                                            .then_inc(chm, 1)
                                        dve.wait_ge(chm, m + 1)
                                        ts(rm[:, NQ + 1:NQ + 2], rm[:, NQ:NQ + 1], -1.0, None, ALU.mult)\
                                            .then_inc(chm, 1)
                                        dve.wait_ge(chm, m + 2)
                                else:
                                    dve.sem_inc(s_ge, 1)
                    a, b = First(s), Second(s)
                    for n in range(NG):
                        a.at(n)
                    for n in range(NG):
                        b.at(n)

            link = linker(chf)
            cnt_fd = [0]

            def mark(k, ins):
                cnt_fd[0] += 1
                assert cnt_fd[0] == k
                ins.then_inc(s_fd, 1)
                dve.wait_ge(s_fd, k)
            dve.wait_ge(s_st, NSB + 1)
            dve.tensor_copy(STacc[:, :], pST[:, :]).then_inc(s_std, 1)
            for k, (_, dst) in enumerate(TURNED):
                dve.wait_ge(s_ft, k + 1)
                bank = (tpf[0], tpf[1], tpf[2])[k % 3]
                for j, (d, src) in enumerate(dst):
                    last = dve.tensor_copy(d, src(bank))
                last.then_inc(s_ftc, 1)
            dve.wait_ge(s_fp, 1)
            link(dve.tensor_copy(SN, pW[:, :]))
            link(ts(rS, SN, 1e-5, None, ALU.add))
            link(dve.reciprocal(rS, rS))
            dve.wait_ge(s_fp, 2)
            for half in range(2):
                r = slice(half * 64, half * 64 + 64)
                snh = SN[r, :].rearrange("p (c t g) -> p c t g", t=2, g=G)[:, :, half, :]
                rsh = rS[r, :].rearrange("p (c t g) -> p c t g", t=2, g=G)[:, :, half, :]
                link(tts(uT[r, :, :], snh, bfx[r, :].unsqueeze(2).to_broadcast([64, KC, G]), ALU.mult))
                link(tts(uT[r, :, :], uT[r, :, :], pL[r, 0:KC * G].rearrange("p (c g) -> p c g", g=G), ALU.add))
                if half == 0:
                    link(tts(uT[r, :, :], uT[r, :, :], rsh, ALU.mult))
                else:
                    mark(F_UT, tts(uT[r, :, :], uT[r, :, :], rsh, ALU.mult))
            link(dve.memset(xb, 0.0))
            link(dve.memset(Csh[0:NS, :], 0.0))
            dve.wait_ge(s_fp, 3)
            v3 = lambda ap, g=G: ap.rearrange("p (c g) -> p c g", g=g)
            mark(F_ZEXP, dve.tensor_copy(zT, v3(pS[:, 0:KC * G])))
            dve.tensor_copy(xb[:, 0:KC, 2:], v3(pST[:, 0:KC * G])).then_inc(chf, 1)
            cnt[chf.name] += 1
            link(dve.tensor_copy(xb[0:NS, KC:6, 2:], v3(acc[0:NS, 0:2 * G])))
            for r, cs in ((slice(0, P), slice(0, KC)), (slice(0, NS), slice(KC, 6))):
                n = cs.stop - cs.start
                m = r.stop
                for k in range(3):
                    wk = cw[r, cs, k].unsqueeze(2).to_broadcast([m, n, G])
                    if k == 0:
                        link(tts(xa[r, cs, :], xb[r, cs, 0:G], wk, ALU.mult))
                    else:
                        link(tts(xg[r, cs, :], xb[r, cs, k:k + G], wk, ALU.mult))
                        link(tts(xa[r, cs, :], xa[r, cs, :], xg[r, cs, :], ALU.add))
                bk = cb[r, cs].unsqueeze(2).to_broadcast([m, n, G])
                if cs.start == 0:
                    link(tts(xa[r, cs, :], xa[r, cs, :], bk, ALU.add))
                else:
                    mark(F_SILU, tts(xa[r, cs, :], xa[r, cs, :], bk, ALU.add))
            T = lambda k: dts[0:G, k, :]
            link(tts(T(0), tpf[0][0:G, 0:2 * H], dtb[0:G, :], ALU.add))
            link(ts(T(3), T(0), -1.0, None, ALU.mult))
            mark(F_DTEXP, tts(T(1), T(0), T(3), ALU.min))
            dve.wait_ge(s_fa, 5)
            log1p(link, T(2), None, T(4), T(5), T(6), cap=1.0)
            link(ts(T(0), T(0), 0.0, None, ALU.max))
            link(tts(T(0), T(0), T(4), ALU.add))
            link(tts(T(7), T(0), Ae[0:G, :], ALU.mult))
            link(ts(T(7), T(7), -1.0, -1e30, ALU.mult, ALU.max))
            dve.wait_ge(s_fg, 4)
            link(tts(hg(aF[0:G, :]), dts[0:G, 7, 0:H].unsqueeze(2).to_broadcast([G, H, G]),
                     M1[0:G, :].unsqueeze(1).to_broadcast([G, H, G]), ALU.mult))
            mark(F_AD, tts(hg(aB[0:G, :]), dts[0:G, 7, H:2 * H].unsqueeze(2).to_broadcast([G, H, G]),
                           M2[0:G, :].unsqueeze(1).to_broadcast([G, H, G]), ALU.mult))
            for r, cs in ((slice(0, P), slice(0, KC)), (slice(0, NS), slice(KC, 6))):
                link(ts(xg[r, cs, :], xg[r, cs, :], 1.0, None, ALU.add))
                link(dve.reciprocal(xg[r, cs, :], xg[r, cs, :]))
                link(tts(xa[r, cs, :], xa[r, cs, :], xg[r, cs, :], ALU.mult))
            link(dve.tensor_copy(Csh[0:NS, 1:G], xa[0:NS, 5, 0:G - 1]))
            mark(F_XA, dve.tensor_copy(Csh[0:NS, G:2 * G - 1], xa[0:NS, 5, 1:G]))
            dve.wait_ge(s_fp, 4)
            link(dve.tensor_copy(EF[0:G, :], tpf[1][0:G, :]))
            mark(F_SEG, dve.tensor_copy(EB[0:G, :], tpf[2][0:G, :]))
            dve.wait_ge(s_fp, 5)
            link(dve.tensor_copy(xt[0:G, :], pL[0:G, :]))
            link(dve.tensor_copy(CB[0:G, :], tpf[0][0:G, 64:64 + 2 * G]))
            link(tts(CB[0:G, 0:G], CB[0:G, 0:G], M1[0:G, :], ALU.mult))
            link(tts(CB[0:G, G:2 * G], CB[0:G, G:2 * G], M2[0:G, :], ALU.mult))
            dve.wait_ge(s_fa, 7)
            for k, Et in enumerate((EF, EB)):
                link(tts(hg(Et[0:G, :]), hg(Et[0:G, :]),
                         CB[0:G, k * G:(k + 1) * G].unsqueeze(1).to_broadcast([G, H, G]), ALU.mult))
                link(tts(hg(Et[0:G, :]), hg(Et[0:G, :]),
                         dts[0:G, 0, k * H:(k + 1) * H].unsqueeze(2).to_broadcast([G, H, G]), ALU.mult))
            mark(F_M, tts(EF[0:G, :], EF[0:G, :], EB[0:G, :], ALU.add))
            link(tts(yT, v3(pW[:, 0:KC * G]), Dc.unsqueeze(2).to_broadcast([P, KC, G]), ALU.add))
            link(tts(yT, yT, xa[:, 0:KC, :], ALU.mult))
            link(ts(sgz, sgz, 1.0, None, ALU.add))
            link(dve.reciprocal(sgz, sgz))
            link(tts(sgz, sgz, zT, ALU.mult))
            dve.wait_ge(s_fp, 6)
            link(tts(yT, yT, v3(acc[:, 0:KC * G]), ALU.add))
            link(tts(yT, yT, sgz, ALU.mult))
            mark(F_YQ, tts(yq, yT, yT, ALU.mult))
            dve.wait_ge(s_fp, 7)
            mark(F_RMS, ts(rms, tpf[1][:, 0:G], 1.0 / DI, 1e-5, ALU.mult, ALU.add))
            link(tts(yT, yT, nw.unsqueeze(2).to_broadcast([P, KC, G]), ALU.mult))
            dve.wait_ge(s_fg, 5)
            mark(F_YN, tts(yT, yT, rms.unsqueeze(1).to_broadcast([P, KC, G]), ALU.mult))
            dve.wait_ge(s_fp, 8)
            mark(F_OT, dve.tensor_copy(otT, v3(tpf[2][:, 0:KC * G])))
            dve.wait_ge(s_fp, 9)
            mark(F_MO, dve.tensor_copy(Mo[:, :, :], v3(pW[:, :], D)))

            dve.wait_ge(s_ob, 16)
            dve.sem_inc(s_fy2, 2)
            with dve.Fori(0, NSB // 2) as g:
                for b in range(2):
                    s = 2 * g + b
                    for a in range(1, TA, 2):
                        dve.wait_ge(s_fT, s * TA + a + 1)
                        dve.tensor_copy(swT[:, 1, :], tpf[1]).then_inc(s_fTd, 1)
                    dve.wait_ge(s_fl[b], 32 * g + 32)
                    tts(x1l[:, b, :, :], x1l[:, b, :, :], obB[:, :].unsqueeze(1).to_broadcast([P, TA, D]), ALU.add)\
                        .then_inc(s_x1b, 1)
                    dve.wait_ge(s_x1b, s + 1)
                    dve.wait_ge(s_fm, s + 1)
                    dve.wait_ge(s_out[b], 16 * g)
                    tts(yo[:, b, :, :], v3((pW, pL)[b][:, :], D), x1l[:, b, :, :], ALU.add).then_inc(s_fy, 1)
                    dve.wait_ge(s_fy, s + 1)
                    dve.sem_inc(s_fy2, 1)


_INS = ['x', 'adj', 'L0_gnn_W_gcn', 'L0_gnn_W_att', 'L0_gnn_a_att', 'L0_ffn_W_fx', 'L0_ffn_b_fx', 'L0_ffn_W_x',
        'L0_ffn_b_x', 'L0_ffn_W_slice', 'L0_ffn_b_slice', 'L0_ffn_temperature', 'L0_ffn_hy_in_w',
        'L0_ffn_hy_conv_w', 'L0_ffn_hy_conv_b', 'L0_ffn_hy_dt_bias', 'L0_ffn_hy_A_log', 'L0_ffn_hy_D',
        'L0_ffn_hy_fcD_w', 'L0_ffn_hy_norm_w', 'L0_ffn_hy_out_w', 'L0_ffn_out_w', 'L0_ffn_out_b']


def kernel(**inputs):
    import numpy as _np
    import concourse.bacc as _bacc
    from concourse import mybir as _mybir
    from concourse.bass_utils import run_bass_kernel_spmd as _run

    nc = _bacc.Bacc("TRN2", target_bir_lowering=False, num_devices=1)
    arrays, args = {}, []
    for name in _INS:
        a = _np.ascontiguousarray(inputs[name])
        arrays[f"in_{name}_dram"] = a
        args.append(nc.dram_tensor(f"in_{name}_dram", a.shape, _mybir.dt.from_np(a.dtype), kind="ExternalInput").ap())
    out = nc.dram_tensor("out_0_dram", inputs["x"].shape, _mybir.dt.float32, kind="ExternalOutput").ap()
    gnn_ffn(nc, *args, out)
    r = _run(nc, [arrays], core_ids=[0])
    return r.results[0]["out_0_dram"]
```

```python
from contextlib import ExitStack

import numpy as np

import concourse.bass as bass
from concourse import mybir

F32 = mybir.dt.float32
F32R = mybir.dt.float32r
BF16 = mybir.dt.bfloat16
I32 = mybir.dt.int32
ALU = mybir.AluOpType
ACT = mybir.ActivationFunctionType
AXX = mybir.AxisListType.X

P = 128
D = 128
TA = 4
ROWS = TA * P
STEP = 1024
GROUP = 2
MCOLS = 512
NMB = 4
MLEAD = 5
MHEAD = 3
NBUF = 4
NTP = 4
NAT = 4
LEAD = 3
MASKED = -9.0e15
EPS1 = float(np.float32(1.0 + 1e-7) - np.float32(1.0))
MIN_NORM = 1e-15
LN2 = float(np.log(2.0))
NXB = 8
EARLY = 3
SPREAD = 80.0

PRO_ACTS = [(10, 9, ACT.Exp, 1.0), (11, 9, ACT.Exp, -1.0)]
EPI_ROOTS = [(2, 0, 2, 0.5), (5, 4, 1, 0.5), (15, 14, 1, 0.5), (21, 20, 1, 0.5), (24, 23, 1, -0.5)]
LOGITS = (13, 16, 20, 23)
MAXIMA = (16, 19, 22, 25)
SUBTRACT = (15, 18, 21, 24)
EXPS = (19, 22, 25, 28)
SUMS = (20, 23, 26, 29)
WEIGHTS = (19, 22, 25, 28)
SLICES = (23, 26, 29, 31)
CHAIN_A = 36
CHAIN_B = 12
(F_UT, F_SILU, F_DTEXP, F_AD, F_ZEXP, F_XA, F_SEG, F_M, F_YQ, F_YN, F_OT, F_MO) = range(1, 13)
NFB = 4
NFW = 18


def fetch_shapes(adj, in_w, fc):
    return adj.shape[0], in_w.shape[0], fc.shape[0]


def gnn_ffn(nc, x, adj, W_gcn, W_att, a_att, W_fx, b_fx, W_x, b_x, W_slice, b_slice, temperature,
            in_w, conv_w, conv_b, dt_bias, A_log, hy_D, fcD_w, norm_w, hy_out_w, out_w, out_b, out):
    N, DIP, H = fetch_shapes(adj, in_w, fcD_w)
    NT = N // P
    NSB = N // ROWS
    NQ = N // STEP
    NG = NT // GROUP
    GPQ = STEP // (GROUP * P)
    MPQ = STEP // MCOLS
    GPM = GPQ // MPQ
    NM = NQ * MPQ
    G = W_slice.shape[0]
    HD = W_slice.shape[1]
    DI = H * HD
    KC = DI // P
    NS = (conv_w.shape[0] - DI) // 2
    assert G == 64 and HD == 64 and NS == 64 and D == P and KC == 4 and NQ % NBUF == 0

    x1_d = nc.dram_tensor("x1_scratch", [N, D], F32).ap()
    sw_d = nc.dram_tensor("slice_weights_scratch", [N, H * G], F32).ap()
    t_d = nc.dram_tensor("t_scratch", [N], F32).ap()

    ctx = ExitStack()
    with ctx:
        def sem(name):
            return ctx.enter_context(nc.semaphore(name))

        def sb(name, shape, dt=F32, c=None):
            return (c or ctx).enter_context(nc.sbuf_tensor(name, shape, dt))

        tp = [ctx.enter_context(nc.psum_tensor(f"tp{i}", [P, 1024], BF16)) for i in range(NTP)]
        tpf = [t[:, :].bitcast(F32) for t in tp]
        acc = ctx.enter_context(nc.psum_tensor("acc", [P, 512], F32))
        pW = ctx.enter_context(nc.psum_tensor("pW", [P, 512], F32))
        pS = tpf[3]
        pL = ctx.enter_context(nc.psum_tensor("pL", [P, 512], F32))
        pST = ctx.enter_context(nc.psum_tensor("pST", [P, 512], F32))

        identb = sb("identb", [P, P], BF16)
        identf = sb("identf", [P, P])
        ones = sb("ones", [P, P])
        Wg = sb("Wg", [P, P])
        WAe = sb("WAe", [P, P + 1])
        WA, e0 = WAe[:, 0:P], WAe[:, P:P + 1]
        Hs = sb("Hs", [P, P])
        WcH = sb("WcH", [P, H * G], F32R)
        WcL = sb("WcL", [P, H * G], F32R)
        bl = sb("bl", [P, H * G])
        zeros = sb("zeros", [P, P])
        swsum = sb("swsum", [P, H * G])
        beta = sb("beta", [P, NT])
        tt = sb("tt", [P, NT])
        tm = sb("tm", [P, 8])
        flag = sb("flag", [P, 1], I32)
        accS = sb("accS", [P, ROWS])
        STacc = accS
        xin = sb("xin", [P, TA, D])
        hp = sb("hp", [P, TA, D])
        ex = sb("ex", [P, TA, D])
        yy = sb("yy", [P, TA, D])
        x1 = sb("x1", [P, TA, D])
        x1n = sb("x1n", [P, TA, D])
        x1nH = sb("x1nH", [P, ROWS], F32R)
        x1nL = sb("x1nL", [P, ROWS], F32R)
        lg = sb("lg", [P, 2, H * G])
        es = sb("es", [P, 2, H * G])
        sw = sb("sw", [P, TA, H * G])
        r8 = sb("r8", [P, 2, 2, H])
        csum, pick, csb = x1[0:4, :, :].rearrange("p a d -> p (a d)"), ex[0:4, :, :], x1n[:, 0, :]
        c4 = sb("c4", [P, 32, TA])
        bst = sb("bst", [P, TA, 6])
        mv = sb("mv", [P, TA, 2])
        bits = sb("bits", [P, 2, TA], I32)
        expo = sb("expo", [P, 2, NT])

        n64 = sw[:, :, :].rearrange("p a b -> p (a b)")[:, 0:24 * NT].rearrange("p (k n) -> p k n", n=NT)
        obB = sb("obB", [P, D])
        over = ExitStack()
        AB = sb("mixer", [P, NBUF * TA * STEP], F32, over)
        over.close()
        adj0 = sb("adj0", [P, EARLY, TA * STEP], I32)
        over = ExitStack()
        V = sb("V", [P, NT, D], F32, over)
        over.close()
        adj1 = sb("adj1", [P, TA * STEP], I32)
        adjT = sb("adjT", [P, NAT, GROUP * ROWS], F32R)
        mask = sb("mask", [P, NMB, TA, MCOLS], BF16)
        adjb = [adj0[:, q, :] for q in range(EARLY)] + [adj1[:, :]]
        assert len(adjb) == NBUF
        SPLIT = list(range(NT // 2, NT)) + list(range(NT // 2))
        gs = ExitStack()
        ghi = sb("ghi", [P, NT, D], F32R, gs)
        glo = sb("glo", [P, NT, D], F32R, gs)
        gs.close()
        pro = ExitStack()
        xs = sb("xs", [P, NXB, TA, D], F32, pro)
        xT = sb("xT", [P, 4, ROWS], F32, pro)
        vq = sb("vq", [P, 2, TA, D], F32, pro)
        xst = sb("xst", [P, 2, TA, 6], F32, pro)
        xmv = sb("xmv", [P, NT, 2], F32, pro)
        xma = sb("xma", [P, 2, TA, 2], F32, pro)
        bits64 = sb("bits64", [P, 3, NT], I32, pro)
        centre = sb("centre", [P, P], F32, pro)
        Wgc = sb("Wgc", [P, P], F32, pro)
        Wx_n = sb("Wx_n", [HD, H, D], F32, pro)
        Wsl = sb("Wsl", [G, HD], F32, pro)
        WslT = sb("WslT", [HD, G], F32, pro)
        bxT = sb("bxT", [HD, H], F32, pro)
        bxB = sb("bxB", [HD, H, P], F32, pro)
        bsB = sb("bsB", [P, G], F32, pro)
        tmpB = sb("tmpB", [P, H], F32, pro)
        WAT = sb("WAT", [P, P], F32, pro)
        WgT = sb("WgT", [P, P], F32, pro)
        WAf = sb("WAf", [P, P], F32, pro)
        a2 = sb("a2", [P, 1], F32, pro)
        v2 = sb("v2", [P, 1], F32, pro)
        m2 = sb("m2", [2, 4], F32, pro)
        pro.close()
        gen = ExitStack()
        tb = sb("tb", [P, STEP], F32, gen)
        eb = sb("eb", [P, STEP], F32, gen)
        mb = sb("mb", [P, STEP], F32, gen)
        pT = sb("pT", [P, STEP], F32, gen)
        rm = sb("rm", [P, NQ + 2], F32, gen)
        gen.close()
        inw = sb("inw", [P, 10, DI])
        inT = sb("inT", [P, KC, DIP])
        cut = [0]

        def ab(w):
            a = cut[0]
            cut[0] += w
            assert cut[0] <= NBUF * TA * STEP
            return AB[:, a:a + w]

        ow = ab(KC * DI).rearrange("p (a b) -> p a b", a=KC)
        oT = ab(KC * DI).rearrange("p (a b) -> p a b", a=KC)
        wf = ab(KC * D).rearrange("p (a b) -> p a b", a=KC)
        wfT = ab(DI)
        wo = ab(DI)
        woT = ab(KC * D).rearrange("p (a b) -> p a b", a=KC)
        fc = ab(DI)
        fcT = ab(KC * DI).rearrange("p (a b) -> p a b", a=KC)
        z6 = lambda n, w=G: ab(n * w).rearrange("p (a b) -> p a b", a=n)
        uT = z6(KC)
        zT = z6(KC)
        xb = z6(6, G + 2)
        xa = z6(6)
        xg = z6(6)
        xt = ab(DI)
        cw = ab(18).rearrange("p (a b) -> p a b", a=6)
        cb = ab(6)
        bfx = ab(KC)
        Dc = ab(KC)
        nw = ab(KC)
        dtb = ab(2 * H)
        Ae = ab(2 * H)
        dts = ab(12 * 2 * H).rearrange("p (a b) -> p a b", a=12)
        M1 = ab(G)
        M2 = ab(G)
        SN = z6(KC)
        rS = z6(KC)
        aF = ab(H * G)
        aB = ab(H * G)
        EF = ab(H * G)
        EB = ab(H * G)
        Csh = ab(2 * G)
        CB = ab(2 * G)
        sgz = z6(KC)
        yT = z6(KC)
        yq = z6(KC)
        rms = ab(G)
        rsq = ab(G)
        rst = ab(G)
        rsb = ab(G).bitcast(I32)
        otT = z6(KC)
        Mo = sb("Mo", [P, KC, D])
        swl0 = sb("swl", [P, 2, TA, H * G])
        inTf = inT[:, :, :].rearrange("p a b -> p (a b)")
        swl = [swl0[:, 0, :, :], swl0[:, 1, :, :]] + [inTf[:, b * TA * DI:(b + 1) * TA * DI]
                                                      .rearrange("p (a b) -> p a b", a=TA) for b in range(2)]
        x1l = [hp[:, :, :], yy[:, :, :], x1n[:, :, :], ex[:, :, :]]
        swT = inw[:, 0:TA, :]
        yo = lg[:, :, :].rearrange("p b (a d) -> p b a d", a=TA)

        s_wg = sem("attention_weights_loaded")
        s_w = sem("weights_loaded")
        s_id = sem("idents_made")
        s_one = sem("ones_made")
        s_wz = sem("weights_zeroed")
        s_tr = sem("weight_transposed")
        s_trc = sem("weight_copied")
        s_xs = [sem(f"x_loaded{b}") for b in range(NXB)]
        s_xfree = sem("x_statistics_done")
        s_xx = sem("x_first_column_copied")
        s_xag = sem("x_statistics_merged")
        s_xmv = sem("x_statistics_copied")
        s_ctr = sem("centre_made")
        s_wp = sem("scaled_weights_ready")
        s_beta = sem("beta_ready")
        s_pT = sem("x_transposed")
        s_pTc = sem("x_transposed_copied")
        s_V = sem("V_product")
        s_Vc = sem("V_copied")
        s_Vq = sem("V_squared")
        s_ssv = sem("V_sums_done")
        s_pa = sem("acts_asked")
        s_pd = sem("acts_done")
        s_mx = sem("extrema_ready")
        s_mxT = sem("extrema_transposed")
        s_m2 = sem("extrema_reduced")
        s_mb = sem("extrema_spread")
        s_flag = sem("flag_ready")
        s_cs = sem("column_sums")
        s_csc = sem("column_sums_copied")
        s_cs2 = sem("column_sums_merged")
        s_csb = sem("column_sums_spread")
        s_hs = sem("mean_product")
        s_hsc = sem("Hs_ready")
        s_wexp = sem("w_ready")
        s_gh = sem("ghi_ready")
        s_gl = sem("glo_ready")
        ch = sem("dve_chain")
        che = sem("dve_first_chain")
        che2 = sem("dve_second_chain")
        chf = sem("dve_mixer_chain")
        chg = sem("dve_general_chain")
        s_adj = [sem(f"adj_loaded{b}") for b in range(NBUF)]
        s_mask = sem("mask_made")
        s_tp = sem("group_transposed")
        s_ev = sem("group_evacuated")
        s_mm = sem("group_multiplied")
        s_acc = sem("acc_done")
        s_accS = sem("acc_copied")
        s_xin = sem("xin_loaded")
        s_agg = sem("agg_done")
        s_hp = sem("hp_ready")
        s_ex = sem("exp_hp")
        s_den = sem("denominators_copied")
        s_rd = sem("row_scales_ready")
        s_hps = sem("means_scaled")
        s_re = sem("relu_ready")
        s_y = sem("elu_ready")
        s_sy = sem("elu_squares_summed")
        s_x0 = sem("one_added")
        s_lf = sem("log_factor_ready")
        s_th = sem("tanh_ready")
        s_ss = sem("sigmoid_squares_summed")
        s_kr = sem("sinh_factor_ready")
        s_sv = sem("sinh_applied")
        s_lb = sem("logits_bank_read")
        s_lx = sem("logits_maximum")
        s_rs = sem("logits_sum_inverted")
        s_rq1 = sem("first_root_asked")
        s_rq2 = sem("second_roots_asked")
        s_rt = sem("first_roots")
        s_rt2 = sem("second_roots")
        s_nn = sem("norm_ready")
        s_sh = sem("sinh_exps")
        s_x1 = sem("x1_ready")
        s_x1n = sem("x1n_ready")
        s_x1T = sem("x1n_transposed")
        s_x1Tc = sem("x1nH_copied")
        s_x1L = sem("x1nL_ready")
        s_lg = sem("logits_product")
        s_lm = sem("logits_shifted")
        s_es = sem("logits_exp")
        s_sw = sem("sw_ready")
        s_sws = sem("swsum_added")
        s_st = sem("st_product")
        s_zero = sem("zeroes_made")
        s_std = sem("st_copied")
        s_x1o = sem("x1_stored")
        s_swo = sem("sw_stored")
        sp_tick = sem("sp_tick")
        pool_tick = sem("pool_tick")
        dve_tick = sem("dve_tick")
        s_out = [sem(f"out_stored{b}") for b in range(2)]
        s_tst = sem("t_stored")
        s_tout = sem("t_written")
        s_gt = sem("general_t_loaded")
        s_ga = sem("general_adj_loaded")
        s_gh2 = sem("h_in_ready")
        s_gm = sem("general_chunk_used")
        s_ge = sem("general_logits")
        s_gp = sem("general_probabilities")
        s_gT = sem("general_transposed")
        s_gTc = sem("general_transposed_copied")
        s_fw = sem("mixer_weights_loaded")
        s_ft = sem("mixer_transposed")
        s_ftc = sem("mixer_transposed_copied")
        s_fp = sem("mixer_product")
        s_fd = sem("mixer_dve")
        s_fa = sem("mixer_act")
        s_fg = sem("mixer_pool")
        s_fl = [sem(f"final_loaded{b}") for b in range(NFB)]
        s_fT = sem("sw_transposed")
        s_fTc = sem("sw_transposed_copied")
        s_fm = sem("final_product")
        s_fy = sem("final_sum")
        s_ob = sem("out_b_loaded")
        s_fTd = sem("sw_transposed_copied_by_dve")
        s_fy2 = sem("final_bank_free")
        s_x1b = sem("x1_with_out_b")
        s_gw = sem("V_scaled")
        chm = sem("dve_row_maximum_chain")

        def turned():
            for k in range(KC):
                for a0, a1 in ((0, 4), (4, 8), (8, 10)):
                    blocks = [(inw[0:min(P, DIP - a * P), a, k * P:(k + 1) * P], min(P, DIP - a * P))
                              for a in range(a0, a1)]
                    w = sum(n for _, n in blocks)
                    yield blocks, [(inT[:, k, a0 * P:a0 * P + w], lambda bank, w=w: bank[:, 0:w])]
            for k in range(KC):
                yield [(ow[:, a, k * P:(k + 1) * P], P) for a in range(KC)], [(oT[:, k, :], lambda bank: bank)]
            yield [(wf[:, a, :], P) for a in range(KC)], [(wfT, lambda bank: bank)]
            yield [(wo[:, k * P:(k + 1) * P], P) for k in range(KC)], \
                [(woT.rearrange("p a b -> p (a b)"), lambda bank: bank)]
            yield [(fc[0:H, k * P:(k + 1) * P], H) for k in range(KC)], \
                [(fcT[:, k, :].rearrange("p (h c) -> p h c", h=H),
                  lambda bank, k=k: bank[:, k * P:k * P + H].unsqueeze(2).to_broadcast([P, H, HD]))
                 for k in range(KC)]
        TURNED = list(turned())

        def turned_at(n):
            return range(len(TURNED))[max(0, 2 * (n - 5)):max(0, 2 * (n - 4))]

        block = ctx.enter_context(nc.Block())

        x_v = x.rearrange("(s a p) d -> s p a d", a=TA, p=P)
        adj_v = adj.rearrange("(s a p) (q j) -> s q p a j", a=TA, p=P, j=STEP)
        x1_v = x1_d.rearrange("(s a p) d -> s p a d", a=TA, p=P)
        sw_v = sw_d.rearrange("(s a p) g -> s p a g", a=TA, p=P)
        out_v = out.rearrange("(s a p) d -> s p a d", a=TA, p=P)

        def wait(eng, s, v):
            if not isinstance(v, int) or v > 0:
                eng.wait_ge(s, v)

        hg = lambda ap: ap.rearrange("p (h g) -> p h g", h=H)

        def mean_of(a, w):
            return pL[:, 0:w] if a == TA - 1 else pW[:, a * (P + 1):a * (P + 1) + w]

        @block.sync
        def _(sp):
            def wait_sp(s, v):
                wait(sp, s, v)
                if not isinstance(v, int):
                    sp.sem_inc(sp_tick, 1)

            with nc.allow_non_contiguous_dma(reason="small weights"):
                sp.wait_ge(s_wz, 4)
                sp.dma_start(Wg[1:P, 1:P], W_gcn).then_inc(s_wg, 16)
                sp.dma_start(WAf[:, :], W_att).then_inc(s_wg, 16)
                sp.dma_start(a2[:, :], a_att[P:2 * P, :]).then_inc(s_wg, 16)
                for b in range(NXB):
                    sp.dma_start(xs[:, b, :, :], x_v[b, :, :, :]).then_inc(s_xs[b], 16)
                sp.dma_start(WA[1:P, :], W_att[1:P, :]).then_inc(s_w, 16)
                sp.dma_start(Wx_n[:, :, :], W_x.rearrange("(h q) d -> q h d", q=HD)).then_inc(s_w, 16)
                sp.dma_start(Wsl[:, :], W_slice).then_inc(s_w, 16)
                sp.dma_start(bxT[:, :], b_x.rearrange("(h q) -> q h", q=HD)).then_inc(s_w, 16)
                sp.dma_start(bsB[:, :], b_slice.rearrange("(a g) -> a g", a=1).to_broadcast([P, G]))\
                    .then_inc(s_w, 16)
                sp.dma_start(tmpB[:, :], temperature.rearrange("a h b c -> a (h b c)").to_broadcast([P, H]))\
                    .then_inc(s_w, 16)
                sp.dma_start(obB[:, :], out_b.rearrange("(a d) -> a d", a=1).to_broadcast([P, D]))\
                    .then_inc(s_ob, 16)
            with sp.Fori(1, NSB // NXB) as g:
                for b in range(NXB):
                    k = NXB * g + b
                    wait_sp(s_xfree, k - NXB + 1)
                    wait_sp(s_pT, k - NXB + 1)
                    wait_sp(s_xx, k - NXB + 1)
                    sp.dma_start(xs[:, b, :, :], x_v[k, :, :, :]).then_inc(s_xs[b], 16)

            def load_adj(s, q):
                if not (isinstance(s, int) and s == 0 and q < NBUF):
                    wait_sp(s_mask, (NQ * s + q - NBUF + 1) * MPQ)
                elif q >= EARLY:
                    sp.wait_ge(s_cs, NT // 4)
                    sp.wait_ge(s_gl, 1 + NT)
                sp.dma_start(adjb[q % NBUF].rearrange("p (a j) -> p a j", a=TA),
                             adj_v[s, q, :, :, :]).then_inc(s_adj[q % NBUF], 16)

            for q in range(EARLY):
                load_adj(0, q)
            sp.wait_ge(s_flag, 1)
            one_shift = sp.value_load(flag[0:1, 0:1])
            with sp.If(one_shift > 0):
                for q in range(EARLY, NQ):
                    load_adj(0, q)
                with sp.Fori(1, NSB) as s:
                    for q in range(NQ):
                        load_adj(s, q)
                sp.wait_ge(s_mask, NM * NSB)
                sp.wait_ge(s_mm, NG * NSB)
            with sp.Else():
                sp.wait_ge(s_tst, 1)
                sp.wait_ge(s_mask, NMB)
                sp.wait_ge(s_adj[EARLY - 1], 16)
                with nc.allow_non_contiguous_dma(reason="one value per row"):
                    sp.dma_start(t_d.rearrange("(c p) -> p c", p=P), tt[:, :]).then_inc(s_tout, 16)
                sp.wait_ge(s_tout, 16)
                with sp.Fori(0, NSB) as s:
                    for a in range(TA):
                        for c in range(2 * NQ):
                            wait_sp(s_gm, (s * TA + a) * 2 * NQ + c)
                            sp.dma_start(adjb[0][:, 0:STEP], adj_v[s, c % NQ, :, a, :]).then_inc(s_ga, 16)
                            sp.dma_start(tb[:, :], t_d[c % NQ * STEP:(c % NQ + 1) * STEP]
                                         .rearrange("(a j) -> a j", a=1).to_broadcast([P, STEP]))\
                                .then_inc(s_gt, 16)
                sp.wait_ge(s_acc, NSB)
            with nc.allow_non_contiguous_dma(reason="small weights"):
                sp.dma_start(inw[:, 0:9, :], in_w[0:9 * P, :].rearrange("(a p) k -> p a k", p=P)).then_inc(s_fw, 16)
                sp.dma_start(inw[0:DIP - 9 * P, 9, :], in_w[9 * P:DIP, :]).then_inc(s_fw, 16)
                sp.dma_start(ow, hy_out_w.rearrange("(a p) k -> p a k", p=P)).then_inc(s_fw, 16)
                sp.dma_start(wf, W_fx.rearrange("(a p) k -> p a k", p=P)).then_inc(s_fw, 16)
                sp.dma_start(wo, out_w).then_inc(s_fw, 16)
                sp.dma_start(fc[0:H, :], fcD_w).then_inc(s_fw, 16)
                sp.dma_start(cw[:, 0:KC, :], conv_w[0:DI, :].rearrange("(a p) k -> p a k", p=P)).then_inc(s_fw, 16)
                sp.dma_start(cw[0:NS, KC:6, :], conv_w[DI:, :].rearrange("(a p) k -> p a k", p=NS)).then_inc(s_fw, 16)
                sp.dma_start(cb[:, 0:KC], conv_b[0:DI].rearrange("(a p) -> p a", p=P)).then_inc(s_fw, 16)
                sp.dma_start(cb[0:NS, KC:6], conv_b[DI:].rearrange("(a p) -> p a", p=NS)).then_inc(s_fw, 16)
                sp.dma_start(bfx, b_fx.rearrange("(a p) -> p a", p=P)).then_inc(s_fw, 16)
                sp.dma_start(nw, norm_w.rearrange("(a p) -> p a", p=P)).then_inc(s_fw, 16)
                for half in range(2):
                    sp.dma_start(Dc[half * 64:half * 64 + 64, :],
                                 hy_D.rearrange("(c t) -> t c", t=2)[half:half + 1, :].to_broadcast([64, KC]))\
                        .then_inc(s_fw, 16)
                    sp.dma_start(dtb[0:G, half * H:half * H + H],
                                 dt_bias.rearrange("(a h) -> a h", a=1).to_broadcast([G, H])).then_inc(s_fw, 16)
                    sp.dma_start(Ae[0:G, half * H:half * H + H],
                                 A_log.rearrange("(a h) -> a h", a=1).to_broadcast([G, H])).then_inc(s_fw, 16)

            def load_final(s, b):
                sp.dma_start(swl[b], sw_v[s, :, :, :]).then_inc(s_fl[b], 16)
                sp.dma_start(x1l[b], x1_v[s, :, :, :]).then_inc(s_fl[b], 16)

            def store_final(s, b):
                wait_sp(s_fy, s + 1)
                sp.dma_start(out_v[s, :, :, :], yo[:, b % 2, :, :]).then_inc(s_out[b % 2], 16)

            sp.wait_ge(s_x1o, 16 * NSB)
            sp.wait_ge(s_swo, 16 * NSB)
            for b in range(NFB):
                if b == 2:
                    sp.wait_ge(s_fp, 5)
                load_final(b, b)
            with sp.Fori(0, NSB // NFB - 1) as g:
                for b in range(NFB):
                    store_final(NFB * g + b, b)
                    load_final(NFB * g + b + NFB, b)
            for b in range(NFB):
                store_final(NSB - NFB + b, b)
            for b in range(2):
                sp.wait_ge(s_out[b], 16 * (NSB // 2))

        @block.gpsimd
        def _(pool):
            def wait_pool(s, v):
                wait(pool, s, v)
                if not isinstance(v, int):
                    pool.sem_inc(pool_tick, 1)

            pool.memset(Wg[:, :], 0.0).then_inc(s_wz, 1)
            pool.memset(WA[:, :], 0.0).then_inc(s_wz, 1)
            pool.memset(e0[:, :], 0.0).then_inc(s_wz, 1)
            pool.wait_ge(s_wz, 3)
            pool.memset(e0[0:1, :], 1.0).then_inc(s_wz, 1)
            pool.memset(ones[:, :], 1.0).then_inc(s_one, 1)
            pool.memset(swsum[:, :], 0.0).then_inc(s_one, 1)
            pool.memset(identf[:, :], 0.0).then_inc(s_id, 1)
            pool.memset(identb[:, :], 0.0).then_inc(s_id, 1)
            pool.wait_ge(s_id, 2)
            for m in (identf, identb):
                pool.affine_select(out=m[:, :], in_=m[:, :], compare_op=ALU.not_equal, fill=1.0, base=0,
                                   pattern=[[-1, P]], channel_multiplier=1).then_inc(s_id, 1)

            pool.memset(expo[:, 0, :], 0.5).then_inc(s_one, 1)
            pool.memset(expo[:, 1, :], -0.5).then_inc(s_one, 1)
            pool.wait_ge(s_one, 4)

            def root(out_ap, in_ap, power, asked, n, done):
                wait_pool(asked, n)
                w = expo[:, 0 if power > 0 else 1, 0:int(np.prod(in_ap.shape[1:]))]
                if len(in_ap.shape) == 3:
                    w = w.rearrange("p (a b) -> p a b", a=in_ap.shape[1])
                pool.tensor_tensor(out_ap, in_ap, w, ALU.pow).then_inc(done, 1)

            with pool.Fori(0, NSB // NXB) as g:
                for b in range(NXB):
                    k = NXB * g + b
                    col = bass.ds(TA * k, TA)
                    wait_pool(s_xs[b], 16 * g + 16)
                    pool.tensor_copy(n64[:, 1, col], xs[:, b, :, 0]).then_inc(s_xx, 1)
                    wait_pool(s_xag, k + 1)
                    pool.tensor_copy(xmv[:, col, :], xma[:, b % 2, :, :]).then_inc(s_xmv, 1)

            def roots(e, k):
                o, i, n, power = EPI_ROOTS[k]
                if k == 0:
                    wait_pool(s_sy, e + 1)
                    pool.tensor_scalar(c4[:, 1, :], c4[:, 0, :], 1.0, None, ALU.add).then_inc(s_x0, 1)
                    root(c4[:, o:o + n, :], c4[:, i:i + n, :], power, s_x0, e + 1, s_rt)
                elif k == 2:
                    root(c4[:, o:o + n, :], c4[:, i:i + n, :], power, s_ss, e + 1, s_rt)
                else:
                    root(c4[:, o:o + n, :], c4[:, i:i + n, :], power, *((s_rq1, e + 1, s_rt) if k == 1 else
                                                                        (s_rq2, 2 * e + k - 2, s_rt2)))

            def subtract_maximum(e, a):
                wait_pool(s_lx, TA * e + a + 1)
                pool.tensor_tensor(hg(lg[:, a % 2, :]), hg(lg[:, a % 2, :]),
                                   r8[:, a % 2, 0, :].unsqueeze(2).to_broadcast([P, H, G]),
                                   ALU.subtract).then_inc(s_lm, 1)

            def slice_weights(e, a):
                if a == 0:
                    wait_pool(s_swo, 16 * e)
                    wait_pool(s_st, e)
                wait_pool(s_rs, TA * e + a + 1)
                pool.tensor_tensor(hg(sw[:, a, :]), hg(es[:, a % 2, :]),
                                   r8[:, a % 2, 1, :].unsqueeze(2).to_broadcast([P, H, G]),
                                   ALU.mult).then_inc(s_sw, 1)
                wait_pool(s_sw, TA * e + a + 1)
                wait_pool(s_sws, TA * e + a)
                pool.tensor_tensor(swsum[:, :], swsum[:, :], sw[:, a, :], ALU.add).then_inc(s_sws, 1)

            def first(e, n):
                if n in (13, 17, 23):
                    roots(e, (13, 17, 23).index(n))

            def second(e, n):
                if n in (0, 3):
                    roots(e, 3 + (0, 3).index(n))
                if n in SUBTRACT:
                    subtract_maximum(e, SUBTRACT.index(n))
                if n in WEIGHTS:
                    slice_weights(e, WEIGHTS.index(n))

            pool.wait_ge(s_flag, 1)
            one_shift = pool.value_load(flag[0:1, 0:1])
            with pool.If(one_shift > 0):
                for n in range(NG):
                    first(0, n)
                with pool.Fori(1, NSB) as e:
                    for n in range(NG):
                        second(e - 1, n)
                        first(e, n)
                for n in range(NG):
                    second(NSB - 1, n)
            with pool.Else():
                with pool.Fori(0, NSB) as e:
                    for n in range(NG):
                        first(e, n)
                    for n in range(NG):
                        second(e, n)
            pool.wait_ge(s_st, NSB + 1)
            pool.memset(M1[0:G, :], 1.0).then_inc(s_fg, 1)
            pool.memset(M2[0:G, :], 1.0).then_inc(s_fg, 1)
            pool.wait_ge(s_fg, 2)
            pool.affine_select(out=M1[0:G, :], in_=M1[0:G, :], compare_op=ALU.is_gt, fill=0.0, base=0,
                               pattern=[[1, G]], channel_multiplier=-1).then_inc(s_fg, 1)
            pool.affine_select(out=M2[0:G, :], in_=M2[0:G, :], compare_op=ALU.is_gt, fill=0.0, base=0,
                               pattern=[[-1, G]], channel_multiplier=1).then_inc(s_fg, 1)

        @block.scalar
        def _(act):
            act.sem_inc(s_Vq, 2)

            def copy_xT(g, b0):
                for b in (b0, b0 + 1):
                    act.wait_ge(s_pT, NXB * g + b + 1)
                    act.activation(xT[:, b % 4, :], tpf[b % 4], ACT.Copy).then_inc(s_pTc, 1)

            def copy_V(g, b0):
                for b in (b0, b0 + 1):
                    k = NXB * g + b
                    act.wait_ge(s_V, k + 1)
                    pv = (pW, pL)[b % 2]
                    act.activation(V[:, bass.ds(TA * k, TA), :].rearrange("p a d -> p (a d)"), pv[:, :],
                                   ACT.Copy).then_inc(s_Vc, 1)
                    act.wait_ge(s_ssv, k + 1)
                    act.activation(vq[:, b % 2, :, :].rearrange("p a d -> p (a d)"), pv[:, :], ACT.Square)\
                        .then_inc(s_Vq, 1)

            copy_xT(0, 0)
            with act.Fori(0, NSB // NXB - 1) as g:
                for b0 in range(0, NXB, 2):
                    copy_xT(*((g, b0 + 2) if b0 + 2 < NXB else (g + 1, 0)))
                    copy_V(g, b0)
            for b0 in range(0, NXB, 2):
                if b0 + 2 < NXB:
                    copy_xT(NSB // NXB - 1, b0 + 2)
                copy_V(NSB // NXB - 1, b0)
            for k, (o, i, f, sc) in enumerate(PRO_ACTS):
                act.wait_ge(s_pa, 1)
                act.activation(n64[:, o, :], n64[:, i, :], f, scale=sc).then_inc(s_pd, 1)
            act.wait_ge(s_flag, 1)

            def copy_acc(e, general):
                act.wait_ge(*((s_acc, e + 1) if general else (s_mm, NG * e + NG)))
                act.activation(accS[:, :], acc[:, :], ACT.Copy).then_inc(s_accS, 1)

            def load_x(e):
                wait(act, s_x1, e)
                act.dma_start(xin[:, :, :], x_v[e, :, :, :]).then_inc(s_xin, 16)

            def scale_means(e):
                act.wait_ge(s_rd, e + 1)
                for a in range(TA):
                    last = act.activation(hp[:, a, :], mean_of(a, P), ACT.Copy, scale=c4[:, 2, a:a + 1])
                last.then_inc(s_hps, 1)

            def elu_parts(e):
                act.wait_ge(s_hp, e + 1)
                act.activation(yy[:, :, :], hp[:, :, :], ACT.Relu).then_inc(s_re, 1)
                act.activation(ex[:, :, :], ex[:, :, :], ACT.Exp).then_inc(s_ex, 1)

            def square_elu(e):
                act.wait_ge(s_y, e + 1)
                for a in range(TA):
                    last = act.activation(ex[:, a, 1:D], yy[:, a, 1:D], ACT.Square, accum_out=c4[:, 0, a:a + 1])
                last.then_inc(s_sy, 1)

            def sigmoid(e):
                act.wait_ge(s_lf, e + 1)
                for a in range(TA):
                    last = act.activation(ex[:, a, :], yy[:, a, :], ACT.Tanh, scale=c4[:, 9, a:a + 1])
                last.then_inc(s_th, 1)
                act.wait_ge(s_th, e + 1)
                for a in range(TA):
                    last = act.activation(hp[:, a, 1:D], ex[:, a, 1:D], ACT.Square, scale=0.5, bias=expo[:, 0, 0:1],
                                          accum_out=c4[:, 14, a:a + 1])
                last.then_inc(s_ss, 1)

            def exp_norm(e):
                act.wait_ge(s_nn, e + 1)
                act.activation(c4[:, 16, :], c4[:, 15, :], ACT.Exp).then_inc(s_sh, 1)
                act.activation(c4[:, 17, :], c4[:, 15, :], ACT.Exp, scale=-1.0).then_inc(s_sh, 1)

            def apply_sinh(e):
                act.wait_ge(s_kr, e + 1)
                for a in range(TA):
                    last = act.activation(hp[:, a, :], ex[:, a, :], ACT.Identity, scale=c4[:, 25, a:a + 1],
                                          bias=c4[:, 25, a:a + 1])
                last.then_inc(s_sv, 1)

            def copy_x1nH(e):
                act.wait_ge(s_x1T, e + 1)
                act.activation(x1nH[:, :], pW[:, :], ACT.Copy).then_inc(s_x1Tc, 1)

            def exp_logits(e, a):
                act.wait_ge(s_lm, TA * e + a + 1)
                wait(act, s_sw, TA * e + max(a - 1, 0))
                act.activation(es[:, a % 2, :], lg[:, a % 2, :], ACT.Exp).then_inc(s_es, 1)

            def store_x1(e):
                act.wait_ge(s_x1, e + 1)
                act.dma_start(x1_v[e, :, :, :], x1[:, :, :]).then_inc(s_x1o, 16)

            def store_sw(e):
                act.wait_ge(s_sw, TA * e + TA)
                act.dma_start(sw_v[e, :, :, :], sw[:, :, :]).then_inc(s_swo, 16)

            def first(e, n, general=False):
                if n == LEAD:
                    copy_acc(e, general)
                if n == 7:
                    scale_means(e)
                if n == 9:
                    load_x(e)
                if n == 11:
                    elu_parts(e)
                if n == 15:
                    square_elu(e)
                if n == 24:
                    sigmoid(e)
                if n == 28:
                    exp_norm(e)

            def second(e, n):
                if n == 4:
                    apply_sinh(e)
                if n == 8:
                    store_x1(e)
                if n == 12:
                    copy_x1nH(e)
                if n in EXPS:
                    exp_logits(e, EXPS.index(n))

            def copy_turned(k):
                act.wait_ge(s_ft, k + 1)
                for d, src in TURNED[k][1]:
                    last = act.activation(d, src(tpf[k % 3]), ACT.Copy)
                last.then_inc(s_ftc, 1)

            def evacuate(s, n):
                k = NG * s + n
                act.wait_ge(s_tp, k + 1)
                if not (isinstance(s, int) and k < NAT):
                    act.wait_ge(s_mm, k - NAT + 1)
                act.activation(adjT[:, n % NAT, :], tp[n % NTP][:, :], ACT.Copy).then_inc(s_ev, 1)

            one_shift = act.value_load(flag[0:1, 0:1])
            with act.If(one_shift > 0):
                act.activation(n64[:, 23, :], tt[:, :], ACT.Exp, bias=tm[:, 3:4]).then_inc(s_wexp, 1)
                act.wait_ge(s_wexp, 1)
                act.activation(ghi[:, :, 0], n64[:, 23, :], ACT.Copy).then_inc(s_gh, 1)
                act.wait_ge(s_wp, 1)
                def split(c):
                    act.activation(ghi[:, c, 1:D], V[:, c, 1:D], ACT.Copy, scale=n64[:, 22, c:c + 1]).then_inc(s_gh, 1)

                for c in SPLIT[:NT // 2]:
                    split(c)
                act.wait_ge(s_cs, NT // 8)
                act.wait_ge(s_gl, 1 + NT // 2)
                for n in range(NG):
                    for c in SPLIT[NT // 2:][4 * n:4 * n + 4]:
                        split(c)
                    evacuate(0, n)
                for n in range(NG):
                    first(0, n)
                    evacuate(1, n)
                with act.Fori(2, NSB) as s:
                    for n in range(NG):
                        second(s - 2, n)
                        first(s - 1, n)
                        evacuate(s, n)
                    store_sw(s - 2)
                for n in range(NG):
                    second(NSB - 2, n)
                    first(NSB - 1, n)
                store_sw(NSB - 2)
                for n in range(NG):
                    second(NSB - 1, n)
                    for k in turned_at(n):
                        copy_turned(k)
                store_sw(NSB - 1)
            with act.Else():
                with act.Fori(0, NSB) as s:
                    for a in range(TA):
                        for c in range(NQ):
                            k = (s * TA + a) * NQ + c
                            act.wait_ge(s_ge, k + 1)
                            act.activation(eb[:, :], eb[:, :], ACT.Exp, bias=rm[:, NQ + 1:NQ + 2])\
                                .then_inc(s_gp, 1)
                            act.wait_ge(s_gT, k + 1)
                            act.activation(pT[:, 0:512], pW[:, :], ACT.Copy).then_inc(s_gTc, 1)
                            act.activation(pT[:, 512:1024], pL[:, :], ACT.Copy).then_inc(s_gTc, 1)
                    for n in range(NG):
                        first(s, n, general=True)
                    for n in range(NG):
                        second(s, n)
                    store_sw(s)
                for k in range(len(TURNED)):
                    copy_turned(k)


            def fa(need, *args, **kw):
                act.wait_ge(s_fd, need)
                act.activation(*args, **kw).then_inc(s_fa, 1)
            act.wait_ge(s_fw, 16 * NFW)
            act.activation(Ae[0:G, :], Ae[0:G, :], ACT.Exp).then_inc(s_fa, 1)
            fa(F_SILU, xg[:, 0:KC, :], xa[:, 0:KC, :], ACT.Exp, scale=-1.0)
            act.activation(xg[0:NS, KC:6, :], xa[0:NS, KC:6, :], ACT.Exp, scale=-1.0).then_inc(s_fa, 1)
            fa(F_DTEXP, dts[0:G, 2, :], dts[0:G, 1, :], ACT.Exp)
            fa(F_ZEXP, sgz, zT, ACT.Exp, scale=-1.0)
            fa(F_SEG, EF[0:G, :], EF[0:G, :], ACT.Exp)
            act.activation(EB[0:G, :], EB[0:G, :], ACT.Exp).then_inc(s_fa, 1)
            with act.Fori(0, NSB // NFB) as g:
                for b in range(NFB):
                    for a in range(0, TA, 2):
                        act.wait_ge(s_fT, (NFB * g + b) * TA + a + 1)
                        act.activation(swT[:, a, :], tpf[a], ACT.Copy).then_inc(s_fTc, 1)

        @block.tensor
        def _(pe):
            def mm(out_ap, lhsT, rhs, start=True, stop=True):
                return pe.matmul(out_ap, lhsT, rhs, start=start, stop=stop)

            pe.wait_ge(s_id, 4)
            pe.wait_ge(s_one, 2)
            pe.wait_ge(s_wg, 16 * 3)
            pe.transpose(pW[:, 0:P], WAf[:, :], identf[:, :]).then_inc(s_tr, 1)
            pe.transpose(pL[:, 0:P], Wg[:, :], identf[:, :]).then_inc(s_tr, 1)
            pe.wait_ge(s_trc, 1)
            mm(pST[:, 0:1], WAT[:, :], a2[:, :]).then_inc(s_tr, 1)
            pe.wait_ge(s_trc, 3)
            mm(pST[:, 2:3], WgT[:, :], v2[:, :]).then_inc(s_tr, 1)
            pe.wait_ge(s_trc, 4)
            pe.wait_ge(s_ctr, 1)
            mm(pST[:, 128:256], centre[:, :], Wg[:, :]).then_inc(s_tr, 1)
            pe.wait_ge(s_trc, 5)
            def turn_x(g, b0):
                for b in (b0, b0 + 1):
                    pe.wait_ge(s_xs[b], 16 * g + 16)
                    for a in range(TA):
                        last = pe.transpose(tpf[b % 4][:, a * P:(a + 1) * P], xs[:, b, a, :], identf[:, :])
                    last.then_inc(s_pT, 1)

            def times_weight(g, b0):
                for b in (b0, b0 + 1):
                    k = NXB * g + b
                    pe.wait_ge(s_pTc, k + 1)
                    pe.wait_ge(s_Vq, k + 1)
                    for a in range(TA):
                        last = mm((pW, pL)[b % 2][:, a * P:(a + 1) * P], xT[:, b % 4, a * P:(a + 1) * P], Wgc[:, :])
                    last.then_inc(s_V, 1)

            turn_x(0, 0)
            with pe.Fori(0, NSB // NXB - 1) as g:
                for b0 in range(0, NXB, 2):
                    turn_x(*((g, b0 + 2) if b0 + 2 < NXB else (g + 1, 0)))
                    times_weight(g, b0)
            for b0 in range(0, NXB, 2):
                if b0 + 2 < NXB:
                    turn_x(NSB // NXB - 1, b0 + 2)
                times_weight(NSB // NXB - 1, b0)
            pe.wait_ge(s_w, 16 * 6)
            pe.wait_ge(s_Vq, NSB + 2)
            pe.transpose(pS[0:HD, 0:G], Wsl[:, :], identf[0:G, 0:G]).then_inc(s_tr, 1)
            pe.wait_ge(s_trc, 7)
            for h in range(H):
                last = mm(acc[:, h * G:(h + 1) * G], Wx_n[:, h, :], WslT[:, :])
            last.then_inc(s_tr, 1)
            for h in range(H):
                last = mm(pS[:, h * G:(h + 1) * G], bxB[:, h, :], WslT[:, :])
            last.then_inc(s_tr, 1)
            pe.wait_ge(s_mx, 1)
            pe.transpose(pST[0:2, 0:P], tm[:, 0:2], identf[:, :]).then_inc(s_mxT, 1)
            pe.wait_ge(s_m2, 1)
            mm(pST[:, 256:258], ones[0:2, :], m2[:, 2:4]).then_inc(s_mb, 1)
            def sum_v(c):
                pe.wait_ge(s_beta, 1)
                k = SPLIT[4 * c]
                mm(pL[0:4, :], beta[:, k:k + 4], V[:, k:k + 4, :].rearrange("p a d -> p (a d)"),
                   start=c == 0, stop=c == NT // 4 - 1).then_inc(s_cs, 1)

            def spread_v():
                pe.wait_ge(s_csc, 2)
                for i in range(4):
                    last = mm(pL[:, 0:P], csum[:, i * P:(i + 1) * P], pick[:, i, :], start=i == 0, stop=i == 3)
                last.then_inc(s_cs2, 1)

            def mean_of_all():
                pe.wait_ge(s_csb, 1)
                mm(pW[:, 0:P], csb[:, :], WA[:, :]).then_inc(s_hs, 1)

            def transposes(s, n):
                k = NG * s + n
                if n % GPM == 0:
                    pe.wait_ge(s_mask, NM * s + n // GPM + 1)
                if not (isinstance(s, int) and k < NTP):
                    pe.wait_ge(s_ev, k - NTP + 1)
                for c in range(GROUP):
                    j = (n % GPM) * GROUP + c
                    for a in range(TA):
                        last = pe.transpose(tp[n % NTP][:, c * ROWS + a * P:c * ROWS + (a + 1) * P],
                                            mask[:, n // GPM % NMB, a, j * P:(j + 1) * P], identb[:, :])
                last.then_inc(s_tp, 1)

            def products(s, n):
                k = NG * s + n
                if n == 0 and not (isinstance(s, int) and s == 0):
                    pe.wait_ge(s_accS, s)
                pe.wait_ge(s_ev, k + 1)
                for c in range(GROUP):
                    jc = n * GROUP + c
                    for half in (ghi, glo):
                        last = mm(acc[:, :], half[:, jc, :], adjT[:, n % NAT, c * ROWS:(c + 1) * ROWS],
                                  start=jc == 0 and half is ghi, stop=jc == NT - 1 and half is glo)
                last.then_inc(s_mm, 1)

            def aggregate(e):
                pe.wait_ge(s_accS, e + 1)
                for a in range(TA):
                    last = mm(mean_of(a, P + 1), accS[:, a * P:(a + 1) * P], WAe[:, :])
                last.then_inc(s_agg, 1)

            def turn_x1n(e, sums):
                pe.wait_ge(s_x1n, e + 1)
                pe.wait_ge(s_hps, sums)
                for a in range(TA):
                    last = pe.transpose(pW[:, a * P:(a + 1) * P], x1n[:, a, :], identf[:, :])
                last.then_inc(s_x1T, 1)

            def logits(e, a):
                pe.wait_ge(s_x1L, e + 1)
                wait(pe, s_lb, TA * e + a)
                r = slice(a * P, (a + 1) * P)
                mm(pL[:, :], x1nL[:, r], WcH[:, :], start=True, stop=False)
                mm(pL[:, :], x1nH[:, r], WcL[:, :], start=False, stop=False)
                mm(pL[:, :], x1nH[:, r], WcH[:, :], start=False, stop=True).then_inc(s_lg, 1)

            def turn(k):
                if k == 0:
                    pe.wait_ge(s_fw, 16 * NFW)
                if k >= 3:
                    pe.wait_ge(s_ftc, k - 2)
                for j, (src, n) in enumerate(TURNED[k][0]):
                    last = pe.transpose(tpf[k % 3][:, j * P:j * P + n], src, identf[0:n, 0:n])
                last.then_inc(s_ft, 1)

            def zero_slices():
                pe.wait_ge(s_zero, 1)
                mm(pST[:, :], zeros[:, :], bl[:, :], start=True, stop=False)

            def slices(e, a):
                pe.wait_ge(s_sw, TA * e + a + 1)
                last = mm(pST[:, :], x1n[:, a, :], sw[:, a, :], start=False, stop=False)
                if a == TA - 1:
                    last.then_inc(s_st, 1)

            def first(e, n):
                if n == 1:
                    aggregate(e)

            def second(e, n, dens):
                if n == 9:
                    turn_x1n(e, dens)
                if n in LOGITS:
                    logits(e, LOGITS.index(n))
                if n in SLICES:
                    slices(e, SLICES.index(n))

            pe.wait_ge(s_flag, 1)
            one_shift = pe.value_load(flag[0:1, 0:1])
            with pe.If(one_shift > 0):
                zero_slices()
                for c in range(NT // 4):
                    sum_v(c)
                for n in range(LEAD):
                    transposes(0, n)

                def stream(s, behind, final):
                    for n in range(NG):
                        if n + LEAD < NG:
                            transposes(s, n + LEAD)
                        elif not final:
                            transposes(s + 1, n + LEAD - NG)
                        if behind > 1 and n < NG - 1:
                            second(s - 2, n, s)
                        if behind > 0:
                            first(s - 1, n)
                        if behind == 0:
                            pe.wait_ge(s_gl, min(1 + NT // 2 + GROUP * (n + 1), 1 + NT))
                            if n == 14:
                                spread_v()
                            if n == 24:
                                mean_of_all()
                        products(s, n)
                        if behind > 1 and n == NG - 1:
                            second(s - 2, n, s)

                stream(0, 0, False)
                pe.wait_ge(s_hsc, 1)
                stream(1, 1, False)
                with pe.Fori(2, NSB - 1) as s:
                    stream(s, 2, False)
                stream(NSB - 1, 2, True)
                for n in range(NG):
                    second(NSB - 2, n, NSB)
                    first(NSB - 1, n)
                for n in range(NG):
                    second(NSB - 1, n, NSB)
                    for k in turned_at(n):
                        turn(k)
            with pe.Else():
                for c in range(NT // 4):
                    sum_v(c)
                spread_v()
                mean_of_all()
                pe.wait_ge(s_hsc, 1)
                pe.wait_ge(s_gh2, 1)
                zero_slices()
                with pe.Fori(0, NSB) as s:
                    for a in range(TA):
                        for c in range(NQ):
                            k = (s * TA + a) * NQ + c
                            pe.wait_ge(s_gp, k + 1)
                            for j in range(8):
                                last = pe.transpose((pW, pL)[j // 4][:, j % 4 * P:(j % 4 + 1) * P],
                                                    eb[:, j * P:(j + 1) * P], identf[:, :])
                            last.then_inc(s_gT, 1)
                            pe.wait_ge(s_gTc, 2 * k + 2)
                            for j in range(8):
                                last = mm(acc[:, a * P:(a + 1) * P], V[:, c * 8 + j, :], pT[:, j * P:(j + 1) * P],
                                          start=c == 0 and j == 0, stop=c == NQ - 1 and j == 7)
                    last.then_inc(s_acc, 1)
                    for n in range(NG):
                        first(s, n)
                    for n in range(NG):
                        second(s, n, s + 1)
                for k in range(len(TURNED)):
                    turn(k)

            mm(pST[:, :], zeros[:, :], bl[:, :], start=False, stop=True).then_inc(s_st, 1)
            pe.wait_ge(s_sws, TA * NSB)
            mm(pW[:, :], ones[:, :], swsum[:, :]).then_inc(s_fp, 1)
            pe.wait_ge(s_ftc, len(TURNED))
            pe.wait_ge(s_std, 1)
            for h in range(H):
                r = (h % 2) * 64
                last = mm(pL[r:r + 64, (h // 2) * G:(h // 2 + 1) * G], wfT[:, h * HD:(h + 1) * HD],
                          STacc[:, h * G:(h + 1) * G])
            last.then_inc(s_fp, 1)
            pe.wait_ge(s_fd, F_UT)
            for c in range(KC):
                for k in range(KC):
                    last = mm(pST[:, c * G:(c + 1) * G], inT[:, k, DI + c * P:DI + (c + 1) * P], uT[:, k, :],
                              k == 0, k == KC - 1)
            for c in range(2):
                a = 2 * DI + c * NS
                for k in range(KC):
                    last = mm(acc[0:NS, c * G:(c + 1) * G], inT[:, k, a:a + NS], uT[:, k, :], k == 0, k == KC - 1)
            last.then_inc(s_fp, 1)
            for k in range(KC):
                last = mm(tpf[0][0:G, 0:2 * H], uT[:, k, :], inT[:, k, DIP - 2 * H:DIP], k == 0, k == KC - 1)
            last.then_inc(s_fp, 1)
            for c in range(KC):
                for k in range(KC):
                    last = mm(pS[:, c * G:(c + 1) * G], inT[:, k, c * P:(c + 1) * P], uT[:, k, :], k == 0, k == KC - 1)
            last.then_inc(s_fp, 1)
            pe.wait_ge(s_fd, F_AD)
            pe.wait_ge(s_fg, 4)
            mm(tpf[1][0:G, :], M2[0:G, :], aF[0:G, :])
            mm(tpf[2][0:G, :], M1[0:G, :], aB[0:G, :]).then_inc(s_fp, 1)
            pe.wait_ge(s_fd, F_XA)
            for c in range(KC):
                pe.transpose(pL[0:G, c * P:(c + 1) * P], xa[:, c, :], identf[:, :])
            mm(tpf[0][0:G, 64:64 + 2 * G], xa[0:NS, KC, :], Csh[0:NS, :])
            for c in range(KC):
                for k in range(KC):
                    last = mm(pW[:, c * G:(c + 1) * G], fcT[:, k, c * P:(c + 1) * P], xa[:, k, :], k == 0, k == KC - 1)
            last.then_inc(s_fp, 1)
            pe.wait_ge(s_fd, F_M)
            for h in range(H):
                r = (h % 2) * 64
                last = mm(acc[r:r + 64, (h // 2) * G:(h // 2 + 1) * G], xt[0:G, h * HD:(h + 1) * HD],
                          EF[0:G, h * G:(h + 1) * G])
            last.then_inc(s_fp, 1)
            pe.wait_ge(s_fd, F_YQ)
            for c in range(KC):
                last = mm(tpf[1][:, 0:G], ones[:, :], yq[:, c, :], c == 0, c == KC - 1)
            last.then_inc(s_fp, 1)
            pe.wait_ge(s_fd, F_YN)
            for c in range(KC):
                for k in range(KC):
                    last = mm(tpf[2][:, c * G:(c + 1) * G], oT[:, k, c * P:(c + 1) * P], yT[:, k, :], k == 0, k == KC - 1)
            last.then_inc(s_fp, 1)
            pe.wait_ge(s_fd, F_OT)
            for h in range(H):
                r = (h % 2) * 64
                last = mm(pW[r:r + 64, (h // 2) * D:(h // 2 + 1) * D], otT[r:r + 64, h // 2, :],
                          woT[r:r + 64, h // 2, :])
            last.then_inc(s_fp, 1)
            pe.wait_ge(s_fd, F_MO)

            with pe.Fori(0, NSB // NFB) as g:
                for b in range(NFB):
                    s = NFB * g + b
                    pe.wait_ge(s_fl[b], 32 * g + 32)
                    for a in range(TA):
                        for c in range(KC):
                            last = pe.transpose(tpf[a][:, c * P:(c + 1) * P], swl[b][:, a, c * P:(c + 1) * P],
                                                identf[:, :])
                        last.then_inc(s_fT, 1)
                    pe.wait_ge(s_fy2, s + 1)
                    for a in range(TA):
                        pe.wait_ge((s_fTc, s_fTd)[a % 2], 2 * s + a // 2 + 1)
                        for c in range(KC):
                            last = mm((pW, pL)[b % 2][:, a * P:(a + 1) * P], swT[:, a, c * P:(c + 1) * P],
                                      Mo[:, c, :], c == 0, c == KC - 1)
                    last.then_inc(s_fm, 1)

        @block.vector
        def _(dve):
            cnt = {}

            def linker(s):
                cnt[s.name] = 0

                def link(ins, wait=True):
                    ins.then_inc(s, 1)
                    cnt[s.name] += 1
                    if wait:
                        dve.wait_ge(s, cnt[s.name])
                    return ins
                return link
            link = linker(ch)
            ts, tts, stt = dve.tensor_scalar, dve.tensor_tensor, dve.scalar_tensor_tensor

            def log1p_fraction(link, u, z, el, t, b):
                link(ts(t, u, 1.0, None, ALU.add))
                link(ts(b, t.bitcast(I32), 23, None, ALU.logical_shift_right))
                link(ts(el, b, -127.0, LN2, ALU.add, ALU.mult))
                link(ts(b, t.bitcast(I32), 0x7fffff, 0x3f800000, ALU.bitwise_and, ALU.bitwise_or))
                link(ts(z, b.bitcast(F32), -1.0, None, ALU.add))
                link(tts(t, u, z, ALU.subtract))
                link(stt(out=t, in0=el, scalar=0.0, in1=t, op0=ALU.is_equal, op1=ALU.mult))
                link(tts(z, z, t, ALU.add))
                link(ts(t, z, 2.0, None, ALU.add))
                link(dve.reciprocal(t, t))
                link(tts(z, z, t, ALU.mult))

            def log1p_sum(link, o, z, el, t):
                link(tts(t, z, z, ALU.mult))
                link(ts(o, t, 1.0 / 17, None, ALU.mult))
                for k in (15, 13, 11, 9, 7, 5, 3):
                    link(stt(out=o, in0=o, scalar=1.0 / k, in1=t, op0=ALU.add, op1=ALU.mult))
                link(stt(out=o, in0=o, scalar=1.0, in1=z, op0=ALU.add, op1=ALU.mult))
                if el is None:
                    link(ts(o, o, 2.0, None, ALU.mult))
                else:
                    link(stt(out=o, in0=o, scalar=2.0, in1=el, op0=ALU.mult, op1=ALU.add))

            dve.wait_ge(s_tr, 1)
            dve.tensor_copy(WAT[:, :], pW[:, 0:P]).then_inc(s_trc, 1)
            dve.wait_ge(s_tr, 2)
            dve.tensor_copy(WgT[:, :], pL[:, 0:P]).then_inc(s_trc, 1)
            dve.wait_ge(s_tr, 3)
            dve.tensor_copy(v2[:, :], pST[:, 0:1]).then_inc(s_trc, 1)
            dve.wait_ge(s_tr, 4)
            dve.tensor_copy(Wg[:, 0:1], pST[:, 2:3]).then_inc(s_trc, 1)
            dve.wait_ge(s_id, 4)
            ts(centre[:, :], identf[:, :], -1.0 / D, None, ALU.add).then_inc(s_ctr, 1)
            dve.wait_ge(s_tr, 5)
            dve.tensor_copy(Wgc[:, :], pST[:, 128:256]).then_inc(s_trc, 1)
            dve.memset(zeros[:, :], 0.0).then_inc(s_zero, 1)

            def spread_bias():
                dve.wait_ge(s_w, 16 * 6)
                dve.tensor_copy(bxB[:, :, :], bxT[:, :].unsqueeze(2).to_broadcast([HD, H, P])).then_inc(s_trc, 1)
                dve.wait_ge(s_tr, 6)
                dve.tensor_copy(WslT[:, :], pS[0:HD, 0:G]).then_inc(s_trc, 1)

            def slice_weight():
                link(ts(tmpB[:, :], tmpB[:, :], 1e-6, None, ALU.max))
                link(dve.reciprocal(tmpB[:, :], tmpB[:, :]))
                dve.wait_ge(s_tr, 7)
                link(tts(hg(lg[:, 0, :]), hg(acc[:, :]), tmpB[:, :].unsqueeze(2).to_broadcast([P, H, G]), ALU.mult))
                link(dve.tensor_copy(WcH[:, :], lg[:, 0, :]))
                link(tts(WcL[:, :], lg[:, 0, :], WcH[:, :].bitcast(F32), ALU.subtract))
                dve.wait_ge(s_tr, 8)
                link(tts(hg(bl[:, :]), hg(pS[:, :]), bsB[:, :].unsqueeze(1).to_broadcast([P, H, G]), ALU.add))
                link(tts(hg(bl[:, :]), hg(bl[:, :]), tmpB[:, :].unsqueeze(2).to_broadcast([P, H, G]), ALU.mult))

            def make_mask(s, h):
                if h >= NM:
                    s, h = s + 1, h - NM
                q = h // MPQ
                dve.wait_ge(s_adj[q % NBUF], 16 * ((NQ // NBUF) * s + q // NBUF + 1))
                if not (isinstance(s, int) and s == 0 and h < NMB):
                    dve.wait_ge(s_tp, NG * s + (h - NMB + 1) * GPM)
                ts(mask[:, h % NMB, :, :], adjb[q % NBUF].rearrange("p (a j) -> p a j", a=TA)
                   [:, :, h % MPQ * MCOLS:(h % MPQ + 1) * MCOLS], 0, None, ALU.is_gt).then_inc(s_mask, 1)

            early = iter(range(NMB))

            def early_mask():
                make_mask(0, next(early))

            N64 = lambda k, n=1: n64[:, k, :] if n == 1 else n64[:, k:k + n, :]
            dve.sem_inc(s_ssv, 2)
            dve.sem_inc(s_xmv, 2)
            with dve.Fori(0, NSB // NXB) as g:
                for b in range(NXB):
                    k = NXB * g + b
                    col = bass.ds(TA * k, TA)
                    dve.wait_ge(s_xs[b], 16 * g + 16)
                    for a in range(TA):
                        last = dve.bn_stats(xst[:, b % 2, a, :], xs[:, b, a, 1:D])
                    last.then_inc(s_xfree, 1)
                    dve.wait_ge(s_xfree, k + 1)
                    dve.wait_ge(s_Vq, k + 3)
                    dve.wait_ge(s_xmv, k + 1)
                    dve.tensor_reduce(n64[:, 6, col], vq[:, b % 2, :, 1:D], AXX, ALU.add).then_inc(s_ssv, 1)
                    for a in range(TA):
                        last = dve.bn_aggr(xma[:, b % 2, a, :], xst[:, b % 2, a, :])
                    last.then_inc(s_xag, 1)

            def rsqrt(o, x, t, b, link=link):
                link(ts(b, x.bitcast(I32), 1, None, ALU.logical_shift_right))
                link(ts(o.bitcast(I32), b, -1.0, float(0x5f3759df), ALU.mult, ALU.add))
                for _ in range(3):
                    link(tts(t, o, o, ALU.mult))
                    link(stt(out=t, in0=t, scalar=-0.5, in1=x, op0=ALU.mult, op1=ALU.mult))
                    link(stt(out=o, in0=t, scalar=1.5, in1=o, op0=ALU.add, op1=ALU.mult))

            def sqrt(o, x, t, b):
                link(ts(x, x, 1e-37, None, ALU.max))
                rsqrt(o, x, t, b)
                link(tts(o, o, x, ALU.mult))

            spread_bias()
            dve.wait_ge(s_xmv, NSB + 2)
            dve.wait_ge(s_xx, NSB)
            dve.wait_ge(s_ssv, NSB + 2)
            link(tts(N64(2), N64(1), xmv[:, :, 0], ALU.subtract))
            link(ts(N64(0), xmv[:, :, 1], float(D - 1), None, ALU.mult))
            link(tts(N64(3), N64(2), N64(2), ALU.mult))
            link(stt(out=N64(4), in0=N64(3), scalar=(D - 1) / D / D, in1=N64(0), op0=ALU.mult, op1=ALU.add))
            link(stt(out=N64(5), in0=N64(3), scalar=(D - 1) / D, in1=N64(0), op0=ALU.mult, op1=ALU.add))
            link(ts(N64(5), N64(5), 1.0 / D, 1e-5, ALU.mult, ALU.add))
            link(ts(N64(4, 3), N64(4, 3), 1e-37, None, ALU.max))
            rsqrt(N64(7, 3), N64(4, 3), N64(10, 3), bits64[:, :, :])
            link(tts(N64(7), N64(7), N64(4), ALU.mult))
            link(tts(N64(6), N64(9), N64(6), ALU.mult))
            link(ts(N64(2), N64(2), (D - 1) / D, None, ALU.mult))
            link(tts(N64(2), N64(2), N64(8), ALU.mult))
            link(ts(N64(2), N64(2), -1.0, EPS1, ALU.add, ALU.max))
            link(stt(out=N64(9), in0=N64(2), scalar=2.0, in1=N64(2), op0=ALU.add, op1=ALU.mult))
            b64 = bits64[:, 0, :]
            sqrt(N64(10), N64(9), N64(12), b64)
            link(tts(N64(11), N64(10), N64(2), ALU.add))
            log1p_fraction(link, N64(11), N64(12), N64(13), N64(15), b64)
            log1p_sum(link, N64(14), N64(12), N64(13), N64(15))
            link(tts(N64(7), N64(7), N64(8), ALU.mult))
            link(ts(N64(7), N64(7), MIN_NORM, None, ALU.max))
            link(dve.reciprocal(N64(7), N64(7)))
            link(tts(N64(14), N64(14), N64(7), ALU.mult))
            link(tts(N64(14), N64(14), N64(8), ALU.mult))
            link(tts(N64(8), N64(6), N64(14), ALU.mult))
            ts(N64(9), N64(8), MIN_NORM, None, ALU.max).then_inc(s_pa, 1)
            dve.wait_ge(s_pa, 1)
            slice_weight()
            link(dve.reciprocal(N64(16), N64(9)))
            link(ts(N64(15), N64(9), 1.0, None, ALU.min))
            link(tts(N64(15), N64(15), N64(15), ALU.mult))
            link(ts(N64(12), N64(15), 1.0 / 362880, None, ALU.mult))
            for k in (5040, 120, 6):
                link(stt(out=N64(12), in0=N64(12), scalar=1.0 / k, in1=N64(15), op0=ALU.add, op1=ALU.mult))
            link(ts(N64(12), N64(12), 1.0, None, ALU.add))
            dve.wait_ge(s_pd, 2)
            link(tts(N64(10), N64(10), N64(11), ALU.subtract))
            link(stt(out=N64(10), in0=N64(10), scalar=0.5, in1=N64(16), op0=ALU.mult, op1=ALU.mult))
            link(tts(N64(10), N64(10), N64(12), ALU.subtract))
            link(stt(out=N64(10), in0=N64(9), scalar=1.0, in1=N64(10), op0=ALU.is_gt, op1=ALU.mult))
            link(tts(N64(10), N64(10), N64(12), ALU.add))
            link(tts(N64(8), N64(8), N64(10), ALU.mult))
            link(tts(N64(9), N64(8), N64(8), ALU.mult))
            link(ts(N64(12), N64(9), 1.0, None, ALU.add))
            sqrt(N64(13), N64(12), N64(15), b64)
            link(ts(N64(13), N64(13), 1.0, None, ALU.add))
            link(dve.reciprocal(N64(13), N64(13)))
            link(tts(N64(9), N64(9), N64(13), ALU.mult))
            link(ts(N64(9), N64(9), EPS1, None, ALU.max))
            link(stt(out=N64(12), in0=N64(9), scalar=2.0, in1=N64(9), op0=ALU.add, op1=ALU.mult))
            sqrt(N64(13), N64(12), N64(15), b64)
            link(tts(N64(9), N64(9), N64(13), ALU.add))
            log1p_fraction(link, N64(9), N64(12), N64(13), N64(15), b64)
            log1p_sum(link, N64(17), N64(12), N64(13), N64(15))
            link(ts(N64(8), N64(8), MIN_NORM, None, ALU.max))
            link(dve.reciprocal(N64(8), N64(8)))
            link(tts(N64(17), N64(17), N64(8), ALU.mult))
            link(tts(N64(17), N64(17), N64(10), ALU.mult))
            link(tts(beta[:, :], N64(17), N64(14), ALU.mult))
            dve.wait_ge(s_Vc, NSB)
            link(tts(tt[:, :], beta[:, :], V[:, :, 0], ALU.mult))
            link(ts(N64(18), tt[:, :], -1.0, None, ALU.mult))
            link(dve.tensor_reduce(tm[:, 0:1], tt[:, :], AXX, ALU.max))
            dve.tensor_reduce(tm[:, 1:2], N64(18), AXX, ALU.max).then_inc(s_mx, 1)
            dve.wait_ge(s_mx, 1)
            dve.sem_inc(s_beta, 1)
            early_mask()
            dve.wait_ge(s_mxT, 1)
            link(dve.tensor_reduce(m2[:, 0:1], pST[0:2, 0:P], AXX, ALU.max))
            ts(m2[:, 2:4], identf[0:2, 0:2], m2[:, 0:1], None, ALU.mult).then_inc(s_m2, 1)
            early_mask()
            dve.wait_ge(s_mb, 1)
            link(dve.tensor_copy(tm[:, 4:6], pST[:, 256:258]))
            link(tts(tm[:, 2:3], tm[:, 4:5], tm[:, 5:6], ALU.add))
            link(tts(tm[:, 3:4], tm[:, 5:6], tm[:, 4:5], ALU.subtract))
            link(ts(tm[:, 3:4], tm[:, 3:4], 0.5, None, ALU.mult))
            ts(flag[:, :], tm[:, 2:3], SPREAD, None, ALU.is_le).then_inc(s_flag, 1)
            early_mask()
            early_mask()
            dve.wait_ge(s_flag, 1)

            def sum_of_all():
                dve.tensor_copy(pick[:, :, :], identf[0:4, 0:4].unsqueeze(2).to_broadcast([4, 4, P])).then_inc(s_csc, 1)
                dve.wait_ge(s_cs, NT // 4)
                dve.tensor_copy(csum[:, :], pL[0:4, :]).then_inc(s_csc, 1)

            def spread_blocks():
                dve.wait_ge(s_cs2, 1)
                dve.tensor_copy(csb[:, :], pL[:, 0:P]).then_inc(s_csb, 1)

            def spread_sum():
                dve.wait_ge(s_hs, 1)
                dve.tensor_copy(Hs[:, :], pW[:, 0:P]).then_inc(s_hsc, 1)
                dve.wait_ge(s_hsc, 1)

            C = lambda k, n=1: c4[:, k, :]

            class Chain:
                def __init__(self, s, e, total):
                    self.s, self.e, self.total, self.n = s, e, total, 0

                def __call__(self, ins):
                    self.n += 1
                    ins.then_inc(self.s, 1)
                    dve.wait_ge(self.s, self.total * self.e + self.n)

            class First:
                def __init__(self, e):
                    self.e, self.link = e, Chain(che, e, CHAIN_A)

                def row_scales(self):
                    e, link = self.e, self.link
                    dve.wait_ge(s_agg, e + 1)
                    dve.tensor_copy(c4[:, 0, 0:TA - 1], pW[:, 0:(TA - 1) * (P + 1)]
                                    .rearrange("p (a w) -> p a w", a=TA - 1)[:, :, P]).then_inc(s_den, 1)
                    dve.tensor_copy(c4[:, 0, TA - 1:TA], pL[:, P:P + 1]).then_inc(s_den, 1)
                    dve.wait_ge(s_den, 2 * e + 2)
                    link(ts(C(1), C(0), 0.0, None, ALU.is_equal))
                    link(stt(out=C(2), in0=C(1), scalar=float(N), in1=C(0), op0=ALU.mult, op1=ALU.add))
                    link(dve.reciprocal(C(2), C(2)))
                    tts(C(1), C(1), C(2), ALU.mult).then_inc(s_rd, 1)

                def means(self):
                    e, link = self.e, self.link
                    dve.wait_ge(s_hps, e + 1)
                    for a in range(TA):
                        last = stt(out=hp[:, a, :], in0=Hs[:, :], scalar=c4[:, 1, a:a + 1], in1=hp[:, a, :],
                                   op0=ALU.mult, op1=ALU.add)
                    link(last)
                    ts(ex[:, :, :], hp[:, :, :], 0.0, None, ALU.min).then_inc(s_hp, 1)

                def elu(self):
                    e = self.e
                    dve.wait_ge(s_re, e + 1)
                    dve.wait_ge(s_ex, e + 1)
                    stt(out=yy[:, :, :], in0=ex[:, :, :], scalar=-1.0, in1=yy[:, :, :], op0=ALU.add, op1=ALU.add)\
                        .then_inc(s_y, 1)

                def theta(self):
                    e, link = self.e, self.link
                    dve.wait_ge(s_rt, 3 * e + 1)
                    link(ts(C(2), C(2), MIN_NORM, None, ALU.max))
                    link(ts(C(3), C(3), 1.0, None, ALU.add))
                    link(dve.reciprocal(C(3), C(3)))
                    link(tts(C(3), C(3), C(0), ALU.mult))
                    link(ts(C(3), C(3), EPS1, None, ALU.max))
                    link(stt(out=C(4), in0=C(3), scalar=2.0, in1=C(3), op0=ALU.add, op1=ALU.mult))
                    dve.sem_inc(s_rq1, 1)
                    link(dve.reciprocal(C(2), C(2)))
                    link(ts(C(2), C(2), 0.5, None, ALU.mult))

                def log_argument(self):
                    e, link = self.e, self.link
                    dve.wait_ge(s_rt, 3 * e + 2)
                    link(tts(C(6), C(3), C(5), ALU.add))
                    log1p_fraction(link, C(6), C(7), C(8), C(10), bits[:, 0, :])

                def log_factor(self):
                    log1p_sum(self.link, C(9), C(7), C(8), C(10))
                    tts(C(9), C(9), C(2), ALU.mult).then_inc(s_lf, 1)

                def norm_s(self):
                    e, link = self.e, self.link
                    dve.wait_ge(s_rt, 3 * e + 3)
                    ts(C(15), C(15), MIN_NORM, None, ALU.max).then_inc(s_nn, 1)
                    dve.wait_ge(s_nn, e + 1)
                    link(dve.reciprocal(C(19), C(15)))

                    assert self.link.n == CHAIN_A, self.link.n

                def at(self, n):
                    if n == 5:
                        self.row_scales()
                    if n == 8:
                        self.means()
                    if n == 12:
                        self.elu()
                    if n == 18:
                        self.theta()
                    if n == 20:
                        self.log_argument()
                        self.log_factor()
                    if n == 26:
                        self.norm_s()

            class Second:
                def __init__(self, e):
                    self.e, self.link = e, Chain(che2, e, CHAIN_B)

                def sinh(self):
                    e, link = self.e, self.link
                    dve.wait_ge(s_sh, 2 * e + 2)
                    link(tts(C(18), C(16), C(17), ALU.subtract))
                    stt(out=C(25), in0=C(18), scalar=0.25, in1=C(19), op0=ALU.mult, op1=ALU.mult).then_inc(s_kr, 1)
                    dve.wait_ge(s_kr, e + 1)
                    link(tts(C(20), C(25), C(25), ALU.mult))
                    link(tts(C(20), C(20), C(14), ALU.mult))
                    link(ts(C(20), C(20), 4.0, 1.0, ALU.mult, ALU.add))
                    dve.sem_inc(s_rq2, 1)

                def residual(self):
                    e, link = self.e, self.link
                    dve.wait_ge(s_sv, e + 1)
                    dve.wait_ge(s_rt2, 2 * e + 1)
                    link(dve.tensor_copy(hp[:, :, 0], C(21)))
                    dve.wait_ge(s_xin, 16 * e + 16)
                    wait(dve, s_x1o, 16 * e)
                    tts(x1[:, :, :], hp[:, :, :], xin[:, :, :], ALU.add).then_inc(s_x1, 1)
                    dve.wait_ge(s_x1, e + 1)

                def statistics(self):
                    link = self.link
                    for a in range(TA):
                        last = dve.bn_stats(bst[:, a, :], x1[:, a, :])
                    link(last)
                    dve.sem_inc(dve_tick, 1)
                    for a in range(TA):
                        last = dve.bn_aggr(mv[:, a, :], bst[:, a, :])
                    link(last)
                    link(ts(C(23), mv[:, :, 1], 1e-5, None, ALU.add))
                    dve.sem_inc(s_rq2, 1)

                def layernorm(self):
                    dve.wait_ge(s_rt2, 2 * self.e + 2)
                    wait(dve, s_st, self.e)
                    for a in range(TA):
                        last = ts(x1n[:, a, :], x1[:, a, :], mv[:, a, 0:1], c4[:, 24, a:a + 1], ALU.subtract, ALU.mult)
                    last.then_inc(s_x1n, 1)

                def lower_half(self):
                    dve.wait_ge(s_x1Tc, self.e + 1)
                    tts(x1nL[:, :], pW[:, :], x1nH[:, :].bitcast(F32), ALU.subtract).then_inc(s_x1L, 1)

                def logits(self, a):
                    e = self.e
                    dve.wait_ge(s_lg, TA * e + a + 1)
                    wait(dve, s_es, TA * e + max(a - 1, 0))
                    tts(lg[:, a % 2, :], pL[:, :], bl[:, :], ALU.add).then_inc(s_lb, 1)
                    dve.wait_ge(s_lb, TA * e + a + 1)
                    dve.tensor_reduce(r8[:, a % 2, 0, :], hg(lg[:, a % 2, :]), AXX, ALU.max).then_inc(s_lx, 1)

                def sums(self, a):
                    e, link = self.e, self.link
                    dve.wait_ge(s_es, TA * e + a + 1)
                    link(dve.tensor_reduce(r8[:, a % 2, 1, :], hg(es[:, a % 2, :]), AXX, ALU.add))
                    dve.reciprocal(r8[:, a % 2, 1, :], r8[:, a % 2, 1, :]).then_inc(s_rs, 1)

                def at(self, n):
                    if n == 0:
                        self.sinh()
                    if n == 4:
                        self.residual()
                        self.statistics()
                    if n == 6:
                        self.layernorm()
                    if n == 13:
                        self.lower_half()
                    if n in MAXIMA:
                        self.logits(MAXIMA.index(n))
                    if n in SUMS:
                        self.sums(SUMS.index(n))
                    if n == NG - 1:
                        assert self.link.n == CHAIN_B, self.link.n

            one_shift = dve.value_load(flag[0:1, 0:1])
            with dve.If(one_shift > 0):
                dve.wait_ge(s_wexp, 1)
                tts(N64(22), N64(23), beta[:, :], ALU.mult).then_inc(s_wp, 1)
                dve.wait_ge(s_gh, 1)
                tts(glo[:, :, 0], N64(23), ghi[:, :, 0].bitcast(F32), ALU.subtract).then_inc(s_gl, 1)
                dve.wait_ge(s_wp, 1)
                for k, c in enumerate(SPLIT):
                    dve.wait_ge(s_gh, k + 2)
                    stt(out=glo[:, c, 1:D], in0=V[:, c, 1:D], scalar=n64[:, 22, c:c + 1],
                        in1=ghi[:, c, 1:D].bitcast(F32), op0=ALU.mult, op1=ALU.subtract).then_inc(s_gl, 1)
                for h in range(NMB, NM + MHEAD):
                    make_mask(0, h)
                    if h == 6:
                        sum_of_all()
                    if h == 10:
                        spread_blocks()
                spread_sum()

                def stream(s, second, final):
                    b = Second(s - 2)
                    a = First(s - 1)
                    for n in range(NG):
                        if n % GPM == 1 and not (final and (n + MLEAD) // GPM >= NM):
                            make_mask(s, (n + MLEAD) // GPM)
                        if second:
                            b.at(n)
                        a.at(n)
                stream(1, False, False)
                with dve.Fori(2, NSB - 1) as s:
                    stream(s, True, False)
                stream(NSB - 1, True, True)
                b, a = Second(NSB - 2), First(NSB - 1)
                for n in range(NG):
                    b.at(n)
                    a.at(n)
                b = Second(NSB - 1)
                for n in range(NG):
                    b.at(n)
            with dve.Else():
                sum_of_all()
                spread_blocks()
                spread_sum()
                dve.sem_inc(s_tst, 1)
                tts(V[:, :, :], V[:, :, :], beta[:, :].unsqueeze(2).to_broadcast([P, NT, D]), ALU.mult)\
                    .then_inc(s_gw, 1)
                dve.wait_ge(s_gw, 1)
                dve.memset(V[:, :, 0], 1.0).then_inc(s_gh2, 1)
                with dve.Fori(0, NSB) as s:
                    for a in range(TA):
                        for sweep in range(2):
                            for c in range(NQ):
                                k = ((s * TA + a) * 2 + sweep) * NQ + c
                                n = 3 * k
                                dve.wait_ge(s_ga, 16 * k + 16)
                                dve.wait_ge(s_gt, 16 * k + 16)
                                if c == 0 and sweep == 0:
                                    dve.wait_ge(s_gT, (s * TA + a) * NQ)
                                if sweep == 1 and c > 0:
                                    dve.wait_ge(s_gT, (s * TA + a) * NQ + c)
                                ts(mb[:, :], adjb[0][:, 0:STEP], 0, None, ALU.is_gt).then_inc(chg, 1)
                                dve.wait_ge(chg, n + 1)
                                tts(eb[:, :], mb[:, :], tb[:, :], ALU.mult).then_inc(chg, 1)
                                dve.wait_ge(chg, n + 2)
                                ts(mb[:, :], mb[:, :], -MASKED, MASKED, ALU.mult, ALU.add).then_inc(chg, 1)
                                dve.wait_ge(chg, n + 3)
                                tts(eb[:, :], eb[:, :], mb[:, :], ALU.add).then_inc(s_gm, 1)
                                dve.wait_ge(s_gm, k + 1)
                                if sweep == 0:
                                    dve.tensor_reduce(rm[:, c:c + 1], eb[:, :], AXX, ALU.max).then_inc(chm, 1)
                                    if c == NQ - 1:
                                        m = (s * TA + a) * (NQ + 2) + NQ
                                        dve.wait_ge(chm, m)
                                        dve.tensor_reduce(rm[:, NQ:NQ + 1], rm[:, 0:NQ], AXX, ALU.max)\
                                            .then_inc(chm, 1)
                                        dve.wait_ge(chm, m + 1)
                                        ts(rm[:, NQ + 1:NQ + 2], rm[:, NQ:NQ + 1], -1.0, None, ALU.mult)\
                                            .then_inc(chm, 1)
                                        dve.wait_ge(chm, m + 2)
                                else:
                                    dve.sem_inc(s_ge, 1)
                    a, b = First(s), Second(s)
                    for n in range(NG):
                        a.at(n)
                    for n in range(NG):
                        b.at(n)

            link = linker(chf)
            cnt_fd = [0]

            def mark(k, ins):
                cnt_fd[0] += 1
                assert cnt_fd[0] == k
                ins.then_inc(s_fd, 1)
                dve.wait_ge(s_fd, k)
            dve.wait_ge(s_st, NSB + 1)
            dve.tensor_copy(STacc[:, :], pST[:, :]).then_inc(s_std, 1)
            link(dve.memset(xb, 0.0))
            link(dve.memset(Csh[0:NS, :], 0.0))
            dve.wait_ge(s_fp, 1)
            for half in range(2):
                r = slice(half * 64, half * 64 + 64)
                link(dve.tensor_copy(SN[r, :, :], pW[r, :].rearrange("p (c t g) -> p c t g", t=2, g=G)[:, :, half, :]))
            link(ts(rS, SN, 1e-5, None, ALU.add))
            link(dve.reciprocal(rS, rS))
            link(tts(uT, SN, bfx.unsqueeze(2).to_broadcast([P, KC, G]), ALU.mult))
            dve.wait_ge(s_fp, 2)
            link(tts(uT, uT, pL[:, 0:KC * G].rearrange("p (c g) -> p c g", g=G), ALU.add))
            mark(F_UT, tts(uT, uT, rS, ALU.mult))
            dve.wait_ge(s_fp, 3)
            v3 = lambda ap, g=G: ap.rearrange("p (c g) -> p c g", g=g)
            dve.tensor_copy(xb[:, 0:KC, 2:], v3(pST[:, 0:KC * G])).then_inc(chf, 1)
            cnt[chf.name] += 1
            link(dve.tensor_copy(xb[0:NS, KC:6, 2:], v3(acc[0:NS, 0:2 * G])))
            for r, cs in ((slice(0, P), slice(0, KC)), (slice(0, NS), slice(KC, 6))):
                n = cs.stop - cs.start
                m = r.stop
                for k in range(3):
                    wk = cw[r, cs, k].unsqueeze(2).to_broadcast([m, n, G])
                    if k == 0:
                        link(tts(xa[r, cs, :], xb[r, cs, 0:G], wk, ALU.mult))
                    else:
                        link(tts(xg[r, cs, :], xb[r, cs, k:k + G], wk, ALU.mult))
                        link(tts(xa[r, cs, :], xa[r, cs, :], xg[r, cs, :], ALU.add))
                bk = cb[r, cs].unsqueeze(2).to_broadcast([m, n, G])
                if cs.start == 0:
                    link(tts(xa[r, cs, :], xa[r, cs, :], bk, ALU.add))
                else:
                    mark(F_SILU, tts(xa[r, cs, :], xa[r, cs, :], bk, ALU.add))
            T = lambda k: dts[0:G, k, :]
            dve.wait_ge(s_fp, 4)
            link(tts(T(0), tpf[0][0:G, 0:2 * H], dtb[0:G, :], ALU.add))
            link(ts(T(3), T(0), -1.0, None, ALU.mult))
            mark(F_DTEXP, tts(T(1), T(0), T(3), ALU.min))
            dve.wait_ge(s_fa, 4)
            link(ts(T(6), T(2), 2.0, None, ALU.add))
            link(dve.reciprocal(T(6), T(6)))
            link(tts(T(5), T(2), T(6), ALU.mult))
            log1p_sum(link, T(4), T(5), None, T(6))
            link(ts(T(0), T(0), 0.0, None, ALU.max))
            link(tts(T(0), T(0), T(4), ALU.add))
            link(tts(T(7), T(0), Ae[0:G, :], ALU.mult))
            link(ts(T(7), T(7), -1.0, -1e30, ALU.mult, ALU.max))
            dve.wait_ge(s_fg, 4)
            link(tts(hg(aF[0:G, :]), dts[0:G, 7, 0:H].unsqueeze(2).to_broadcast([G, H, G]),
                     M1[0:G, :].unsqueeze(1).to_broadcast([G, H, G]), ALU.mult))
            mark(F_AD, tts(hg(aB[0:G, :]), dts[0:G, 7, H:2 * H].unsqueeze(2).to_broadcast([G, H, G]),
                           M2[0:G, :].unsqueeze(1).to_broadcast([G, H, G]), ALU.mult))
            dve.wait_ge(s_fp, 5)
            mark(F_ZEXP, dve.tensor_copy(zT, v3(pS[:, 0:KC * G])))
            for r, cs in ((slice(0, P), slice(0, KC)), (slice(0, NS), slice(KC, 6))):
                link(ts(xg[r, cs, :], xg[r, cs, :], 1.0, None, ALU.add))
                link(dve.reciprocal(xg[r, cs, :], xg[r, cs, :]))
                link(tts(xa[r, cs, :], xa[r, cs, :], xg[r, cs, :], ALU.mult))
            link(dve.tensor_copy(Csh[0:NS, 1:G], xa[0:NS, 5, 0:G - 1]))
            mark(F_XA, dve.tensor_copy(Csh[0:NS, G:2 * G - 1], xa[0:NS, 5, 1:G]))
            dve.wait_ge(s_fp, 6)
            link(dve.tensor_copy(EF[0:G, :], tpf[1][0:G, :]))
            mark(F_SEG, dve.tensor_copy(EB[0:G, :], tpf[2][0:G, :]))
            dve.wait_ge(s_fa, 5)
            link(ts(sgz, sgz, 1.0, None, ALU.add))
            link(dve.reciprocal(sgz, sgz))
            link(tts(sgz, sgz, zT, ALU.mult))
            dve.wait_ge(s_fp, 7)
            link(dve.tensor_copy(xt[0:G, :], pL[0:G, :]))
            link(dve.tensor_copy(CB[0:G, :], tpf[0][0:G, 64:64 + 2 * G]))
            link(tts(CB[0:G, 0:G], CB[0:G, 0:G], M1[0:G, :], ALU.mult))
            link(tts(CB[0:G, G:2 * G], CB[0:G, G:2 * G], M2[0:G, :], ALU.mult))
            dve.wait_ge(s_fa, 7)
            for k, Et in enumerate((EF, EB)):
                link(tts(hg(Et[0:G, :]), hg(Et[0:G, :]),
                         CB[0:G, k * G:(k + 1) * G].unsqueeze(1).to_broadcast([G, H, G]), ALU.mult))
                link(tts(hg(Et[0:G, :]), hg(Et[0:G, :]),
                         dts[0:G, 0, k * H:(k + 1) * H].unsqueeze(2).to_broadcast([G, H, G]), ALU.mult))
            mark(F_M, tts(EF[0:G, :], EF[0:G, :], EB[0:G, :], ALU.add))
            link(tts(yT, v3(pW[:, 0:KC * G]), Dc.unsqueeze(2).to_broadcast([P, KC, G]), ALU.add))
            link(tts(yT, yT, xa[:, 0:KC, :], ALU.mult))
            dve.wait_ge(s_fp, 8)
            link(tts(yT, yT, v3(acc[:, 0:KC * G]), ALU.add))
            link(tts(yT, yT, sgz, ALU.mult))
            mark(F_YQ, tts(yq, yT, yT, ALU.mult))
            dve.wait_ge(s_fp, 9)
            link(ts(rsq, tpf[1][:, 0:G], 1.0 / DI, 1e-5, ALU.mult, ALU.add))
            rsqrt(rms, rsq, rst, rsb, link)
            link(tts(yT, yT, nw.unsqueeze(2).to_broadcast([P, KC, G]), ALU.mult))
            mark(F_YN, tts(yT, yT, rms.unsqueeze(1).to_broadcast([P, KC, G]), ALU.mult))
            dve.wait_ge(s_fp, 10)
            mark(F_OT, dve.tensor_copy(otT, v3(tpf[2][:, 0:KC * G])))
            dve.wait_ge(s_fp, 11)
            mark(F_MO, dve.tensor_copy(Mo[:, :, :], v3(pW[:, :], D)))

            dve.wait_ge(s_ob, 16)
            dve.sem_inc(s_fy2, 2)
            with dve.Fori(0, NSB // NFB) as g:
                for b in range(NFB):
                    s = NFB * g + b
                    for a in range(1, TA, 2):
                        dve.wait_ge(s_fT, s * TA + a + 1)
                        dve.tensor_copy(swT[:, a, :], tpf[a]).then_inc(s_fTd, 1)
                    dve.wait_ge(s_fl[b], 32 * g + 32)
                    tts(x1l[b], x1l[b], obB[:, :].unsqueeze(1).to_broadcast([P, TA, D]), ALU.add)\
                        .then_inc(s_x1b, 1)
                    dve.wait_ge(s_x1b, s + 1)
                    dve.wait_ge(s_fm, s + 1)
                    dve.wait_ge(s_out[b % 2], 16 * (2 * g + b // 2))
                    tts(yo[:, b % 2, :, :], v3((pW, pL)[b % 2][:, :], D), x1l[b], ALU.add).then_inc(s_fy, 1)
                    dve.wait_ge(s_fy, s + 1)
                    dve.sem_inc(s_fy2, 1)


_INS = ['x', 'adj', 'L0_gnn_W_gcn', 'L0_gnn_W_att', 'L0_gnn_a_att', 'L0_ffn_W_fx', 'L0_ffn_b_fx', 'L0_ffn_W_x',
        'L0_ffn_b_x', 'L0_ffn_W_slice', 'L0_ffn_b_slice', 'L0_ffn_temperature', 'L0_ffn_hy_in_w',
        'L0_ffn_hy_conv_w', 'L0_ffn_hy_conv_b', 'L0_ffn_hy_dt_bias', 'L0_ffn_hy_A_log', 'L0_ffn_hy_D',
        'L0_ffn_hy_fcD_w', 'L0_ffn_hy_norm_w', 'L0_ffn_hy_out_w', 'L0_ffn_out_w', 'L0_ffn_out_b']


def kernel(**inputs):
    import numpy as _np
    import concourse.bacc as _bacc
    from concourse import mybir as _mybir
    from concourse.bass_utils import run_bass_kernel_spmd as _run

    nc = _bacc.Bacc("TRN2", target_bir_lowering=False, num_devices=1)
    arrays, args = {}, []
    for name in _INS:
        a = _np.ascontiguousarray(inputs[name])
        arrays[f"in_{name}_dram"] = a
        args.append(nc.dram_tensor(f"in_{name}_dram", a.shape, _mybir.dt.from_np(a.dtype), kind="ExternalInput").ap())
    out = nc.dram_tensor("out_0_dram", inputs["x"].shape, _mybir.dt.float32, kind="ExternalOutput").ap()
    gnn_ffn(nc, *args, out)
    r = _run(nc, [arrays], core_ids=[0])
    return r.results[0]["out_0_dram"]
```
